# Optimizing a Trainium2 kernel written in Bass

```python
import numpy as np
import jax
import jax.numpy as jnp

def _softmax(x, axis=-1):
    return jax.nn.softmax(x, axis=axis)

def _gelu(x):
    return jax.nn.gelu(x, approximate=True)

def _silu(x):
    return jax.nn.silu(x)

def _sigmoid(x):
    return jax.nn.sigmoid(x)

def _layernorm(x, axis=-1, eps=1e-05):
    m = jnp.mean(x, axis=axis, keepdims=True)
    v = jnp.var(x, axis=axis, keepdims=True)
    return (x - m) / jnp.sqrt(v + eps)

def _scatter_add(tgt, idx, src, axis=0):
    return tgt.at[idx].add(src)

def _segment_sum(src, seg, n):
    return jax.ops.segment_sum(src, seg, n)
kernel_name = 'mk_flamingo_gated_d2_seqx_r8_864242'

def setup_inputs(seed: int=0):
    np.random.seed(seed)
    _w = jnp.asarray

    def _rec_inputs():
        import jax
        import jax.numpy as jnp
        _rk = jax.random.key(seed)
        x = 7.22e-05 + 1 * jax.random.normal(jax.random.fold_in(_rk, 1), (8, 256, 256), jnp.float32)
        _lenS = 256 - jax.random.randint(jax.random.fold_in(_rk, 7), (8,), 0, max(1, 256 // 4) + 1, jnp.int32)
        _lenS2 = 64 - jax.random.randint(jax.random.fold_in(_rk, 8), (8,), 0, max(1, 64 // 4) + 1, jnp.int32)
        _ctx_2048P = jax.random.normal(jax.random.fold_in(_rk, 11), (8, 16, 256), jnp.float32)
        _ctx_2048c = jax.random.dirichlet(jax.random.fold_in(_rk, 511), 0.3 * jnp.ones((16,), jnp.float32), (8, 64))
        _ctx_2048t = jnp.einsum('bsk,bkd->bsd', _ctx_2048c, _ctx_2048P)
        _ctx_2048t = _ctx_2048t * jax.lax.rsqrt(jnp.mean(jnp.square(_ctx_2048t)) + 1e-12) * 0.953939
        ctx_2048 = -0.000514642 + 1.00011 * (_ctx_2048t + 0.3 * jax.random.normal(jax.random.fold_in(_rk, 611), (8, 64, 256), jnp.float32))
        _validS = jnp.arange(256)[None, :] < _lenS[:, None]
        _validS2 = jnp.arange(64)[None, :] < _lenS2[:, None]
        _causal = jnp.tril(jnp.ones((256, 256), dtype=bool))
        mask_BxS2_bk0 = jnp.logical_not(jnp.broadcast_to(_validS2[:, :], (8, 64)))
        _g = jax.random.normal(jax.random.fold_in(_rk, 9001), (2, 2), jnp.float32)
        _g = jnp.sign(_g) * jnp.maximum(jnp.abs(_g), 1.0) + (_g == 0) * 1.0
        g_xattn = _g[0]
        g_ffn = _g[1]
        return (x, ctx_2048, mask_BxS2_bk0, g_xattn, g_ffn)
    x, ctx_2048, mask_BxS2_bk0, g_xattn, g_ffn = _rec_inputs()

    def _L0_xattn_setup():
        import jax, jax.numpy as jnp
        import numpy as np
        D_MODEL = 256
        NUM_HEADS = 16
        HEAD_DIM = D_MODEL // NUM_HEADS

        def _fq_sym(x, axis):
            s = jnp.max(jnp.abs(x), axis=axis, keepdims=True) / 127.0
            s = jnp.maximum(s, 1e-08)
            q = jnp.clip(jnp.round(x / s), -127.0, 127.0) * s
            return x + jax.lax.stop_gradient(q - x)

        def _fq_unsigned(x, axis):
            s = jnp.max(x, axis=axis, keepdims=True) / 255.0
            s = jnp.maximum(s, 1e-08)
            q = jnp.clip(jnp.round(x / s), 0.0, 255.0) * s
            return x + jax.lax.stop_gradient(q - x)
        key = jax.random.key(seed)
        ks = jax.random.split(key, 8)
        B, N, M, C = (2, 256, 64, D_MODEL)
        return {'x': jax.random.normal(ks[0], (B, N, C), jnp.float32), 'cond': jax.random.normal(ks[1], (B, M, C), jnp.float32), 'Wq': jax.random.normal(ks[2], (C, C), jnp.float32) * 0.02, 'bq': jnp.zeros((C,), jnp.float32), 'Wkv': jax.random.normal(ks[3], (C, 2 * C), jnp.float32) * 0.02, 'bkv': jnp.zeros((2 * C,), jnp.float32), 'Wp': jax.random.normal(ks[4], (C, C), jnp.float32) * 0.02, 'bp': jnp.zeros((C,), jnp.float32)}
    _L0_xattn_all = _L0_xattn_setup()
    _L0_xattn_in = {k: v for k, v in _L0_xattn_all.items() if k in ('Wq', 'bq', 'Wkv', 'bkv', 'Wp', 'bp')}
    del _L0_xattn_all

    def _L0_ffn_setup():
        import jax, jax.numpy as jnp
        import numpy as np
        EPS = 1e-05

        def _quant_weight(w):
            scale = jnp.mean(jnp.abs(w)) + EPS
            wq = jnp.clip(jnp.round(w / scale), -1.0, 1.0) * scale
            return w + jax.lax.stop_gradient(wq - w)

        def _quant_act(x):
            scale = jnp.maximum(jnp.max(jnp.abs(x), axis=-1, keepdims=True), EPS) / 127.0
            xq = jnp.clip(jnp.round(x / scale), -128.0, 127.0) * scale
            return x + jax.lax.stop_gradient(xq - x)

        def bitlinear(x, w):
            return jnp.einsum('bsi,oi->bso', _quant_act(x), _quant_weight(w))
        key = jax.random.key(seed)
        k1, k2, k3, k4 = jax.random.split(key, 4)
        d_model, d_ff = (256, 1024)
        B, S = (4, 256)
        x = jax.random.normal(k1, (B, S, d_model), dtype=jnp.float32)
        w_gate = jax.random.normal(k2, (d_ff, d_model), dtype=jnp.float32) * 0.02
        w_up = jax.random.normal(k3, (d_ff, d_model), dtype=jnp.float32) * 0.02
        w_down = jax.random.normal(k4, (d_model, d_ff), dtype=jnp.float32) * 0.02
        return {'x': x, 'w_gate': w_gate, 'w_up': w_up, 'w_down': w_down}
    _L0_ffn_all = _L0_ffn_setup()
    _L0_ffn_in = {k: v for k, v in _L0_ffn_all.items() if k in ('w_gate', 'w_up', 'w_down')}
    del _L0_ffn_all

    def _L1_xattn_setup():
        import jax, jax.numpy as jnp
        import numpy as np
        key = jax.random.key(seed)
        k1, k2, k3 = jax.random.split(key, 3)
        B, S, D, M = (8, 256, 256, 128)
        hidden_states = jax.random.normal(k1, (B, S, D), dtype=jnp.float32)
        memory_tokens = jax.random.normal(k2, (B, M, D), dtype=jnp.float32)
        memory_mask = jax.random.randint(k3, (B, M), 0, 2).astype(jnp.bool_)
        return {'hidden_states': hidden_states, 'memory_tokens': memory_tokens, 'memory_mask': memory_mask}
    _L1_xattn_all = _L1_xattn_setup()
    _L1_xattn_in = {k: v for k, v in _L1_xattn_all.items() if k in ()}
    del _L1_xattn_all

    def _L1_ffn_setup():
        import jax, jax.numpy as jnp
        import numpy as np
        D_MODEL = 256
        MLP_RATIO = 4
        TOP_K = 2
        N_EXPERTS = 8
        D_INT = D_MODEL * MLP_RATIO // TOP_K
        BATCH, SEQ = (2, 512)
        key = jax.random.key(seed)
        kx, kr, ki, ko = jax.random.split(key, 4)
        x = jax.random.normal(kx, (BATCH, SEQ, D_MODEL), dtype=jnp.float32)
        Wr = jax.random.normal(kr, (N_EXPERTS, D_MODEL), dtype=jnp.float32) * 0.02
        Win = jax.random.normal(ki, (N_EXPERTS, D_INT, D_MODEL), dtype=jnp.float32) * 0.02
        Wout = jax.random.normal(ko, (N_EXPERTS, D_MODEL, D_INT), dtype=jnp.float32) * 0.02
        return {'x': x, 'Wr': Wr, 'Win': Win, 'Wout': Wout}
    _L1_ffn_all = _L1_ffn_setup()
    _L1_ffn_in = {k: v for k, v in _L1_ffn_all.items() if k in ('Wr', 'Win', 'Wout')}
    del _L1_ffn_all
    return {'x': x, 'ctx_2048': ctx_2048, 'mask_BxS2_bk0': mask_BxS2_bk0, 'g_xattn': g_xattn, 'g_ffn': g_ffn, 'L0_xattn_Wq': _L0_xattn_in['Wq'], 'L0_xattn_bq': _L0_xattn_in['bq'], 'L0_xattn_Wkv': _L0_xattn_in['Wkv'], 'L0_xattn_bkv': _L0_xattn_in['bkv'], 'L0_xattn_Wp': _L0_xattn_in['Wp'], 'L0_xattn_bp': _L0_xattn_in['bp'], 'L0_ffn_w_gate': _L0_ffn_in['w_gate'], 'L0_ffn_w_up': _L0_ffn_in['w_up'], 'L0_ffn_w_down': _L0_ffn_in['w_down'], 'L1_ffn_Wr': _L1_ffn_in['Wr'], 'L1_ffn_Win': _L1_ffn_in['Win'], 'L1_ffn_Wout': _L1_ffn_in['Wout']}

def reference(x, ctx_2048, mask_BxS2_bk0, g_xattn, g_ffn, L0_xattn_Wq, L0_xattn_bq, L0_xattn_Wkv, L0_xattn_bkv, L0_xattn_Wp, L0_xattn_bp, L0_ffn_w_gate, L0_ffn_w_up, L0_ffn_w_down, L1_ffn_Wr, L1_ffn_Win, L1_ffn_Wout):
    import jax
    import jax.numpy as jnp

    def _L0_xattn_ref(x, cond, Wq, bq, Wkv, bkv, Wp, bp):
        import jax, jax.numpy as jnp
        import numpy as np
        D_MODEL = 256
        NUM_HEADS = 16
        HEAD_DIM = D_MODEL // NUM_HEADS

        def _fq_sym(x, axis):
            s = jnp.max(jnp.abs(x), axis=axis, keepdims=True) / 127.0
            s = jnp.maximum(s, 1e-08)
            q = jnp.clip(jnp.round(x / s), -127.0, 127.0) * s
            return x + jax.lax.stop_gradient(q - x)

        def _fq_unsigned(x, axis):
            s = jnp.max(x, axis=axis, keepdims=True) / 255.0
            s = jnp.maximum(s, 1e-08)
            q = jnp.clip(jnp.round(x / s), 0.0, 255.0) * s
            return x + jax.lax.stop_gradient(q - x)
        B, N, C = x.shape
        H, hd = (NUM_HEADS, HEAD_DIM)
        q = (x @ Wq + bq).reshape(1, B * N, H, hd)
        kv = (cond @ Wkv + bkv).reshape(1, -1, 2, H, hd)
        k, v = (kv[:, :, 0], kv[:, :, 1])
        scale = 1.0 / np.sqrt(hd).astype(np.float32)
        q = jnp.transpose(q * scale, (0, 2, 1, 3))
        k = jnp.transpose(k, (0, 2, 1, 3))
        v = jnp.transpose(v, (0, 2, 1, 3))
        q = _fq_sym(q, axis=-1)
        k = _fq_sym(k, axis=-1)
        v = _fq_sym(v, axis=2)
        attn = jnp.einsum('bhqd,bhkd->bhqk', q, k)
        attn = jax.nn.softmax(attn.astype(jnp.float32), axis=-1)
        attn = _fq_unsigned(attn, axis=-1)
        out = jnp.einsum('bhqk,bhkd->bhqd', attn, v)
        out = jnp.transpose(out, (0, 2, 1, 3)).reshape(B, N, C)
        return out @ Wp + bp

    def _L0_ffn_ref(x, w_gate, w_up, w_down):
        import jax, jax.numpy as jnp
        import numpy as np
        EPS = 1e-05

        def _quant_weight(w):
            scale = jnp.mean(jnp.abs(w)) + EPS
            wq = jnp.clip(jnp.round(w / scale), -1.0, 1.0) * scale
            return w + jax.lax.stop_gradient(wq - w)

        def _quant_act(x):
            scale = jnp.maximum(jnp.max(jnp.abs(x), axis=-1, keepdims=True), EPS) / 127.0
            xq = jnp.clip(jnp.round(x / scale), -128.0, 127.0) * scale
            return x + jax.lax.stop_gradient(xq - x)

        def bitlinear(x, w):
            return jnp.einsum('bsi,oi->bso', _quant_act(x), _quant_weight(w))
        gate = jax.nn.sigmoid(bitlinear(x, w_gate))
        up = bitlinear(x, w_up)
        h = gate * up
        return bitlinear(h, w_down)

    def _L1_xattn_ref(hidden_states, memory_tokens, memory_mask):
        import jax, jax.numpy as jnp
        import numpy as np
        B, S, D = hidden_states.shape
        scale = 1.0 / jnp.sqrt(jnp.asarray(D, hidden_states.dtype))
        scores = jnp.einsum('bsd,bmd->bsm', hidden_states, memory_tokens) * scale
        neg_inf = jnp.asarray(-1e+30, scores.dtype)
        scores = jnp.where(memory_mask[:, None, :], scores, neg_inf)
        attn = jax.nn.softmax(scores, axis=-1)
        readout = jnp.einsum('bsm,bmd->bsd', attn, memory_tokens)
        valid_b = jnp.any(memory_mask, axis=-1)
        out = jnp.where(valid_b[:, None, None], readout, jnp.zeros_like(readout))
        return out

    def _L1_ffn_ref(x, Wr, Win, Wout):
        import jax, jax.numpy as jnp
        import numpy as np
        D_MODEL = 256
        MLP_RATIO = 4
        TOP_K = 2
        N_EXPERTS = 8
        D_INT = D_MODEL * MLP_RATIO // TOP_K
        BATCH, SEQ = (2, 512)
        orig_shape = x.shape
        xf = x.reshape(-1, orig_shape[-1])
        T = xf.shape[0]
        logits = xf @ Wr.T
        scores, expert = jax.lax.top_k(logits, TOP_K)
        weights = jax.nn.softmax(scores, axis=-1)
        gate = jnp.zeros((T, N_EXPERTS), dtype=xf.dtype)
        gate = gate.at[jnp.arange(T)[:, None], expert].add(weights)
        y = jnp.zeros_like(xf)
        for e in range(N_EXPERTS):
            h = jax.nn.silu(xf @ Win[e].T)
            y = y + gate[:, e:e + 1] * (h @ Wout[e].T)
        return y.reshape(orig_shape)
    x = x + jnp.tanh(g_xattn[0]) * _L0_xattn_ref(_layernorm(x, axis=-1), ctx_2048, L0_xattn_Wq, L0_xattn_bq, L0_xattn_Wkv, L0_xattn_bkv, L0_xattn_Wp, L0_xattn_bp)
    x = x + jnp.tanh(g_ffn[0]) * _L0_ffn_ref(_layernorm(x, axis=-1), L0_ffn_w_gate, L0_ffn_w_up, L0_ffn_w_down)
    x = x + jnp.tanh(g_xattn[1]) * _L1_xattn_ref(_layernorm(x, axis=-1), ctx_2048, mask_BxS2_bk0)
    x = x + jnp.tanh(g_ffn[1]) * _L1_ffn_ref(_layernorm(x, axis=-1), L1_ffn_Wr, L1_ffn_Win, L1_ffn_Wout)
    return x

_drawn_inputs = setup_inputs


def setup_inputs(seed=0):
    import zlib

    import numpy as np

    out = dict(_drawn_inputs(seed))
    spreads = {'g_ffn': (-1.0, 0.6),
     'L0_xattn_bq': (0.0, 0.8),
     'L0_xattn_bkv': (0.0, 0.352),
     'L0_xattn_bp': (0.0, 0.1)}
    factors = {'L0_xattn_Wq': 8.0, 'L0_xattn_Wkv': 5.062, 'L0_ffn_w_gate': 27.199}
    for name, (base, spread) in spreads.items():
        noise = np.random.default_rng([zlib.crc32(name.encode()), seed]).standard_normal(out[name].shape)
        drawn = base * np.exp(spread * noise) if base else spread * noise
        out[name] = jnp.asarray(drawn.astype(out[name].dtype))
    for name, factor in factors.items():
        out[name] = (out[name] * factor).astype(out[name].dtype)
    return out
```

```python
import concourse.bass as bass
from concourse import mybir

ReduceOp = bass.bass_isa.ReduceOp
from contextlib import ExitStack

F32 = mybir.dt.float32
BF16 = mybir.dt.bfloat16
I16 = mybir.dt.int16
U8 = mybir.dt.uint8
ALU = mybir.AluOpType
ACT = mybir.ActivationFunctionType
AX = mybir.AxisListType

P = 128
TOKENS, C = 2048, 256
NT = TOKENS // P
CC = C // P
KEYS = 512
KB = KEYS // P
H, HD = 16, 16
BATCH, M = 8, 64
FF = 1024
E, DI = 8, 512
SPLIT = 8
MAGIC = 12582912.0
LN255 = 5.541263545158426
LN_EPS = 1e-5
Q_EPS = 1e-8
F_EPS = 1e-5
NEG = 1e30
ACT_PAIRS = (1, 3, 5, 7)
DVE_PAIRS = tuple(j for j in range(8) if j not in ACT_PAIRS)


def flamingo_kernel(nc, x_d, ctx_d, ctxT_d, mask_d, gx_d, gf_d, wq_d, bq_d, wkv_d, bkv_d, wp_d, bp_d,
                    wg_d, wu_d, wd_d, wr_d, win_d, wout_d, out_d):
    stack = ExitStack()
    with stack:
        def sb(name, shape, dt=F32):
            return stack.enter_context(nc.sbuf_tensor(name, shape, dt))

        def pb(name, shape, dt=F32):
            return stack.enter_context(nc.psum_tensor(name, shape, dt))

        def sem(name):
            return stack.enter_context(nc.semaphore(name))

        x = sb("x_tokens", [P, NT, C])
        ident = sb("ident", [P, P])
        identb = sb("identb", [P, P], BF16)
        gates = sb("gates", [P, 4])
        graw = sb("graw", [P, 4])
        ctxT = sb("ctxT", [P, CC, KEYS])
        ctxn = sb("ctxn", [M, BATCH, C])
        wq = sb("wq", [P, CC, C])
        wkv = sb("wkv", [P, CC, 2 * C])
        wp = sb("wp", [P, CC, C])
        wps = sb("wps", [P, CC, C])
        bq = sb("bq", [P, C])
        bkv = sb("bkv", [P, 2 * C])
        bp = sb("bp", [P, C])
        wr = sb("wr", [P, CC, E])
        wf = [sb("wg", [P, CC * FF]), sb("wu", [P, CC * FF]), sb("wd", [P, CC * FF])]
        wi = [sb("wgi", [P, CC * FF], BF16), sb("wui", [P, CC * FF], BF16), sb("wdi", [P, CC * FF], BF16)]
        maskb = sb("maskb", [P, BATCH * M], U8)
        madd = sb("madd", [P, BATCH * M])
        valid = sb("valid", [P, BATCH])
        kv = sb("kv", [P, KB, 2 * C])
        ktmp = sb("ktmp", [P, KB, C])
        kamax = sb("kamax", [P, KB * H])
        kscale = sb("kscale", [P, KB * H])
        kinv = sb("kinv", [P, KB * H])
        KC = sb("KC", [P, KB, H, SPLIT * HD], BF16)
        KT = sb("KT", [P, H, KEYS], BF16)
        vmax = sb("vmax", [P, C])
        vmaxb = sb("vmaxb", [P, C])
        vscale = sb("vscale", [P, C])
        vinv = sb("vinv", [P, C])
        V = sb("V", [P, KB, C], BF16)
        wabs = sb("wabs", [P, 3])
        wabs_all = sb("wabs_all", [P, 3])
        wscale = sb("wscale", [P, 3])
        winv = sb("winv", [P, 3])
        wjunk = KT
        st = sb("st", [P, NT, 6])
        mv = sb("mv", [P, NT, 2])
        lnt = sb("lnt", [P, 4, NT])
        rstd = sb("rstd", [P, NT])
        nbias = sb("nbias", [P, NT])
        xh = sb("xh", [P, C])
        xT = sb("xT", [P, C])
        q = sb("q", [P, C])
        qy = sb("qy", [P, C])
        qr = sb("qr", [P, C])
        qamax = sb("qamax", [P, H])
        qscale = sb("qscale", [P, H])
        qinv = sb("qinv", [P, H])
        QC = sb("QC", [P, H, SPLIT * HD], BF16)
        QT = sb("QT", [P, H, P], BF16)
        junk = ktmp[:, :, :].rearrange("p k c -> p (k c)").bitcast(BF16).rearrange("p (a k) -> p a k", a=4)
        ebias = sb("ebias", [P, H])
        R = sb("R", [P, 4, 2, KEYS], I16)
        PT = sb("PT", [P, 4, 2 * KB * P], BF16)
        esum = sb("esum", [P, H])
        rsum = sb("rsum", [P, H])
        ao = sb("ao", [P, C])
        aoT = sb("aoT", [P, C])
        gbp = sb("gbp", [P, C])
        fmax = sb("fmax", [P, 1])
        fs = sb("fs", [P, 1])
        finv = sb("finv", [P, 1])
        fg = sb("fg", [P, 2])
        fu = sb("fu", [P, 2])
        xq = sb("xq", [P, C])
        xi = sb("xi", [P, C], BF16)
        xiT = sb("xiT", [P, C], BF16)
        sig = sb("sig", [P, 2, FF // 2])
        hid = sb("hid", [P, FF])
        hmax = sb("hmax", [P, 1])
        hs = sb("hs", [P, 1])
        hinv = sb("hinv", [P, 1])
        hf = sb("hf", [P, 1])
        ho = sb("ho", [P, 1])
        wdg = sb("wdg", [P, 1])
        hq = sb("hq", [P, FF])
        hi = sb("hi", [P, FF], BF16)
        hiT = sb("hiT", [P, FF], BF16)
        xh2 = sb("xh2", [P, 2, C])
        xT2 = sb("xT2", [P, 2, C])
        sm = sb("sm", [P, 2, M])
        smax = sb("smax", [P, 2])
        pe_ = sb("pe_", [P, 2, M])
        ssum = sb("ssum", [P, 2])
        srec = sb("srec", [P, 2])
        sfac = sb("sfac", [P, 2])
        pT = sb("pT", [M, 2, P])
        gvalid = sb("gvalid", [P, BATCH])
        xTa = KC[:, :, :, :].rearrange("p k h d -> p (k h d)").bitcast(F32).rearrange("p (a t) -> p a t", a=CC)
        lg = sb("lg", [P, E])
        top = sb("top", [P, 8])
        topi = sb("topi", [P, 8], mybir.dt.uint32)
        topf = sb("topf", [P, 8])
        tdiff = sb("tdiff", [P, 2])
        iota = sb("iota", [P, E])
        sel = sb("sel", [P, 2, E])
        G = sb("G", [P, NT, E])
        win = sb("win", [P, 2, CC, DI])
        wout = sb("wout", [P, 2, DI // P, C])
        hT = KT[:, :, :].rearrange("p h k -> p (h k)").bitcast(F32).rearrange("p (b f t) -> p b f t", b=2, f=DI // P)

        S = pb("S", [P, 4, 512])
        T = pb("T", [P, 2, 512])
        PV = pb("PV", [P, 512])
        QB = pb("QB", [P, 512])

        names = """x_in w_in1 w_in2 w_in3 consts iota_r gate_r
            kvp kvb kdv kct kev vred vall vq svT wps_r wabs_r wall wsc wpool wpool_done
            st0 aggr lns lna rstd_r
            xh_r xhT_r xT_r qp_r q_r qa_r qsc_r qi_r qprep qA_r qtA_r qB_r qtB_r
            score_r nm_r nb_r exp_r tr_r evD evA pv_r rs_r ao_r aoT_r aoTe_r op_r xb_r x1_r bs_r gbp_r
            f_xh f_max f_s f_inv f_fg f_rq f_xiT f_xiTe f_gu f_sig f_h f_hm f_hs f_hi f_hf f_hq f_hiT f_hiTe f_dn f_x f_bs
            c_xh c_xhT c_xT c_sc c_sm c_mx c_ex c_rc c_f c_pT c_pTe c_rd c_x c_bs c_mask
            d_xh d_xhT d_xT d_lg d_lgs d_top d_topi d_td d_w d_sel d_g
            d_xTa apart rstd_r2 kct_in kevD d_sel2 m_w0 m_w1 m_h m_hs m_y m_x out_r""".split()
        s = {n: sem("s_" + n) for n in names}
        block = stack.enter_context(nc.Block())

        def ev_sem(t, j):
            if j in ACT_PAIRS:
                return s["evA"], t * len(ACT_PAIRS) + ACT_PAIRS.index(j) + 1
            return s["evD"], t * len(DVE_PAIRS) + DVE_PAIRS.index(j) + 1

        def back(t, j):
            return (t, j) if j >= 0 else (t - 1, j + 8)

        Tb = T[:, :, :].rearrange("p a b -> p (a b)").bitcast(BF16).rearrange("p (a b) -> p a b", a=2)
        Ti = T[:, :, :].rearrange("p a b -> p (a b)").bitcast(I16).rearrange("p (a b) -> p a b", a=2)
        QBb = QB[:, :].bitcast(BF16)
        Sb = S[:, :, :].rearrange("p a b -> p (a b)").bitcast(BF16).rearrange("p (a b) -> p a b", a=4)
        Rb = R[:, :, :, :].rearrange("p a b c -> p (a b c)").bitcast(BF16).rearrange("p (a b c) -> p a b c", a=4, b=2)

        @block.sync
        def _(eng):
            eng.dma_start(ctxT[:, :, :], ctxT_d.rearrange("(a p) k -> p a k", p=P)).then_inc(s["w_in1"], 16)
            eng.dma_start(wkv[:, :, :], wkv_d.rearrange("(a p) k -> p a k", p=P)).then_inc(s["w_in1"], 16)
            eng.dma_start(bkv[:, :], bkv_d.partition_broadcast(P)).then_inc(s["w_in1"], 16)
            for a in range(4):
                eng.dma_start(x[:, 4 * a:4 * a + 4, :],
                              x_d.rearrange("(t p) c -> p t c", p=P)[:, 4 * a:4 * a + 4, :]).then_inc(s["x_in"], 16)
            eng.dma_start(wq[:, :, :], wq_d.rearrange("(a p) k -> p a k", p=P)).then_inc(s["w_in2"], 16)
            eng.dma_start(bq[:, :], bq_d.partition_broadcast(P)).then_inc(s["w_in2"], 16)
            eng.dma_start(graw[:, 0:2], gx_d.partition_broadcast(P)).then_inc(s["w_in2"], 16)
            eng.dma_start(graw[:, 2:4], gf_d.partition_broadcast(P)).then_inc(s["w_in2"], 16)
            eng.dma_start(wp[:, :, :], wp_d.rearrange("(a p) k -> p a k", p=P)).then_inc(s["w_in2"], 16)
            eng.dma_start(bp[:, :], bp_d.partition_broadcast(P)).then_inc(s["w_in2"], 16)
            eng.dma_start(wf[0][:, :].rearrange("p (a k) -> p a k", a=CC),
                          wg_d.rearrange("(a p) k -> p a k", p=P)).then_inc(s["w_in3"], 16)
            eng.dma_start(wf[1][:, :].rearrange("p (a k) -> p a k", a=CC),
                          wu_d.rearrange("(a p) k -> p a k", p=P)).then_inc(s["w_in3"], 16)
            eng.dma_start(wf[2][:, :].rearrange("p (a k) -> p a k", a=FF // P),
                          wd_d.rearrange("(a p) k -> p a k", p=P)).then_inc(s["w_in3"], 16)
            eng.dma_start(ctxn[:, :, :], ctx_d.rearrange("(b m) c -> m b c", m=M)).then_inc(s["w_in3"], 16)
            eng.dma_start(wr[:, :, :], wr_d.rearrange("(a p) k -> p a k", p=P)).then_inc(s["w_in3"], 16)
            eng.dma_start(maskb[:, :], mask_d.partition_broadcast(P)).then_inc(s["w_in3"], 16)
            for b in range(2):
                eng.dma_start(win[:, b, :, :], win_d[b].rearrange("(a p) k -> p a k", p=P)).then_inc(s[f"m_w{b}"], 16)
                eng.dma_start(wout[:, b, :, :], wout_d[b].rearrange("(a p) k -> p a k", p=P)).then_inc(s[f"m_w{b}"], 16)
            with eng.Fori(0, E // 2 - 1) as e2:
                for b in range(2):
                    eng.wait_ge(s["m_y"], e2 * 32 + (b * 16 + 16))
                    eng.dma_start(win[:, b, :, :], win_d[bass.ds(e2 * 2 + (b + 2), 1)].rearrange("o (a p) k -> p (o a) k", p=P)).then_inc(s[f"m_w{b}"], 16)
                    eng.dma_start(wout[:, b, :, :], wout_d[bass.ds(e2 * 2 + (b + 2), 1)].rearrange("o (a p) k -> p (o a) k", p=P)).then_inc(s[f"m_w{b}"], 16)
            for a in range(4):
                eng.wait_ge(s["m_x"], NT * (E - 1) + 4 * a + 4)
                eng.dma_start(out_d.rearrange("(t p) c -> p t c", p=P)[:, 4 * a:4 * a + 4, :],
                              x[:, 4 * a:4 * a + 4, :]).then_inc(s["out_r"], 16)
            eng.wait_ge(s["out_r"], 64)

        @block.gpsimd
        def _(eng):
            eng.memset(ident[:, :], 0.0).then_inc(s["iota_r"], 1)
            eng.memset(identb[:, :], 0.0).then_inc(s["iota_r"], 1)
            eng.wait_ge(s["iota_r"], 2)
            for m in (ident, identb):
                eng.affine_select(out=m[:, :], in_=m[:, :], compare_op=ALU.not_equal, fill=1.0, base=0,
                                  pattern=[[-1, P]], channel_multiplier=1).then_inc(s["consts"], 1)
            eng.iota(iota[:, :], [[1, E]], 0, 0, allow_small_or_imprecise_dtypes=True).then_inc(s["consts"], 1)
            eng.wait_ge(s["vred"], 2)
            eng.partition_all_reduce(vmaxb[:, :], vmax[:, :], P, ReduceOp.max).then_inc(s["vall"], 1)
            eng.wait_ge(s["wabs_r"], 3)
            eng.partition_all_reduce(wabs_all[:, :], wabs[:, :], P, ReduceOp.add).then_inc(s["wall"], 1)

            def apart(which, value):
                eng.wait_ge(which, value)
                eng.sem_inc(s["apart"], 1)

            def q_prep(u):
                v3 = lambda a: a[:, :].rearrange("p (h d) -> p h d", h=H)
                slots = QC[:, :, :].rearrange("p h (s d) -> p h s d", s=SPLIT)
                n = [0]

                def step(ins):
                    n[0] += 1
                    ins.then_inc(s["qprep"], 1)
                    apart(s["qprep"], 9 * u + n[0])
                if not (isinstance(u, int) and u == 0):
                    eng.wait_ge(s["qB_r"], u)
                eng.wait_ge(s["qi_r"], u + 1)
                step(eng.tensor_tensor(v3(qy), v3(q), qinv[:, :].unsqueeze(2).to_broadcast([P, H, HD]), ALU.mult))
                step(eng.tensor_scalar(qy[:, :], qy[:, :], 1.0, MAGIC, ALU.mult, ALU.add))
                step(eng.tensor_scalar(qy[:, :], qy[:, :], -MAGIC, 1.0, ALU.add, ALU.mult))
                step(eng.tensor_tensor(v3(qy), v3(qy), qscale[:, :].unsqueeze(2).to_broadcast([P, H, HD]), ALU.mult))
                step(eng.tensor_scalar(slots[:, :, 0:3, :], v3(qy).unsqueeze(2).to_broadcast([P, H, 3, HD]), 1.0, 0.0, ALU.mult, ALU.add))
                step(eng.tensor_tensor(v3(qr), v3(qy), slots[:, :, 0, :], ALU.subtract))
                step(eng.tensor_scalar(slots[:, :, 3:6, :], v3(qr).unsqueeze(2).to_broadcast([P, H, 3, HD]), 1.0, 0.0, ALU.mult, ALU.add))
                step(eng.tensor_tensor(v3(qy), v3(qr), slots[:, :, 3, :], ALU.subtract))
                step(eng.tensor_scalar(slots[:, :, 6:8, :], v3(qy).unsqueeze(2).to_broadcast([P, H, 2, HD]), 1.0, 0.0, ALU.mult, ALU.add))

            def add_bias(w):
                eng.wait_ge(s["xh_r"], w + 1)
                eng.tensor_tensor(x[:, w, :], x[:, w, :], gbp[:, :], ALU.add).then_inc(s["xb_r"], 1)

            q_prep(0)
            eng.wait_ge(s["gbp_r"], 1)
            with eng.Fori(0, NT - 1) as t:
                add_bias(t)
                q_prep(t + 1)
            add_bias(NT - 1)
            eng.wait_ge(s["wsc"], 3)
            for i in range(3):
                eng.tensor_scalar(wf[i][:, :], wf[i][:, :], winv[:, i:i + 1], MAGIC, ALU.mult, ALU.add).then_inc(s["wpool"], 1)
                eng.wait_ge(s["wpool"], 3 * i + 1)
                eng.tensor_scalar(wf[i][:, :], wf[i][:, :], -MAGIC, 1.0, ALU.add, ALU.mult).then_inc(s["wpool"], 1)
                eng.wait_ge(s["wpool"], 3 * i + 2)
                eng.tensor_scalar(wi[i][:, :], wf[i][:, :], 1.0, -1.0, ALU.min, ALU.max).then_inc(s["wpool"], 1)

            def round_h(t):
                apart(s["f_hf"], t + 1)
                eng.tensor_scalar(hq[:, :], hid[:, :], hf[:, 0:1], MAGIC, ALU.mult, ALU.add).then_inc(s["f_hq"], 1)
                if not (isinstance(t, int) and t == 0):
                    apart(s["f_hiT"], t)
                apart(s["f_hq"], 2 * t + 1)
                eng.tensor_scalar(hi[:, :], hq[:, :], -MAGIC, 1.0, ALU.add, ALU.mult).then_inc(s["f_hq"], 1)

            def rx(u):
                apart(s["f_inv"], u + 1)
                eng.tensor_scalar(xq[:, :], xh[:, :], finv[:, 0:1], MAGIC, ALU.mult, ALU.add).then_inc(s["f_rq"], 1)
                if not (isinstance(u, int) and u == 0):
                    apart(s["f_xiT"], u)
                apart(s["f_rq"], 2 * u + 1)
                eng.tensor_scalar(xi[:, :], xq[:, :], -MAGIC, 1.0, ALU.add, ALU.mult).then_inc(s["f_rq"], 1)

            rx(0)
            rx(1)
            round_h(0)
            with eng.Fori(1, NT - 1) as t:
                rx(t + 1)
                round_h(t)
            round_h(NT - 1)

        @block.scalar
        def _(eng):
            eng.wait_ge(s["w_in3"], 96)
            eng.wait_ge(s["w_in2"], 96)
            eng.activation(gates[:, :], graw[:, :], ACT.Tanh).then_inc(s["gate_r"], 1)
            for i in range(3):
                eng.activation(KC[:, i, :, :].rearrange("p h d -> p (h d)"), wf[i][:, :], ACT.Abs,
                               accum_out=wabs[:, i:i + 1]).then_inc(s["wabs_r"], 1)

            def ln_sqrt(n):
                eng.wait_ge(s["lns"], 3 * n + 1)
                eng.activation(lnt[:, 1, :], lnt[:, 0, :], ACT.Sqrt).then_inc(s["lna"], 1)

            def normalise(out, t):
                return eng.activation(out, x[:, t, :], ACT.Identity, bias=nbias[:, t:t + 1] if isinstance(t, int) else nbias[:, bass.ds(t, 1)],
                                      scale=rstd[:, t:t + 1] if isinstance(t, int) else rstd[:, bass.ds(t, 1)])

            ln_sqrt(0)
            for i in range(8):
                if i % 2:
                    eng.wait_ge(s["kct"], i + 1)
                    eng.activation(KT[:, 8 * (i % 2):8 * (i % 2) + 8, P * (i // 2):P * (i // 2) + P],
                                   Tb[:, i % 2, :].rearrange("p (a b) -> p a b", a=8), ACT.Copy).then_inc(s["kev"], 1)

            def q_norm(u):
                if isinstance(u, int) and u == 0:
                    eng.wait_ge(s["rstd_r"], 2)
                else:
                    eng.wait_ge(s["xhT_r"], u)
                normalise(xh[:, :], u).then_inc(s["xh_r"], 1)

            def q_xT(u):
                eng.wait_ge(s["xhT_r"], u + 1)
                eng.activation(xT[:, :], QB[:, 0:C], ACT.Copy).then_inc(s["xT_r"], 1)

            def body(t, main, prev, nxt):
                first = not prev
                if nxt:
                    q_norm(t + 1)
                for h in range(16):
                    if main:
                        eng.wait_ge(s["nb_r"], t * 16 + (h + 1))
                        if h % 2 == 0 and not (first and h < 8):
                            eng.wait_ge(s["tr_r"], t * 8 + (h // 2 - 3))
                        if h % 8 == 0 and prev:
                            eng.wait_ge(s["rs_r"], t * 2 + (h // 8 - 1))
                        eng.activation(R[:, (h // 2) % 4, h % 2, :], S[:, h % 4, :], ACT.Exp,
                                       bias=ebias[:, h:h + 1], scale=-1.0, accum_out=esum[:, h:h + 1]).then_inc(s["exp_r"], 1)
                    if h == 1 and nxt:
                        q_xT(t + 1)
                    if h % 2 == 0:
                        tt, j = back(t, h // 2 - 1)
                        if j in ACT_PAIRS and (h >= 2 or prev) and (main or h < 2):
                            eng.wait_ge(s["tr_r"], tt * 8 + (j + 1))
                            if not (first and j < 4):
                                eng.wait_ge(s["pv_r"], tt * 8 + (j - 3))
                            eng.activation(PT[:, j % 4, :], Ti[:, j % 2, :], ACT.Copy).then_inc(s["evA"], 1)
                    if h == 6 and prev:
                        eng.wait_ge(s["aoT_r"], t)
                        eng.activation(aoT[:, :], QB[:, 0:C], ACT.Copy).then_inc(s["aoTe_r"], 1)

            q_norm(0)
            q_xT(0)
            body(0, True, False, True)
            with eng.Fori(1, NT - 1) as t:
                body(t, True, True, True)
            body(NT - 1, True, True, False)
            body(NT, False, True, False)

            ln_sqrt(1)

            def f_stage1(u):
                if isinstance(u, int) and u == 0:
                    eng.wait_ge(s["rstd_r"], 4)
                else:
                    eng.wait_ge(s["f_rq"], 2 * u)
                normalise(xh[:, :], u).then_inc(s["f_xh"], 1)

            def f_xiT(u):
                eng.wait_ge(s["f_xiT"], u + 1)
                eng.activation(xiT[:, :], Tb[:, 0, 0:C], ACT.Copy).then_inc(s["f_xiTe"], 1)

            def f_sig(t):
                for k in range(2):
                    eng.wait_ge(s["f_gu"], 2 * t + (k + 1))
                    eng.wait_ge(s["f_fg"], 2 * t + 1)
                    if not (isinstance(t, int) and t == 0):
                        eng.wait_ge(s["f_h"], 2 * t + (k - 1))
                    eng.activation(sig[:, k, :], S[:, 2 * k, :], ACT.Sigmoid, scale=fg[:, 0:1]).then_inc(s["f_sig"], 1)

            def f_hiT(t):
                eng.wait_ge(s["f_hiT"], t + 1)
                eng.activation(hiT[:, :], Tb[:, 1, :], ACT.Copy).then_inc(s["f_hiTe"], 1)

            f_stage1(0)
            f_xiT(0)
            f_stage1(1)
            f_sig(0)
            f_xiT(1)
            f_hiT(0)
            with eng.Fori(1, NT - 1) as t:
                f_stage1(t + 1)
                f_sig(t)
                f_xiT(t + 1)
                f_hiT(t)
            f_sig(NT - 1)
            f_hiT(NT - 1)

            ln_sqrt(2)
            eng.wait_ge(s["rstd_r"], 6)
            with eng.Fori(0, BATCH) as b:
                for i in range(2):
                    eng.activation(xh2[:, i, :], x[:, b * 2 + i, :], ACT.Identity, bias=nbias[:, bass.ds(b * 2 + i, 1)],
                                   scale=rstd[:, bass.ds(b * 2 + i, 1)]).then_inc(s["c_xh"], 1)
                for i in range(2):
                    eng.wait_ge(s["c_xhT"], b * 2 + (i + 1))
                    eng.activation(xT2[:, i, :], S[:, i, 0:C], ACT.Copy).then_inc(s["c_xT"], 1)
                for i in range(2):
                    eng.wait_ge(s["c_mx"], b * 2 + (i + 1))
                    eng.activation(pe_[:, i, :], sm[:, i, :], ACT.Exp, bias=smax[:, i:i + 1],
                                   accum_out=ssum[:, i:i + 1]).then_inc(s["c_ex"], 1)
                for i in range(2):
                    eng.wait_ge(s["c_pT"], b * 2 + (i + 1))
                    eng.activation(pT[:, i, :], T[0:M, i, 0:P], ACT.Copy).then_inc(s["c_pTe"], 1)
                for i in range(2):
                    eng.wait_ge(s["c_x"], b * 2 + (i + 1))

            ln_sqrt(3)
            eng.wait_ge(s["rstd_r"], 8)
            with eng.Fori(0, NT) as t:
                normalise(xh[:, :], t).then_inc(s["d_xh"], 1)
                eng.wait_ge(s["d_xhT"], t + 1)
                eng.activation(xT[:, :], S[:, 0, 0:C], ACT.Copy).then_inc(s["d_xT"], 1)
                eng.wait_ge(s["d_td"], t + 1)
                eng.activation(tdiff[:, 1:2], tdiff[:, 0:1], ACT.Exp).then_inc(s["d_w"], 1)
                eng.wait_ge(s["d_sel"], t * 5 + 5)
            with eng.Fori(0, E // 2) as e2:
                for b in range(2):
                    for tb in range(4):
                        g = b * 4 + tb
                        for fc in range(4):
                            eng.wait_ge(s["m_h"], e2 * 32 + (g * 4 + fc + 1))
                            if fc == 0 and g >= 2:
                                eng.wait_ge(s["m_y"], e2 * 32 + (g * 4 - 4))
                            eng.activation(hT[:, tb % 2, fc, :], S[:, fc, :], ACT.Silu).then_inc(s["m_hs"], 1)

        @block.vector
        def _(eng):
            def layer_norm_scales(n):
                for t in range(NT):
                    last = eng.bn_aggr(mv[:, t, :], st[:, t, :])
                    last.then_inc(s["aggr"], 1)
                eng.wait_ge(s["aggr"], NT * (n + 1))
                eng.tensor_scalar(lnt[:, 0, :], mv[:, :, 1], LN_EPS, None, ALU.add).then_inc(s["lns"], 1)
                eng.wait_ge(s["lna"], n + 1)
                eng.reciprocal(lnt[:, 2, :], lnt[:, 1, :]).then_inc(s["lns"], 1)
                eng.wait_ge(s["lns"], 3 * n + 2)
                eng.tensor_tensor(lnt[:, 3, :], lnt[:, 2, :], lnt[:, 2, :], ALU.mult).then_inc(s["lns"], 1)
                eng.wait_ge(s["lns"], 3 * n + 3)
                eng.tensor_tensor(lnt[:, 1, :], lnt[:, 3, :], lnt[:, 0, :], ALU.mult).then_inc(s["rstd_r2"], 1)
                eng.wait_ge(s["rstd_r2"], 2 * n + 1)
                eng.tensor_scalar(lnt[:, 3, :], lnt[:, 1, :], -0.5, 1.5, ALU.mult, ALU.add).then_inc(s["rstd_r2"], 1)
                eng.wait_ge(s["rstd_r2"], 2 * n + 2)
                eng.tensor_tensor(rstd[:, :], lnt[:, 2, :], lnt[:, 3, :], ALU.mult).then_inc(s["rstd_r"], 1)
                eng.wait_ge(s["rstd_r"], 2 * n + 1)
                eng.scalar_tensor_tensor(out=nbias[:, :], in0=mv[:, :, 0], scalar=-1.0, in1=rstd[:, :], op0=ALU.mult, op1=ALU.mult).then_inc(s["rstd_r"], 1)

            n = [0]

            def link(ins):
                n[0] += 1
                ins.then_inc(s["kdv"], 1)
                eng.wait_ge(s["kdv"], n[0])

            eng.wait_ge(s["w_in1"], 48)
            for kt in range(KB):
                eng.wait_ge(s["kvp"], kt + 1)
                eng.tensor_tensor(kv[:, kt, :], S[:, kt, :], bkv[:, :], ALU.add).then_inc(s["kvb"], 1)
            eng.wait_ge(s["kvb"], KB)
            link(eng.tensor_reduce(vmax[:, :], kv[:, :, C:].rearrange("p k c -> p c k"), AX.X, ALU.max, apply_absolute_value=True))
            eng.sem_inc(s["vred"], 2)
            k4 = kv[:, :, 0:C].rearrange("p k (h d) -> p k h d", h=H)
            t4 = ktmp[:, :, :].rearrange("p k (h d) -> p k h d", h=H)
            b4 = lambda a: a[:, :].rearrange("p (k h) -> p k h", k=KB).unsqueeze(3).to_broadcast([P, KB, H, HD])
            flat = ktmp[:, :, :].rearrange("p k c -> p (k c)")
            link(eng.tensor_reduce(kamax[:, :].rearrange("p (k h) -> p k h", k=KB), k4, AX.X, ALU.max, apply_absolute_value=True))
            link(eng.tensor_scalar(kscale[:, :], kamax[:, :], 1.0 / 127.0, Q_EPS, ALU.mult, ALU.max))
            link(eng.reciprocal(kinv[:, :], kscale[:, :]))
            link(eng.tensor_tensor(t4, k4, b4(kinv), ALU.mult))
            link(eng.tensor_scalar(flat, flat, MAGIC, -MAGIC, ALU.add, ALU.add))
            link(eng.tensor_scalar(kscale[:, :], kscale[:, :], -1.0, None, ALU.mult))
            link(eng.tensor_tensor(t4, t4, b4(kscale), ALU.mult))
            eng.wait_ge(s["wall"], 1)
            parts = KC[:, :, :, :].rearrange("p k h (s d) -> p (k h) s d", s=SPLIT)
            tf = ktmp[:, :, :].rearrange("p k (h d) -> p (k h) d", h=H)
            kf = kv[:, :, 0:C].rearrange("p k (h d) -> p k h d", h=H)
            for part in range(3):
                slots = [i for i in range(SPLIT) if i % 3 == part]
                for i in slots:
                    link(eng.tensor_copy(parts[:, :, i, :], tf))
                if part < 2:
                    link(eng.tensor_tensor(tf, tf, parts[:, :, part, :], ALU.subtract))
            eng.sem_inc(s["kct_in"], 1)
            eng.wait_ge(s["vall"], 1)
            link(eng.tensor_scalar(vscale[:, :], vmaxb[:, :], 1.0 / 127.0, Q_EPS, ALU.mult, ALU.max))
            eng.sem_inc(s["vq"], 1)
            link(eng.reciprocal(vinv[:, :], vscale[:, :]))
            link(eng.tensor_tensor(ktmp[:, :, :], kv[:, :, C:], vinv[:, :].unsqueeze(1).to_broadcast([P, KB, C]), ALU.mult))
            link(eng.tensor_scalar(V[:, :, :].rearrange("p k c -> p (k c)"), flat, MAGIC, -MAGIC, ALU.add, ALU.add))
            eng.sem_inc(s["vq"], 1)
            link(eng.tensor_scalar(wscale[:, :], wabs_all[:, :], 1.0 / (C * FF), F_EPS, ALU.mult, ALU.add))
            eng.reciprocal(winv[:, :], wscale[:, :]).then_inc(s["wsc"], 1)
            eng.wait_ge(s["gate_r"], 1)
            eng.tensor_scalar(wdg[:, :], wscale[:, 2:3], gates[:, 2:3], 1.0 / 127.0, ALU.mult, ALU.mult).then_inc(s["wsc"], 1)
            eng.tensor_scalar(gbp[:, :], bp[:, :], gates[:, 0:1], None, ALU.mult).then_inc(s["gbp_r"], 1)
            eng.tensor_scalar(bq[:, :], bq[:, :], 0.25, None, ALU.mult).then_inc(s["wsc"], 1)
            link(eng.tensor_scalar(madd[:, :], maskb[:, :], -1.0, NEG, ALU.add, ALU.mult))
            link(eng.tensor_reduce(valid[:, :], maskb[:, :].rearrange("p (b m) -> p b m", b=BATCH), AX.X, ALU.max))
            eng.tensor_scalar(gvalid[:, :], valid[:, :], gates[:, 1:2], None, ALU.mult).then_inc(s["c_mask"], 1)
            for a in range(CC):
                eng.wait_ge(s["svT"], 1)
                eng.tensor_scalar(wps[:, a, :], wp[:, a, :], PV[:, a * P:a * P + 1], None, ALU.mult).then_inc(s["wps_r"], 1)
            for t in range(NT):
                if t % 4 == 0:
                    eng.wait_ge(s["x_in"], 64)
                eng.bn_stats(st[:, t, :], x[:, t, :]).then_inc(s["st0"], 1)
            eng.wait_ge(s["st0"], NT)
            layer_norm_scales(0)
            for i in range(0, 8, 2):
                eng.wait_ge(s["kct"], i + 1)
                eng.tensor_copy(KT[:, 0:8, P * (i // 2):P * (i // 2) + P],
                                Tb[:, 0, :].rearrange("p (a b) -> p a b", a=8)).then_inc(s["kevD"], 1)

            def q_scale(u):
                if not (isinstance(u, int) and u == 0):
                    eng.wait_ge(s["qprep"], 9 * u)
                eng.wait_ge(s["qp_r"], u + 1)
                eng.scalar_tensor_tensor(out=q[:, :], in0=QB[:, 0:C], scalar=0.25, in1=bq[:, :], op0=ALU.mult, op1=ALU.add).then_inc(s["q_r"], 1)
                eng.wait_ge(s["q_r"], u + 1)
                eng.tensor_reduce(qamax[:, :], q[:, :].rearrange("p (h d) -> p h d", h=H), AX.X, ALU.max, apply_absolute_value=True).then_inc(s["qa_r"], 1)
                eng.wait_ge(s["qa_r"], u + 1)
                eng.tensor_scalar(qscale[:, :], qamax[:, :], 1.0 / 127.0, Q_EPS, ALU.mult, ALU.max).then_inc(s["qsc_r"], 1)
                eng.wait_ge(s["qsc_r"], u + 1)
                eng.reciprocal(qinv[:, :], qscale[:, :]).then_inc(s["qi_r"], 1)

            def q_half(u, half):
                r, d = (("qA_r", "qtA_r"), ("qB_r", "qtB_r"))[half]
                eng.wait_ge(s[r], u + 1)
                eng.tensor_copy(QT[:, 8 * half:8 * half + 8, :],
                                QBb.rearrange("p (a b) -> p a b", a=8)).then_inc(s[d], 1)

            def body(t, main, prev, nxt):
                first = not prev
                for h in range(16):
                    if main:
                        eng.wait_ge(s["score_r"], t * 16 + (h + 1))
                        if prev:
                            eng.wait_ge(s["exp_r"], t * 16 + (h - 15))
                        eng.tensor_scalar(junk[:, h % 4, :], S[:, h % 4, :], LN255, None, ALU.add, ALU.min,
                                          accum_out=ebias[:, h:h + 1]).then_inc(s["nb_r"], 1)
                    if h % 2:
                        tt, j = back(t, h // 2 - 2)
                        if j in DVE_PAIRS and (h >= 5 or prev) and (main or h < 5):
                            eng.wait_ge(s["tr_r"], tt * 8 + (j + 1))
                            if not (first and j < 4):
                                eng.wait_ge(s["pv_r"], tt * 8 + (j - 3))
                            eng.tensor_copy(PT[:, j % 4, :], Ti[:, j % 2, :]).then_inc(s["evD"], 1)
                    if h == 2 and main:
                        q_half(t, 1)
                    if h == 1 and prev:
                        eng.wait_ge(s["exp_r"], t * 16)
                        eng.reciprocal(rsum[:, 8:16], esum[:, 8:16]).then_inc(s["rs_r"], 1)
                    if h == 6 and nxt:
                        q_scale(t + 1)
                    if h == 7 and prev:
                        eng.wait_ge(s["pv_r"], t * 8)
                        eng.wait_ge(s["rs_r"], t * 2)
                        if not (isinstance(t, int) and t == 1):
                            eng.wait_ge(s["aoT_r"], t - 1) if isinstance(t, int) else None
                        eng.tensor_tensor(ao[:, :].rearrange("p (h d) -> p h d", h=H), PV[:, 0:C].rearrange("p (h d) -> p h d", h=H),
                                          rsum[:, :].unsqueeze(2).to_broadcast([P, H, HD]), ALU.mult).then_inc(s["ao_r"], 1)
                    if h == 12 and prev:
                        eng.wait_ge(s["op_r"], t)
                        eng.wait_ge(s["xb_r"], t)
                        w = t - 1
                        eng.scalar_tensor_tensor(out=x[:, w, :], in0=QB[:, 0:C], scalar=gates[:, 0:1], in1=x[:, w, :],
                                                 op0=ALU.mult, op1=ALU.add).then_inc(s["x1_r"], 1)
                        eng.wait_ge(s["x1_r"], t)
                        eng.bn_stats(st[:, w, :], x[:, w, :]).then_inc(s["bs_r"], 1)
                    if h == 13 and main:
                        eng.wait_ge(s["exp_r"], t * 16 + 8)
                        if prev:
                            eng.wait_ge(s["ao_r"], t)
                        eng.reciprocal(rsum[:, 0:8], esum[:, 0:8]).then_inc(s["rs_r"], 1)
                    if h == 15 and nxt:
                        q_half(t + 1, 0)

            q_scale(0)
            q_half(0, 0)
            body(0, True, False, True)
            with eng.Fori(1, NT - 1) as t:
                body(t, True, True, True)
            body(NT - 1, True, True, False)
            body(NT, False, True, False)

            eng.wait_ge(s["bs_r"], NT)
            layer_norm_scales(1)

            def f_scale(u):
                eng.wait_ge(s["f_xh"], u + 1)
                eng.tensor_reduce(fmax[:, :], xh[:, :], AX.X, ALU.max, apply_absolute_value=True).then_inc(s["f_max"], 1)
                eng.wait_ge(s["f_max"], u + 1)
                eng.tensor_scalar(fs[:, :], fmax[:, :], F_EPS, 1.0 / 127.0, ALU.max, ALU.mult).then_inc(s["f_s"], 1)
                eng.wait_ge(s["f_s"], u + 1)
                eng.reciprocal(finv[:, :], fs[:, :]).then_inc(s["f_inv"], 1)

            def f_scales2(u):
                if not (isinstance(u, int) and u == 0):
                    eng.wait_ge(s["f_sig"], 2 * u)
                    eng.wait_ge(s["f_hs"], 3 * u)
                eng.tensor_scalar(fg[:, 0:1], fs[:, :], wscale[:, 0:1], None, ALU.mult).then_inc(s["f_fg"], 1)
                eng.tensor_scalar(fu[:, 0:1], fs[:, :], wscale[:, 1:2], None, ALU.mult).then_inc(s["f_fg"], 1)
                eng.wait_ge(s["f_fg"], 2 * u + 2)

            def f_hidden(t):
                if not (isinstance(t, int) and t == 0):
                    eng.wait_ge(s["f_hq"], 2 * t)
                for k in range(2):
                    eng.wait_ge(s["f_sig"], 2 * t + (k + 1))
                    eng.tensor_tensor(hid[:, 512 * k:512 * k + 512], S[:, 2 * k + 1, :], sig[:, k, :], ALU.mult).then_inc(s["f_h"], 1)
                eng.wait_ge(s["f_h"], 2 * t + 2)
                eng.tensor_reduce(hmax[:, :], hid[:, :], AX.X, ALU.max, apply_absolute_value=True).then_inc(s["f_hm"], 1)
                eng.wait_ge(s["f_hm"], t + 1)
                eng.tensor_scalar(hs[:, :], hmax[:, :], fu[:, 0:1], F_EPS, ALU.mult, ALU.max).then_inc(s["f_hs"], 1)
                eng.wait_ge(s["f_hs"], 3 * t + 1)
                eng.reciprocal(hinv[:, :], hs[:, :]).then_inc(s["f_hs"], 1)
                eng.wait_ge(s["f_hs"], 3 * t + 2)
                eng.tensor_scalar(hf[:, :], hinv[:, :], fu[:, 0:1], 127.0, ALU.mult, ALU.mult).then_inc(s["f_hf"], 1)
                eng.tensor_scalar(ho[:, :], hs[:, :], wdg[:, 0:1], None, ALU.mult).then_inc(s["f_hs"], 1)

            def f_out(t):
                eng.wait_ge(s["f_dn"], t + 1)
                eng.wait_ge(s["f_hs"], 3 * t + 3)
                eng.scalar_tensor_tensor(out=x[:, t, :], in0=PV[:, 0:C], scalar=ho[:, 0:1], in1=x[:, t, :],
                                         op0=ALU.mult, op1=ALU.add).then_inc(s["f_x"], 1)
                eng.wait_ge(s["f_x"], t + 1)
                eng.bn_stats(st[:, t, :], x[:, t, :]).then_inc(s["f_bs"], 1)

            f_scale(0)
            f_scales2(0)
            f_scale(1)
            f_hidden(0)
            f_scales2(1)
            with eng.Fori(1, NT - 1) as t:
                f_scale(t + 1)
                f_out(t - 1)
                f_hidden(t)
                f_scales2(t + 1)
            f_out(NT - 2)
            f_hidden(NT - 1)
            f_out(NT - 1)

            eng.wait_ge(s["f_bs"], NT)
            layer_norm_scales(2)
            eng.wait_ge(s["c_mask"], 1)
            with eng.Fori(0, BATCH) as b:
                for i in range(2):
                    eng.wait_ge(s["c_sc"], b * 2 + (i + 1))
                    eng.scalar_tensor_tensor(out=sm[:, i, :], in0=S[:, 2 + i, 0:M], scalar=1.0 / 16.0,
                                             in1=madd[:, bass.ds(b * M, M)], op0=ALU.mult, op1=ALU.add).then_inc(s["c_sm"], 1)
                for i in range(2):
                    eng.wait_ge(s["c_sm"], b * 2 + (i + 1))
                    eng.tensor_reduce(smax[:, i:i + 1], sm[:, i, :], AX.X, ALU.max, negate=True).then_inc(s["c_mx"], 1)
                for i in range(2):
                    eng.wait_ge(s["c_ex"], b * 2 + (i + 1))
                    eng.reciprocal(srec[:, i:i + 1], ssum[:, i:i + 1]).then_inc(s["c_rc"], 1)
                for i in range(2):
                    eng.wait_ge(s["c_rc"], b * 2 + (i + 1))
                    eng.tensor_scalar(sfac[:, i:i + 1], srec[:, i:i + 1], gvalid[:, bass.ds(b, 1)], None, ALU.mult).then_inc(s["c_f"], 1)
                for i in range(2):
                    eng.wait_ge(s["c_rd"], b * 2 + (i + 1))
                    eng.wait_ge(s["c_f"], b * 2 + (i + 1))
                    eng.scalar_tensor_tensor(out=x[:, b * 2 + i, :], in0=(PV, QB)[i][:, 0:C], scalar=sfac[:, i:i + 1],
                                             in1=x[:, b * 2 + i, :], op0=ALU.mult, op1=ALU.add).then_inc(s["c_x"], 1)
                for i in range(2):
                    eng.wait_ge(s["c_x"], b * 2 + (i + 1))
                    eng.bn_stats(st[:, b * 2 + i, :], x[:, b * 2 + i, :]).then_inc(s["c_bs"], 1)

            eng.wait_ge(s["c_bs"], NT)
            layer_norm_scales(3)
            with eng.Fori(0, NT) as t:
                eng.wait_ge(s["d_lg"], t + 1)
                eng.tensor_copy(xTa[:, :, bass.ds(t * P, P)], xT[:, :].rearrange("p (a b) -> p a b", a=CC)).then_inc(s["d_xTa"], 1)
                eng.tensor_copy(lg[:, :], S[:, 1, 0:E]).then_inc(s["d_lgs"], 1)
                eng.wait_ge(s["gate_r"], 1)
                eng.wait_ge(s["d_lgs"], t + 1)
                eng.max(top[:, :], lg[:, :]).then_inc(s["d_top"], 1)
                eng.wait_ge(s["gate_r"], 1)
                eng.wait_ge(s["d_top"], t + 1)
                eng.max_index(topi[:, :], top[:, :], lg[:, :]).then_inc(s["d_topi"], 1)
                eng.tensor_tensor(tdiff[:, 0:1], top[:, 1:2], top[:, 0:1], ALU.subtract).then_inc(s["d_td"], 1)
                eng.wait_ge(s["d_topi"], t * 2 + 1)
                eng.tensor_copy(topf[:, :], topi[:, :]).then_inc(s["d_topi"], 1)
                eng.wait_ge(s["d_topi"], t * 2 + 2)
                eng.wait_ge(s["d_w"], t + 1)
                eng.tensor_scalar(srec[:, 0:1], tdiff[:, 1:2], 1.0, None, ALU.add).then_inc(s["d_sel"], 1)
                eng.wait_ge(s["d_sel"], t * 5 + 1)
                eng.reciprocal(srec[:, 1:2], srec[:, 0:1]).then_inc(s["d_sel"], 1)
                eng.wait_ge(s["d_sel"], t * 5 + 2)
                eng.tensor_scalar(sfac[:, 0:1], srec[:, 1:2], gates[:, 3:4], None, ALU.mult).then_inc(s["d_sel"], 1)
                eng.wait_ge(s["d_sel"], t * 5 + 3)
                eng.tensor_scalar(sfac[:, 1:2], sfac[:, 0:1], tdiff[:, 1:2], None, ALU.mult).then_inc(s["d_sel"], 1)
                eng.wait_ge(s["d_sel"], t * 5 + 4)
                eng.tensor_scalar(sel[:, 0, :], iota[:, :], topf[:, 0:1], sfac[:, 0:1], ALU.is_equal, ALU.mult).then_inc(s["d_sel2"], 1)
                eng.tensor_scalar(sel[:, 1, :], iota[:, :], topf[:, 1:2], sfac[:, 1:2], ALU.is_equal, ALU.mult).then_inc(s["d_sel2"], 1)
                eng.wait_ge(s["d_sel2"], t * 2 + 2)
                eng.tensor_tensor(G[:, t, :], sel[:, 0, :], sel[:, 1, :], ALU.add).then_inc(s["d_sel"], 1)
                eng.wait_ge(s["d_sel"], t * 5 + 5)
            with eng.Fori(0, E // 2) as e2:
                for b in range(2):
                    for tile in range(NT):
                        y = (T[:, 0, :], T[:, 1, :], PV[:, :], QB[:, :])[tile % 4]
                        eng.wait_ge(s["m_y"], e2 * 32 + (b * 16 + tile + 1))
                        eng.wait_ge(s["m_x"], e2 * 32 + (b * 16 + tile - 15)) if not (b == 0) else None
                        eng.scalar_tensor_tensor(out=x[:, tile, :], in0=y[:, 0:C], scalar=G[:, tile, bass.ds(e2 * 2 + b, 1)],
                                                 in1=x[:, tile, :], op0=ALU.mult, op1=ALU.add).then_inc(s["m_x"], 1)
                eng.wait_ge(s["m_x"], e2 * 32 + 32)

        @block.tensor
        def _(eng):
            eng.wait_ge(s["w_in1"], 48)
            for kt in range(KB):
                for a in range(CC):
                    mm = eng.matmul(S[:, kt, :], ctxT[:, a, kt * P:kt * P + P], wkv[:, a, :], start=a == 0, stop=a == CC - 1)
                mm.then_inc(s["kvp"], 1)
            eng.wait_ge(s["consts"], 3)
            eng.wait_ge(s["vq"], 1)
            for a in range(CC):
                mm = eng.transpose(PV[:, a * P:a * P + P], vscale[:, a * P:a * P + P], ident[:, :])
            mm.then_inc(s["svT"], 1)
            eng.wait_ge(s["kct_in"], 1)
            for i in range(8):
                kt, half = i // 2, i % 2
                if i >= 2:
                    eng.wait_ge(s["kev" if half else "kevD"], i // 2)
                for k in range(8):
                    mm = eng.transpose(Tb[:, half, k * P:k * P + P], KC[:, kt, 8 * half + k, :], identb[:, :])
                mm.then_inc(s["kct"], 1)

            def q_xhT(u):
                eng.wait_ge(s["xh_r"], u + 1)
                for a in range(CC):
                    mm = eng.transpose(QB[:, a * P:a * P + P], xh[:, a * P:a * P + P], ident[:, :])
                mm.then_inc(s["xhT_r"], 1)

            def q_proj(u):
                eng.wait_ge(s["xT_r"], u + 1)
                for a in range(CC):
                    mm = eng.matmul(QB[:, 0:C], xT[:, a * P:a * P + P], wq[:, a, :], start=a == 0, stop=a == CC - 1)
                mm.then_inc(s["qp_r"], 1)

            def q_turn(u, half):
                for k in range(8):
                    mm = eng.transpose(QBb[:, k * P:k * P + P], QC[:, 8 * half + k, :], identb[:, :])
                mm.then_inc(s[("qA_r", "qB_r")[half]], 1)

            def body(t, main, prev, nxt):
                first = not prev
                for h in range(16):
                    if main:
                        if h == 0:
                            eng.wait_ge(s["qtA_r"], t + 1)
                        if h == 8:
                            eng.wait_ge(s["qtB_r"], t + 1)
                        if not (first and h < 4):
                            eng.wait_ge(s["exp_r"], t * 16 + (h - 3))
                        eng.matmul(S[:, h % 4, :], QT[:, h, :], KT[:, h, :], start=True, stop=True).then_inc(s["score_r"], 1)
                    if h % 2:
                        tt, j = back(t, h // 2 - 2)
                        if (h >= 5 or prev) and (main or h < 5):
                            eng.wait_ge(s["exp_r"], tt * 16 + (2 * j + 2))
                            if not (first and j < 2):
                                eng.wait_ge(*ev_sem(*back(tt, j - 2)))
                            for k in range(2 * KB):
                                mm = eng.transpose(Tb[:, j % 2, k * P:k * P + P], Rb[:, j % 4, k // KB, (k % KB) * P:(k % KB) * P + P], identb[:, :])
                            mm.then_inc(s["tr_r"], 1)
                        tt, j = back(t, h // 2 - 3)
                        if (h >= 7 or prev) and (main or h < 7):
                            eng.wait_ge(*ev_sem(tt, j))
                            if j == 0 and prev:
                                eng.wait_ge(s["ao_r"], tt)
                            for k in range(2 * KB):
                                hh = 2 * j + k // KB
                                mm = eng.matmul(PV[:, hh * HD:hh * HD + HD], PT[:, j % 4, k * P:k * P + P],
                                                V[:, k % KB, hh * HD:hh * HD + HD], start=k % KB == 0, stop=k % KB == KB - 1)
                            mm.then_inc(s["pv_r"], 1)
                    if h == 1 and main:
                        eng.wait_ge(s["qtA_r"], t + 1)
                        q_turn(t, 1)
                    if h == 3 and nxt:
                        eng.wait_ge(s["qtB_r"], t + 1)
                        q_xhT(t + 1)
                    if h == 6 and nxt:
                        q_proj(t + 1)
                    if h == 8 and prev:
                        eng.wait_ge(s["ao_r"], t)
                        if nxt:
                            eng.wait_ge(s["q_r"], t + 2)
                        for a in range(CC):
                            mm = eng.transpose(QB[:, a * P:a * P + P], ao[:, a * P:a * P + P], ident[:, :])
                        mm.then_inc(s["aoT_r"], 1)
                    if h == 11 and prev:
                        eng.wait_ge(s["aoTe_r"], t)
                        for a in range(CC):
                            mm = eng.matmul(QB[:, 0:C], aoT[:, a * P:a * P + P], wps[:, a, :], start=a == 0, stop=a == CC - 1)
                        mm.then_inc(s["op_r"], 1)
                    if h == 14 and nxt:
                        if prev:
                            eng.wait_ge(s["x1_r"], t)
                        eng.wait_ge(s["qprep"], 9 * (t + 1) + 9)
                        q_turn(t + 1, 0)

            eng.wait_ge(s["w_in2"], 96)
            q_xhT(0)
            q_proj(0)
            eng.wait_ge(s["qprep"], 9)
            q_turn(0, 0)
            eng.wait_ge(s["kevD"], 4)
            eng.wait_ge(s["kev"], 4)
            eng.wait_ge(s["vq"], 2)
            eng.wait_ge(s["wps_r"], CC)
            body(0, True, False, True)
            with eng.Fori(1, NT - 1) as t:
                body(t, True, True, True)
            body(NT - 1, True, True, False)
            body(NT, False, True, False)

            def f_turn_x(u):
                eng.wait_ge(s["f_rq"], 2 * u + 2)
                if not (isinstance(u, int) and u == 0):
                    eng.wait_ge(s["f_xiTe"], u)
                for a in range(CC):
                    mm = eng.transpose(Tb[:, 0, a * P:a * P + P], xi[:, a * P:a * P + P], identb[:, :])
                mm.then_inc(s["f_xiT"], 1)

            def f_gate_up(t):
                eng.wait_ge(s["f_xiTe"], t + 1)
                for k in range(2):
                    if not (isinstance(t, int) and t == 0):
                        eng.wait_ge(s["f_h"], 2 * t + (k - 1))
                    for w in range(2):
                        for a in range(CC):
                            mm = eng.matmul(S[:, 2 * k + w, :], xiT[:, a * P:a * P + P],
                                            wi[w][:, a * FF + 512 * k:a * FF + 512 * k + 512], start=a == 0, stop=a == CC - 1)
                    mm.then_inc(s["f_gu"], 1)

            def f_down(t):
                eng.wait_ge(s["f_hq"], 2 * t + 2)
                if not (isinstance(t, int) and t == 0):
                    eng.wait_ge(s["f_hiTe"], t)
                for k in range(8):
                    mm = eng.transpose(Tb[:, 1, k * P:k * P + P], hi[:, k * P:k * P + P], identb[:, :])
                mm.then_inc(s["f_hiT"], 1)

            def f_down2(t):
                eng.wait_ge(s["f_hiTe"], t + 1)
                if not (isinstance(t, int) and t == 0):
                    eng.wait_ge(s["f_x"], t)
                for k in range(8):
                    mm = eng.matmul(PV[:, 0:C], hiT[:, k * P:k * P + P], wi[2][:, k * C:k * C + C], start=k == 0, stop=k == 7)
                mm.then_inc(s["f_dn"], 1)

            eng.wait_ge(s["wpool"], 9)
            f_turn_x(0)
            f_gate_up(0)
            f_turn_x(1)
            f_down(0)
            with eng.Fori(1, NT - 1) as t:
                f_gate_up(t)
                f_down2(t - 1)
                f_turn_x(t + 1)
                f_down(t)
            f_gate_up(NT - 1)
            f_down2(NT - 2)
            f_down(NT - 1)
            f_down2(NT - 1)

            eng.wait_ge(s["f_x"], NT)
            with eng.Fori(0, BATCH) as b:
                for i in range(2):
                    eng.wait_ge(s["c_xh"], b * 2 + (i + 1))
                    for a in range(CC):
                        mm = eng.transpose(S[:, i, a * P:a * P + P], xh2[:, i, a * P:a * P + P], ident[:, :])
                    mm.then_inc(s["c_xhT"], 1)
                for i in range(2):
                    eng.wait_ge(s["c_xT"], b * 2 + (i + 1))
                    for a in range(CC):
                        mm = eng.matmul(S[:, 2 + i, 0:M], xT2[:, i, a * P:a * P + P], ctxT[:, a, bass.ds(b * M, M)],
                                        start=a == 0, stop=a == CC - 1)
                    mm.then_inc(s["c_sc"], 1)
                for i in range(2):
                    eng.wait_ge(s["consts"], 3)
                    eng.wait_ge(s["c_ex"], b * 2 + (i + 1))
                    eng.transpose(T[0:M, i, 0:P], pe_[:, i, :], ident[:, :]).then_inc(s["c_pT"], 1)
                for i in range(2):
                    eng.wait_ge(s["consts"], 3)
                    eng.wait_ge(s["c_pTe"], b * 2 + (i + 1))
                    eng.matmul((PV, QB)[i][:, 0:C], pT[:, i, :], ctxn[:, b, :], start=True, stop=True).then_inc(s["c_rd"], 1)

            with eng.Fori(0, NT) as t:
                eng.wait_ge(s["d_xh"], t + 1)
                for a in range(CC):
                    mm = eng.transpose(S[:, 0, a * P:a * P + P], xh[:, a * P:a * P + P], ident[:, :])
                mm.then_inc(s["d_xhT"], 1)
                eng.wait_ge(s["d_xT"], t + 1)
                for a in range(CC):
                    mm = eng.matmul(S[:, 1, 0:E], xT[:, a * P:a * P + P], wr[:, a, :], start=a == 0, stop=a == CC - 1)
                mm.then_inc(s["d_lg"], 1)
            eng.wait_ge(s["d_xTa"], NT)
            eng.wait_ge(s["d_sel"], 5 * NT)
            with eng.Fori(0, E // 2) as e2:
                for b in range(2):
                    eng.wait_ge(s[f"m_w{b}"], e2 * 32 + 32)
                    for tb in range(4):
                        for fc in range(4):
                            if not (b == 0 and tb == 0):
                                eng.wait_ge(s["m_hs"], e2 * 32 + (b * 16 + tb * 4 + fc - 3))
                            for a in range(CC):
                                mm = eng.matmul(S[:, fc, :], win[:, b, a, fc * P:fc * P + P], xTa[:, a, tb * 512:tb * 512 + 512],
                                                start=a == 0, stop=a == CC - 1)
                            mm.then_inc(s["m_h"], 1)
                        for k in range(4):
                            tile = tb * 4 + k
                            y = (T[:, 0, :], T[:, 1, :], PV[:, :], QB[:, :])[k]
                            eng.wait_ge(s["m_hs"], e2 * 32 + (b * 16 + tb * 4 + 4))
                            if not (b == 0 and tb == 0):
                                eng.wait_ge(s["m_x"], e2 * 32 + (b * 16 + tile - 3))
                            for fc in range(4):
                                mm = eng.matmul(y[:, 0:C], hT[:, tb % 2, fc, k * P:k * P + P], wout[:, b, fc, :],
                                                start=fc == 0, stop=fc == 3)
                            mm.then_inc(s["m_y"], 1)
                eng.wait_ge(s["m_x"], e2 * 32 + 32)


def kernel(**inputs):
    import numpy as _np
    import concourse.bacc as _bacc
    from concourse import mybir as _mybir
    from concourse.bass_utils import run_bass_kernel_spmd as _run

    a = {k: _np.asarray(v) for k, v in inputs.items()}
    laid = {
        "x": a["x"].reshape(TOKENS, C),
        "ctx": a["ctx_2048"].reshape(KEYS, C),
        "ctxT": a["ctx_2048"].reshape(KEYS, C).T,
        "mask": a["mask_BxS2_bk0"].reshape(BATCH * M),
        "gx": a["g_xattn"], "gf": a["g_ffn"],
        "wq": a["L0_xattn_Wq"], "bq": a["L0_xattn_bq"], "wkv": a["L0_xattn_Wkv"], "bkv": a["L0_xattn_bkv"],
        "wp": a["L0_xattn_Wp"], "bp": a["L0_xattn_bp"],
        "wg": a["L0_ffn_w_gate"].T, "wu": a["L0_ffn_w_up"].T, "wd": a["L0_ffn_w_down"].T,
        "wr": a["L1_ffn_Wr"].T, "win": a["L1_ffn_Win"].transpose(0, 2, 1), "wout": a["L1_ffn_Wout"].transpose(0, 2, 1),
    }
    nc = _bacc.Bacc("TRN2", target_bir_lowering=False, num_devices=1)
    arrays, args = {}, []
    for name, v in laid.items():
        v = _np.ascontiguousarray(v)
        arrays[f"in_{name}_dram"] = v
        args.append(nc.dram_tensor(f"in_{name}_dram", v.shape, _mybir.dt.from_np(v.dtype), kind="ExternalInput").ap())
    args.append(nc.dram_tensor("out_dram", (TOKENS, C), F32, kind="ExternalOutput").ap())
    flamingo_kernel(nc, *args)
    r = _run(nc, [arrays], core_ids=[0])
    return r.results[0]["out_dram"].reshape(8, 256, C)
```

```python
import concourse.bass as bass
from concourse import mybir

ReduceOp = bass.bass_isa.ReduceOp
from contextlib import ExitStack

F32 = mybir.dt.float32
BF16 = mybir.dt.bfloat16
I16 = mybir.dt.int16
U8 = mybir.dt.uint8
U32 = mybir.dt.uint32
I32 = mybir.dt.int32
ALU = mybir.AluOpType
ACT = mybir.ActivationFunctionType
AX = mybir.AxisListType

P = 128
TOKENS, C = 2048, 256
NT = TOKENS // P
CC = C // P
KEYS = 512
KB = KEYS // P
H, HD = 16, 16
BATCH, M = 8, 64
FF = 1024
E, DI = 8, 512
TOPK = 2
SLOTS = (TOPK * TOKENS + E * (P - 1)) // P
SPLIT = 8
MAGIC = 12582912.0
LN255 = 5.541263545158426
LN_EPS = 1e-5
Q_EPS = 1e-8
F_EPS = 1e-5
NEG = 1e30
ACT_PAIRS = (1, 3, 5, 7)
DVE_PAIRS = tuple(j for j in range(8) if j not in ACT_PAIRS)


def flamingo_kernel(nc, x_d, ctx_d, ctxT_d, mask_d, gx_d, gf_d, wq_d, bq_d, wkv_d, bkv_d, wp_d, bp_d,
                    wg_d, wu_d, wd_d, wr_d, win_d, wout_d, out_d):
    xn_d = nc.dram_tensor("normalised", (TOKENS, C), F32).ap()
    stack = ExitStack()
    with stack:
        def sb(name, shape, dt=F32):
            return stack.enter_context(nc.sbuf_tensor(name, shape, dt))

        def pb(name, shape, dt=F32):
            return stack.enter_context(nc.psum_tensor(name, shape, dt))

        def sem(name):
            return stack.enter_context(nc.semaphore(name))

        x = sb("x_tokens", [P, NT, C])
        ident = sb("ident", [P, P])
        identb = sb("identb", [P, P], BF16)
        gates = sb("gates", [P, 4])
        graw = sb("graw", [P, 4])
        ctxT = sb("ctxT", [P, CC, KEYS])
        ctxn = sb("ctxn", [M, BATCH, C])
        wq = sb("wq", [P, CC, C])
        wkv = sb("wkv", [P, CC, 2 * C])
        wp = sb("wp", [P, CC, C])
        wps = sb("wps", [P, CC, C])
        bq = sb("bq", [P, C])
        bkv = sb("bkv", [P, 2 * C])
        bp = sb("bp", [P, C])
        wr = sb("wr", [P, CC, E])
        big = sb("big", [P, E * (CC * DI + DI // P * C)])
        WIN, WOUT = big[:, 0:E * CC * DI], big[:, E * CC * DI:]
        KC = big[:, 0:4096].bitcast(BF16).rearrange("p (k h d) -> p k h d", k=KB, h=H)
        KT = big[:, 4096:8192].bitcast(BF16).rearrange("p (h k) -> p h k", h=H)
        wf = [big[:, 8192 + i * CC * FF:8192 + (i + 1) * CC * FF] for i in range(3)]
        R = big[:, 14336:16384].bitcast(I16).rearrange("p (a b c) -> p a b c", a=4, b=2)
        wi = [sb("wgi", [P, CC * FF], BF16), sb("wui", [P, CC * FF], BF16), sb("wdi", [P, CC * FF], BF16)]
        maskb = sb("maskb", [P, BATCH * M], U8)
        madd = sb("madd", [P, BATCH * M])
        valid = sb("valid", [P, BATCH])
        kv = sb("kv", [P, KB, 2 * C])
        ktmp = sb("ktmp", [P, KB, C])
        kamax = sb("kamax", [P, KB * H])
        kscale = sb("kscale", [P, KB * H])
        kinv = sb("kinv", [P, KB * H])
        vmax = sb("vmax", [P, C])
        vmaxb = sb("vmaxb", [P, C])
        vscale = sb("vscale", [P, C])
        vinv = sb("vinv", [P, C])
        V = sb("V", [P, KB, C], BF16)
        wabs = sb("wabs", [P, 3])
        wabs_all = sb("wabs_all", [P, 3])
        wscale = sb("wscale", [P, 3])
        winv = sb("winv", [P, 3])
        st = sb("st", [P, NT, 6])
        mv = sb("mv", [P, NT, 2])
        lnt = sb("lnt", [P, 4, NT])
        rstd = sb("rstd", [P, NT])
        nbias = sb("nbias", [P, NT])
        xh = sb("xh", [P, C])
        xT = sb("xT", [P, C])
        q = sb("q", [P, C])
        qy = sb("qy", [P, C])
        qr = sb("qr", [P, C])
        qamax = sb("qamax", [P, H])
        qscale = sb("qscale", [P, H])
        qinv = sb("qinv", [P, H])
        QC = sb("QC", [P, H, SPLIT * HD], BF16)
        QT = sb("QT", [P, H, P], BF16)
        junk = ktmp[:, :, :].rearrange("p k c -> p (k c)").bitcast(BF16).rearrange("p (a k) -> p a k", a=4)
        ebias = sb("ebias", [P, H])
        PT = sb("PT", [P, 4, 2 * KB * P], BF16)
        esum = sb("esum", [P, H])
        rsum = sb("rsum", [P, H])
        ao = sb("ao", [P, C])
        aoT = sb("aoT", [P, C])
        gbp = sb("gbp", [P, C])
        fmax = sb("fmax", [P, 1])
        fs = sb("fs", [P, 1])
        finv = sb("finv", [P, 1])
        fg = sb("fg", [P, 2])
        fu = sb("fu", [P, 2])
        xq = sb("xq", [P, C])
        xi = sb("xi", [P, C], BF16)
        xiT = sb("xiT", [P, C], BF16)
        sig_ = sb("sig", [P, FF])
        sig = sig_[:, :].rearrange("p (k f) -> p k f", k=2)
        hid_ = sb("hid", [P, FF])
        hid = hid_
        hmax = sb("hmax", [P, 1])
        hs = sb("hs", [P, 1])
        hinv = sb("hinv", [P, 1])
        hf = sb("hf", [P, 1])
        ho = sb("ho", [P, 1])
        wdg = sb("wdg", [P, 1])
        hq = sb("hq", [P, FF])
        hi = sb("hi", [P, FF], BF16)
        hiT = sb("hiT", [P, FF], BF16)
        xh2 = sb("xh2", [P, 2, C])
        xT2 = sb("xT2", [P, 2, C])
        sm = sb("sm", [P, 2, M])
        smax = sb("smax", [P, 2])
        pe_ = sb("pe_", [P, 2, M])
        ssum = sb("ssum", [P, 2])
        srec = sb("srec", [P, 2])
        sfac = sb("sfac", [P, 2])
        pT = sb("pT", [M, 2, P])
        gvalid = sb("gvalid", [P, BATCH])
        xr = sig_[:, :].rearrange("p (i c) -> p i c", i=4)
        xrT = hid_[:, :].rearrange("p (i c) -> p i c", i=4)
        lg = sb("lg", [P, 4, E])
        top = sb("top", [P, 4, 8])
        topi = sb("topi", [P, 4, 8], U32)
        topv = sb("topv", [P, NT, TOPK])
        topx = sb("topx", [P, NT, TOPK])
        gw = sb("gw", [P, 3, NT])
        gk = sb("gk", [P, TOPK, NT])
        pick = sb("pick", [P, TOPK, NT, E])
        picks = sb("picks", [P, NT + 1, E], BF16)
        picked = sb("picked", [P, TOPK, NT, E])
        order = sb("order", [P, NT, E])
        block_ = sb("block", [P, NT, E])
        row_ = sb("row", [P, NT, E])
        tok_row = sb("tok_row", [P, TOPK * NT])
        tok_tile = sb("tok_tile", [P, TOPK * NT])
        cnt = sb("cnt", [P, E])
        tiles_of = sb("tiles_of", [P, E])
        lower = sb("lower", [P, E, E])
        lowprod = sb("lowprod", [P, E, E])
        base = sb("base", [P, E])
        upto = sb("upto", [P, E])
        ended = sb("ended", [P, SLOTS, E])
        tile_e = sb("tile_e", [P, SLOTS])
        tile_off = sb("tile_off", [P, SLOTS], I32)
        iota = sb("iota", [P, P])
        token1 = sb("token1", [P, NT])
        padrow = sb("padrow", [P, 1])
        trib = sb("trib", [P, P], BF16)
        onesb = sb("onesb", [P, P], BF16)
        hitr = sb("hitr", [P, 4, P])
        hitt = sb("hitt", [P, 4, 2, SLOTS])
        zeros = sb("zeros", [P, 2 * SLOTS])
        slot = sb("slot", [P, 2, SLOTS])
        empty = sb("empty", [P, SLOTS])
        slot_in = sb("slot_in", [P, SLOTS], U32)
        slot_out = sb("slot_out", [P, SLOTS], U32)
        rows_in = sb("rows_in", [P, 2], U32)
        rows_out = sb("rows_out", [P, 2], U32)
        xg = sb("xg", [P, 2, C])
        xgT = sb("xgT", [P, 2, C])
        hact, hactT = kv[:, 0:2, :], kv[:, 2:4, :]
        yo = ktmp[:, 0:2, :]

        S = pb("S", [P, 4, 512])
        T = pb("T", [P, 2, 512])
        PV = pb("PV", [P, 512])
        QB = pb("QB", [P, 512])

        names = """x_in w_in1 w_in2 w_in3 consts iota_r gate_r
            kvp kvb kdv kct kev vred vall vq svT wps_r wabs_r wall wsc wpool wpool_done
            st0 aggr lns lna rstd_r
            xh_r xhT_r xT_r qp_r q_r qa_r qsc_r qi_r qprep qA_r qtA_r qB_r qtB_r
            score_r nm_r nb_r exp_r tr_r evD evA pv_r rs_r ao_r aoT_r aoTe_r op_r xb_r x1_r bs_r gbp_r
            f_xh f_max f_s f_inv f_fg f_rq f_xiT f_xiTe f_gu f_sig f_h f_hm f_hs f_hi f_hf f_hq f_hiT f_hiTe f_dn f_x f_bs
            c_xh c_xhT c_xT c_sc c_sm c_mx c_ex c_rc c_f c_pT c_pTe c_rd c_x c_bs c_mask
            rt_xh rt_T rt_xT rt_lg rt_lgs rt_top rt_topi rt_sel rt rt_gap rt_exp rt_const rt_picks rt_order
            rt_store rt_hit rt_mm rt_slots
            w_exp ex_in0 ex_in1 ex_from ex_turn ex_xT ex_h ex_act ex_hT ex_hTe ex_y ex_yo ex_add out_init
            apart apart_d rstd_r2 kct_in kevD""".split()
        s = {n: sem("s_" + n) for n in names}
        block = stack.enter_context(nc.Block())

        def ev_sem(t, j):
            if j in ACT_PAIRS:
                return s["evA"], t * len(ACT_PAIRS) + ACT_PAIRS.index(j) + 1
            return s["evD"], t * len(DVE_PAIRS) + DVE_PAIRS.index(j) + 1

        def after(eng, which, value):
            if not (isinstance(value, int) and value <= 0):
                eng.wait_ge(which, value)

        def col(a, j):
            return a[:, j:j + 1] if isinstance(j, int) else a[:, bass.ds(j, 1)]

        def back(t, j):
            return (t, j) if j >= 0 else (t - 1, j + 8)

        Tb = T[:, :, :].rearrange("p a b -> p (a b)").bitcast(BF16).rearrange("p (a b) -> p a b", a=2)
        Ti = T[:, :, :].rearrange("p a b -> p (a b)").bitcast(I16).rearrange("p (a b) -> p a b", a=2)
        QBb = QB[:, :].bitcast(BF16)
        Sb = S[:, :, :].rearrange("p a b -> p (a b)").bitcast(BF16).rearrange("p (a b) -> p a b", a=4)
        Rb = R[:, :, :, :].rearrange("p a b c -> p (a b c)").bitcast(BF16).rearrange("p (a b c) -> p a b c", a=4, b=2)

        @block.sync
        def _(eng):
            eng.dma_start(ctxT[:, :, :], ctxT_d.rearrange("(a p) k -> p a k", p=P)).then_inc(s["w_in1"], 16)
            eng.dma_start(wkv[:, :, :], wkv_d.rearrange("(a p) k -> p a k", p=P)).then_inc(s["w_in1"], 16)
            eng.dma_start(bkv[:, :], bkv_d.partition_broadcast(P)).then_inc(s["w_in1"], 16)
            for a in range(4):
                eng.dma_start(x[:, 4 * a:4 * a + 4, :],
                              x_d.rearrange("(t p) c -> p t c", p=P)[:, 4 * a:4 * a + 4, :]).then_inc(s["x_in"], 16)
            eng.dma_start(wq[:, :, :], wq_d.rearrange("(a p) k -> p a k", p=P)).then_inc(s["w_in2"], 16)
            eng.dma_start(bq[:, :], bq_d.partition_broadcast(P)).then_inc(s["w_in2"], 16)
            eng.dma_start(graw[:, 0:2], gx_d.partition_broadcast(P)).then_inc(s["w_in2"], 16)
            eng.dma_start(graw[:, 2:4], gf_d.partition_broadcast(P)).then_inc(s["w_in2"], 16)
            eng.dma_start(wp[:, :, :], wp_d.rearrange("(a p) k -> p a k", p=P)).then_inc(s["w_in2"], 16)
            eng.dma_start(bp[:, :], bp_d.partition_broadcast(P)).then_inc(s["w_in2"], 16)
            eng.dma_start(wf[0][:, :].rearrange("p (a k) -> p a k", a=CC),
                          wg_d.rearrange("(a p) k -> p a k", p=P)).then_inc(s["w_in3"], 16)
            eng.dma_start(wf[1][:, :].rearrange("p (a k) -> p a k", a=CC),
                          wu_d.rearrange("(a p) k -> p a k", p=P)).then_inc(s["w_in3"], 16)
            eng.dma_start(wf[2][:, :].rearrange("p (a k) -> p a k", a=FF // P),
                          wd_d.rearrange("(a p) k -> p a k", p=P)).then_inc(s["w_in3"], 16)
            eng.dma_start(ctxn[:, :, :], ctx_d.rearrange("(b m) c -> m b c", m=M)).then_inc(s["w_in3"], 16)
            eng.dma_start(wr[:, :, :], wr_d.rearrange("(a p) k -> p a k", p=P)).then_inc(s["w_in3"], 16)
            eng.dma_start(maskb[:, :], mask_d.partition_broadcast(P)).then_inc(s["w_in3"], 16)
            eng.wait_ge(s["x1_r"], NT)
            for e in range(E):
                eng.dma_start(WIN[:, e * CC * DI:(e + 1) * CC * DI].rearrange("p (a k) -> p a k", a=CC),
                              win_d[e].rearrange("(a p) k -> p a k", p=P)).then_inc(s["w_exp"], 16)
            eng.wait_ge(s["wpool"], 9)
            for e in range(E):
                eng.dma_start(WOUT[:, e * CC * DI:(e + 1) * CC * DI].rearrange("p (a k) -> p a k", a=DI // P),
                              wout_d[e].rearrange("(a p) k -> p a k", p=P)).then_inc(s["w_exp"], 16)
            for a in range(4):
                eng.wait_ge(s["c_x"], 4 * a + 4)
                eng.dma_start(out_d[512 * a:512 * a + 512, :].rearrange("(t p) c -> p t c", p=P),
                              x[:, 4 * a:4 * a + 4, :]).then_inc(s["out_init"], 16)
            eng.dma_start(out_d[TOKENS:TOKENS + P, :], x[:, 0, :]).then_inc(s["out_init"], 16)
            eng.sem_inc(s["rt_store"], 16)
            with eng.Fori(0, NT // 4) as g:
                eng.wait_ge(s["rt_xh"], g * 4 + 4)
                eng.dma_start(xn_d[bass.ds(g * 512, 512), :].rearrange("(t p) c -> p t c", p=P),
                              xr).then_inc(s["rt_store"], 16)
            eng.wait_ge(s["ex_add"], 16 * SLOTS)

        @block.gpsimd
        def _(eng):
            eng.memset(ident[:, :], 0.0).then_inc(s["iota_r"], 1)
            eng.memset(identb[:, :], 0.0).then_inc(s["iota_r"], 1)
            eng.wait_ge(s["iota_r"], 2)
            for m in (ident, identb):
                eng.affine_select(out=m[:, :], in_=m[:, :], compare_op=ALU.not_equal, fill=1.0, base=0,
                                  pattern=[[-1, P]], channel_multiplier=1).then_inc(s["consts"], 1)
            eng.iota(iota[:, :], [[1, P]], 0, 0, allow_small_or_imprecise_dtypes=True).then_inc(s["rt_const"], 1)
            eng.iota(token1[:, :], [[P, NT]], 1, 1, allow_small_or_imprecise_dtypes=True).then_inc(s["rt_const"], 1)
            eng.iota(padrow[:, :], [[0, 1]], TOKENS + 1, 1, allow_small_or_imprecise_dtypes=True).then_inc(s["rt_const"], 1)
            eng.memset(onesb[:, :], 1.0).then_inc(s["rt_const"], 1)
            eng.memset(trib[:, :], 1.0).then_inc(s["rt_const"], 1)
            eng.memset(lower[:, :, :], 1.0).then_inc(s["rt_const"], 1)
            eng.memset(picks[:, NT, :], 0.0).then_inc(s["rt_const"], 1)
            eng.memset(zeros[:, :], 0.0).then_inc(s["rt_const"], 1)
            eng.wait_ge(s["rt_const"], 8)
            eng.affine_select(out=trib[:, :], in_=trib[:, :], compare_op=ALU.is_gt, fill=0.0, base=0,
                              pattern=[[1, P]], channel_multiplier=-1).then_inc(s["rt_const"], 1)
            eng.affine_select(out=lower[:, :, :], in_=lower[:, :, :], compare_op=ALU.is_gt, fill=0.0, base=0,
                              pattern=[[1, E], [-1, E]], channel_multiplier=0).then_inc(s["rt_const"], 1)
            eng.wait_ge(s["vred"], 2)
            eng.partition_all_reduce(vmaxb[:, :], vmax[:, :], P, ReduceOp.max).then_inc(s["vall"], 1)
            eng.wait_ge(s["wabs_r"], 3)
            eng.partition_all_reduce(wabs_all[:, :], wabs[:, :], P, ReduceOp.add).then_inc(s["wall"], 1)

            def apart(which, value):
                eng.wait_ge(which, value)
                eng.sem_inc(s["apart"], 1)

            def q_prep(u):
                v3 = lambda a: a[:, :].rearrange("p (h d) -> p h d", h=H)
                slots = QC[:, :, :].rearrange("p h (s d) -> p h s d", s=SPLIT)
                n = [0]

                def step(ins):
                    n[0] += 1
                    ins.then_inc(s["qprep"], 1)
                    apart(s["qprep"], 9 * u + n[0])
                if not (isinstance(u, int) and u == 0):
                    eng.wait_ge(s["qB_r"], u)
                eng.wait_ge(s["qi_r"], u + 1)
                step(eng.tensor_tensor(v3(qy), v3(q), qinv[:, :].unsqueeze(2).to_broadcast([P, H, HD]), ALU.mult))
                step(eng.tensor_scalar(qy[:, :], qy[:, :], 1.0, MAGIC, ALU.mult, ALU.add))
                step(eng.tensor_scalar(qy[:, :], qy[:, :], -MAGIC, 1.0, ALU.add, ALU.mult))
                step(eng.tensor_tensor(v3(qy), v3(qy), qscale[:, :].unsqueeze(2).to_broadcast([P, H, HD]), ALU.mult))
                step(eng.tensor_scalar(slots[:, :, 0:3, :], v3(qy).unsqueeze(2).to_broadcast([P, H, 3, HD]), 1.0, 0.0, ALU.mult, ALU.add))
                step(eng.tensor_tensor(v3(qr), v3(qy), slots[:, :, 0, :], ALU.subtract))
                step(eng.tensor_scalar(slots[:, :, 3:6, :], v3(qr).unsqueeze(2).to_broadcast([P, H, 3, HD]), 1.0, 0.0, ALU.mult, ALU.add))
                step(eng.tensor_tensor(v3(qy), v3(qr), slots[:, :, 3, :], ALU.subtract))
                step(eng.tensor_scalar(slots[:, :, 6:8, :], v3(qy).unsqueeze(2).to_broadcast([P, H, 2, HD]), 1.0, 0.0, ALU.mult, ALU.add))

            def add_bias(w):
                eng.wait_ge(s["xh_r"], w + 1)
                eng.tensor_tensor(x[:, w, :], x[:, w, :], gbp[:, :], ALU.add).then_inc(s["xb_r"], 1)

            q_prep(0)
            eng.wait_ge(s["gbp_r"], 1)
            with eng.Fori(0, NT - 1) as t:
                add_bias(t)
                q_prep(t + 1)
            add_bias(NT - 1)
            eng.wait_ge(s["wsc"], 3)
            for i in range(3):
                eng.tensor_scalar(wf[i][:, :], wf[i][:, :], winv[:, i:i + 1], MAGIC, ALU.mult, ALU.add).then_inc(s["wpool"], 1)
                eng.wait_ge(s["wpool"], 3 * i + 1)
                eng.tensor_scalar(wf[i][:, :], wf[i][:, :], -MAGIC, 1.0, ALU.add, ALU.mult).then_inc(s["wpool"], 1)
                eng.wait_ge(s["wpool"], 3 * i + 2)
                eng.tensor_scalar(wi[i][:, :], wf[i][:, :], 1.0, -1.0, ALU.min, ALU.max).then_inc(s["wpool"], 1)

            def round_h(t):
                apart(s["f_hf"], t + 1)
                eng.tensor_scalar(hq[:, :], hid[:, :], hf[:, 0:1], MAGIC, ALU.mult, ALU.add).then_inc(s["f_hq"], 1)
                if not (isinstance(t, int) and t == 0):
                    apart(s["f_hiT"], t)
                apart(s["f_hq"], 2 * t + 1)
                eng.tensor_scalar(hi[:, :], hq[:, :], -MAGIC, 1.0, ALU.add, ALU.mult).then_inc(s["f_hq"], 1)

            def rx(u):
                apart(s["f_inv"], u + 1)
                eng.tensor_scalar(xq[:, :], xh[:, :], finv[:, 0:1], MAGIC, ALU.mult, ALU.add).then_inc(s["f_rq"], 1)
                if not (isinstance(u, int) and u == 0):
                    apart(s["f_xiT"], u)
                apart(s["f_rq"], 2 * u + 1)
                eng.tensor_scalar(xi[:, :], xq[:, :], -MAGIC, 1.0, ALU.add, ALU.mult).then_inc(s["f_rq"], 1)

            rx(0)
            rx(1)
            round_h(0)
            with eng.Fori(1, NT - 1) as t:
                rx(t + 1)
                round_h(t)
            round_h(NT - 1)

            def gather(j, b=None):
                b = j % 2 if b is None else b
                if not (isinstance(j, int) and j < 2):
                    eng.wait_ge(s["ex_turn"], j - 1)
                apart(s["ex_from"], j + 1)
                eng.indirect_dma_start(xg[:, b, :], None, xn_d[:, :],
                                       bass.IndirectOffsetOnAxis(ap=rows_in[:, b:b + 1], axis=0)).then_inc(s[f"ex_in{b}"], 16)

            def scatter(j, b):
                if not (isinstance(j, int) and j < 1):
                    eng.wait_ge(s["ex_add"], j * 16)
                apart(s["ex_yo"], 2 * j + 2)
                eng.indirect_dma_start(out_d[:, :], bass.IndirectOffsetOnAxis(ap=rows_out[:, b:b + 1], axis=0),
                                       yo[:, b, :], None, compute_op=ALU.add).then_inc(s["ex_add"], 16)

            eng.wait_ge(s["rt_store"], 16 * (NT // 4) + 16)
            gather(0)
            gather(1)
            gather(2)
            eng.wait_ge(s["out_init"], 80)
            for j in range(3):
                gather(j + 3)
                scatter(j, j % 2)
            with eng.Fori(0, (SLOTS - 7) // 2) as u:
                for i in range(2):
                    gather(u * 2 + (i + 6), i)
                    scatter(u * 2 + (i + 3), 1 - i)
            gather(SLOTS - 1)
            for j in range(SLOTS - 4, SLOTS):
                scatter(j, j % 2)

        @block.scalar
        def _(eng):
            eng.wait_ge(s["w_in3"], 96)
            eng.wait_ge(s["w_in2"], 96)
            eng.activation(gates[:, :], graw[:, :], ACT.Tanh).then_inc(s["gate_r"], 1)
            for i in range(3):
                eng.activation(KC[:, i, :, :].rearrange("p h d -> p (h d)"), wf[i][:, :], ACT.Abs,
                               accum_out=wabs[:, i:i + 1]).then_inc(s["wabs_r"], 1)

            def ln_sqrt(n):
                eng.wait_ge(s["lns"], 3 * n + 1)
                eng.activation(lnt[:, 1, :], lnt[:, 0, :], ACT.Sqrt).then_inc(s["lna"], 1)

            def normalise(out, t):
                return eng.activation(out, x[:, t, :], ACT.Identity, bias=nbias[:, t:t + 1] if isinstance(t, int) else nbias[:, bass.ds(t, 1)],
                                      scale=rstd[:, t:t + 1] if isinstance(t, int) else rstd[:, bass.ds(t, 1)])

            ln_sqrt(0)
            for i in range(8):
                if i % 2:
                    eng.wait_ge(s["kct"], i + 1)
                    eng.activation(KT[:, 8 * (i % 2):8 * (i % 2) + 8, P * (i // 2):P * (i // 2) + P],
                                   Tb[:, i % 2, :].rearrange("p (a b) -> p a b", a=8), ACT.Copy).then_inc(s["kev"], 1)

            def q_norm(u):
                if isinstance(u, int) and u == 0:
                    eng.wait_ge(s["rstd_r"], 2)
                else:
                    eng.wait_ge(s["xhT_r"], u)
                normalise(xh[:, :], u).then_inc(s["xh_r"], 1)

            def q_xT(u):
                eng.wait_ge(s["xhT_r"], u + 1)
                eng.activation(xT[:, :], QB[:, 0:C], ACT.Copy).then_inc(s["xT_r"], 1)

            def body(t, main, prev, nxt):
                first = not prev
                if nxt:
                    q_norm(t + 1)
                for h in range(16):
                    if main:
                        eng.wait_ge(s["nb_r"], t * 16 + (h + 1))
                        if h % 2 == 0 and not (first and h < 8):
                            eng.wait_ge(s["tr_r"], t * 8 + (h // 2 - 3))
                        if h % 8 == 0 and prev:
                            eng.wait_ge(s["rs_r"], t * 2 + (h // 8 - 1))
                        eng.activation(R[:, (h // 2) % 4, h % 2, :], S[:, h % 4, :], ACT.Exp,
                                       bias=ebias[:, h:h + 1], scale=-1.0, accum_out=esum[:, h:h + 1]).then_inc(s["exp_r"], 1)
                    if h == 1 and nxt:
                        q_xT(t + 1)
                    if h % 2 == 0:
                        tt, j = back(t, h // 2 - 1)
                        if j in ACT_PAIRS and (h >= 2 or prev) and (main or h < 2):
                            eng.wait_ge(s["tr_r"], tt * 8 + (j + 1))
                            if not (first and j < 4):
                                eng.wait_ge(s["pv_r"], tt * 8 + (j - 3))
                            eng.activation(PT[:, j % 4, :], Ti[:, j % 2, :], ACT.Copy).then_inc(s["evA"], 1)
                    if h == 6 and prev:
                        eng.wait_ge(s["aoT_r"], t)
                        eng.activation(aoT[:, :], QB[:, 0:C], ACT.Copy).then_inc(s["aoTe_r"], 1)

            q_norm(0)
            q_xT(0)
            body(0, True, False, True)
            with eng.Fori(1, NT - 1) as t:
                body(t, True, True, True)
            body(NT - 1, True, True, False)
            body(NT, False, True, False)

            ln_sqrt(1)

            def f_stage1(u):
                if isinstance(u, int) and u == 0:
                    eng.wait_ge(s["rstd_r"], 4)
                else:
                    eng.wait_ge(s["f_rq"], 2 * u)
                normalise(xh[:, :], u).then_inc(s["f_xh"], 1)

            def f_xiT(u):
                eng.wait_ge(s["f_xiT"], u + 1)
                eng.activation(xiT[:, :], Tb[:, 0, 0:C], ACT.Copy).then_inc(s["f_xiTe"], 1)

            def f_sig(t):
                for k in range(2):
                    eng.wait_ge(s["f_gu"], 2 * t + (k + 1))
                    eng.wait_ge(s["f_fg"], 2 * t + 1)
                    if not (isinstance(t, int) and t == 0):
                        eng.wait_ge(s["f_h"], 2 * t + (k - 1))
                    eng.activation(sig[:, k, :], S[:, 2 * k, :], ACT.Sigmoid, scale=fg[:, 0:1]).then_inc(s["f_sig"], 1)

            def f_hiT(t):
                eng.wait_ge(s["f_hiT"], t + 1)
                eng.activation(hiT[:, :], Tb[:, 1, :], ACT.Copy).then_inc(s["f_hiTe"], 1)

            f_stage1(0)
            f_xiT(0)
            f_stage1(1)
            f_sig(0)
            f_xiT(1)
            f_hiT(0)
            with eng.Fori(1, NT - 1) as t:
                f_stage1(t + 1)
                f_sig(t)
                f_xiT(t + 1)
                f_hiT(t)
            f_sig(NT - 1)
            f_hiT(NT - 1)

            ln_sqrt(2)
            eng.wait_ge(s["rstd_r"], 6)
            with eng.Fori(0, BATCH) as b:
                for i in range(2):
                    eng.activation(xh2[:, i, :], x[:, b * 2 + i, :], ACT.Identity, bias=nbias[:, bass.ds(b * 2 + i, 1)],
                                   scale=rstd[:, bass.ds(b * 2 + i, 1)]).then_inc(s["c_xh"], 1)
                for i in range(2):
                    eng.wait_ge(s["c_xhT"], b * 2 + (i + 1))
                    eng.activation(xT2[:, i, :], S[:, i, 0:C], ACT.Copy).then_inc(s["c_xT"], 1)
                for i in range(2):
                    eng.wait_ge(s["c_mx"], b * 2 + (i + 1))
                    eng.activation(pe_[:, i, :], sm[:, i, :], ACT.Exp, bias=smax[:, i:i + 1],
                                   accum_out=ssum[:, i:i + 1]).then_inc(s["c_ex"], 1)
                for i in range(2):
                    eng.wait_ge(s["c_pT"], b * 2 + (i + 1))
                    eng.activation(pT[:, i, :], T[0:M, i, 0:P], ACT.Copy).then_inc(s["c_pTe"], 1)
                for i in range(2):
                    eng.wait_ge(s["c_x"], b * 2 + (i + 1))

            ln_sqrt(3)
            eng.wait_ge(s["rstd_r"], 8)
            with eng.Fori(0, NT // 4) as g:
                eng.wait_ge(s["rt_store"], g * 16 + 16)
                for i in range(4):
                    eng.activation(xr[:, i, :], x[:, g * 4 + i, :], ACT.Identity, bias=nbias[:, bass.ds(g * 4 + i, 1)],
                                   scale=rstd[:, bass.ds(g * 4 + i, 1)]).then_inc(s["rt_xh"], 1)
                for i in range(4):
                    eng.wait_ge(s["rt_T"], g * 4 + (i + 1))
                    eng.activation(xrT[:, i, :], S[:, i, 0:C], ACT.Copy).then_inc(s["rt_xT"], 1)
                eng.wait_ge(s["rt_lg"], g * 4 + 4)
            eng.wait_ge(s["rt_gap"], 1)
            eng.activation(gw[:, 1, :], gw[:, 0, :], ACT.Exp).then_inc(s["rt_exp"], 1)

            def turned_x(j, b):
                eng.wait_ge(s["ex_turn"], j + 1)
                after(eng, s["ex_h"], j - 1)
                eng.activation(xgT[:, b, :], T[:, b, 0:C], ACT.Copy).then_inc(s["ex_xT"], 1)

            def silu(j, b):
                eng.wait_ge(s["ex_h"], j + 1)
                after(eng, s["ex_hT"], j - 1)
                eng.activation(hact[:, b, :], S[:, b, :], ACT.Silu).then_inc(s["ex_act"], 1)

            turned_x(0, 0)
            for j in range(2):
                silu(j, j % 2)
                turned_x(j + 1, (j + 1) % 2)
            with eng.Fori(0, (SLOTS - 3) // 2) as u:
                for i in range(2):
                    silu(u * 2 + (i + 2), i)
                    turned_x(u * 2 + (i + 3), 1 - i)
            silu(SLOTS - 1, 0)

        @block.vector
        def _(eng):
            def layer_norm_scales(n):
                for t in range(NT):
                    last = eng.bn_aggr(mv[:, t, :], st[:, t, :])
                    last.then_inc(s["aggr"], 1)
                eng.wait_ge(s["aggr"], NT * (n + 1))
                eng.tensor_scalar(lnt[:, 0, :], mv[:, :, 1], LN_EPS, None, ALU.add).then_inc(s["lns"], 1)
                eng.wait_ge(s["lna"], n + 1)
                eng.reciprocal(lnt[:, 2, :], lnt[:, 1, :]).then_inc(s["lns"], 1)
                eng.wait_ge(s["lns"], 3 * n + 2)
                eng.tensor_tensor(lnt[:, 3, :], lnt[:, 2, :], lnt[:, 2, :], ALU.mult).then_inc(s["lns"], 1)
                eng.wait_ge(s["lns"], 3 * n + 3)
                eng.tensor_tensor(lnt[:, 1, :], lnt[:, 3, :], lnt[:, 0, :], ALU.mult).then_inc(s["rstd_r2"], 1)
                eng.wait_ge(s["rstd_r2"], 2 * n + 1)
                eng.tensor_scalar(lnt[:, 3, :], lnt[:, 1, :], -0.5, 1.5, ALU.mult, ALU.add).then_inc(s["rstd_r2"], 1)
                eng.wait_ge(s["rstd_r2"], 2 * n + 2)
                eng.tensor_tensor(rstd[:, :], lnt[:, 2, :], lnt[:, 3, :], ALU.mult).then_inc(s["rstd_r"], 1)
                eng.wait_ge(s["rstd_r"], 2 * n + 1)
                eng.scalar_tensor_tensor(out=nbias[:, :], in0=mv[:, :, 0], scalar=-1.0, in1=rstd[:, :], op0=ALU.mult, op1=ALU.mult).then_inc(s["rstd_r"], 1)

            n = [0]

            def link(ins):
                n[0] += 1
                ins.then_inc(s["kdv"], 1)
                eng.wait_ge(s["kdv"], n[0])

            eng.wait_ge(s["w_in1"], 48)
            for kt in range(KB):
                eng.wait_ge(s["kvp"], kt + 1)
                eng.tensor_tensor(kv[:, kt, :], S[:, kt, :], bkv[:, :], ALU.add).then_inc(s["kvb"], 1)
            eng.wait_ge(s["kvb"], KB)
            link(eng.tensor_reduce(vmax[:, :], kv[:, :, C:].rearrange("p k c -> p c k"), AX.X, ALU.max, apply_absolute_value=True))
            eng.sem_inc(s["vred"], 2)
            k4 = kv[:, :, 0:C].rearrange("p k (h d) -> p k h d", h=H)
            t4 = ktmp[:, :, :].rearrange("p k (h d) -> p k h d", h=H)
            b4 = lambda a: a[:, :].rearrange("p (k h) -> p k h", k=KB).unsqueeze(3).to_broadcast([P, KB, H, HD])
            flat = ktmp[:, :, :].rearrange("p k c -> p (k c)")
            link(eng.tensor_reduce(kamax[:, :].rearrange("p (k h) -> p k h", k=KB), k4, AX.X, ALU.max, apply_absolute_value=True))
            link(eng.tensor_scalar(kscale[:, :], kamax[:, :], 1.0 / 127.0, Q_EPS, ALU.mult, ALU.max))
            link(eng.reciprocal(kinv[:, :], kscale[:, :]))
            link(eng.tensor_tensor(t4, k4, b4(kinv), ALU.mult))
            link(eng.tensor_scalar(flat, flat, MAGIC, -MAGIC, ALU.add, ALU.add))
            link(eng.tensor_scalar(kscale[:, :], kscale[:, :], -1.0, None, ALU.mult))
            link(eng.tensor_tensor(t4, t4, b4(kscale), ALU.mult))
            eng.wait_ge(s["wall"], 1)
            parts = KC[:, :, :, :].rearrange("p k h (s d) -> p (k h) s d", s=SPLIT)
            tf = ktmp[:, :, :].rearrange("p k (h d) -> p (k h) d", h=H)
            kf = kv[:, :, 0:C].rearrange("p k (h d) -> p k h d", h=H)
            for part in range(3):
                slots = [i for i in range(SPLIT) if i % 3 == part]
                for i in slots:
                    link(eng.tensor_copy(parts[:, :, i, :], tf))
                if part < 2:
                    link(eng.tensor_tensor(tf, tf, parts[:, :, part, :], ALU.subtract))
            eng.sem_inc(s["kct_in"], 1)
            eng.wait_ge(s["vall"], 1)
            link(eng.tensor_scalar(vscale[:, :], vmaxb[:, :], 1.0 / 127.0, Q_EPS, ALU.mult, ALU.max))
            eng.sem_inc(s["vq"], 1)
            link(eng.reciprocal(vinv[:, :], vscale[:, :]))
            link(eng.tensor_tensor(ktmp[:, :, :], kv[:, :, C:], vinv[:, :].unsqueeze(1).to_broadcast([P, KB, C]), ALU.mult))
            link(eng.tensor_scalar(V[:, :, :].rearrange("p k c -> p (k c)"), flat, MAGIC, -MAGIC, ALU.add, ALU.add))
            eng.sem_inc(s["vq"], 1)
            link(eng.tensor_scalar(wscale[:, :], wabs_all[:, :], 1.0 / (C * FF), F_EPS, ALU.mult, ALU.add))
            eng.reciprocal(winv[:, :], wscale[:, :]).then_inc(s["wsc"], 1)
            eng.wait_ge(s["gate_r"], 1)
            eng.tensor_scalar(wdg[:, :], wscale[:, 2:3], gates[:, 2:3], 1.0 / 127.0, ALU.mult, ALU.mult).then_inc(s["wsc"], 1)
            eng.tensor_scalar(gbp[:, :], bp[:, :], gates[:, 0:1], None, ALU.mult).then_inc(s["gbp_r"], 1)
            eng.tensor_scalar(bq[:, :], bq[:, :], 0.25, None, ALU.mult).then_inc(s["wsc"], 1)
            link(eng.tensor_scalar(madd[:, :], maskb[:, :], -1.0, NEG, ALU.add, ALU.mult))
            link(eng.tensor_reduce(valid[:, :], maskb[:, :].rearrange("p (b m) -> p b m", b=BATCH), AX.X, ALU.max))
            eng.tensor_scalar(gvalid[:, :], valid[:, :], gates[:, 1:2], None, ALU.mult).then_inc(s["c_mask"], 1)
            for a in range(CC):
                eng.wait_ge(s["svT"], 1)
                eng.tensor_scalar(wps[:, a, :], wp[:, a, :], PV[:, a * P:a * P + 1], None, ALU.mult).then_inc(s["wps_r"], 1)
            for t in range(NT):
                if t % 4 == 0:
                    eng.wait_ge(s["x_in"], 64)
                eng.bn_stats(st[:, t, :], x[:, t, :]).then_inc(s["st0"], 1)
            eng.wait_ge(s["st0"], NT)
            layer_norm_scales(0)
            for i in range(0, 8, 2):
                eng.wait_ge(s["kct"], i + 1)
                eng.tensor_copy(KT[:, 0:8, P * (i // 2):P * (i // 2) + P],
                                Tb[:, 0, :].rearrange("p (a b) -> p a b", a=8)).then_inc(s["kevD"], 1)

            def q_scale(u):
                if not (isinstance(u, int) and u == 0):
                    eng.wait_ge(s["qprep"], 9 * u)
                eng.wait_ge(s["qp_r"], u + 1)
                eng.scalar_tensor_tensor(out=q[:, :], in0=QB[:, 0:C], scalar=0.25, in1=bq[:, :], op0=ALU.mult, op1=ALU.add).then_inc(s["q_r"], 1)
                eng.wait_ge(s["q_r"], u + 1)
                eng.tensor_reduce(qamax[:, :], q[:, :].rearrange("p (h d) -> p h d", h=H), AX.X, ALU.max, apply_absolute_value=True).then_inc(s["qa_r"], 1)
                eng.wait_ge(s["qa_r"], u + 1)
                eng.tensor_scalar(qscale[:, :], qamax[:, :], 1.0 / 127.0, Q_EPS, ALU.mult, ALU.max).then_inc(s["qsc_r"], 1)
                eng.wait_ge(s["qsc_r"], u + 1)
                eng.reciprocal(qinv[:, :], qscale[:, :]).then_inc(s["qi_r"], 1)

            def q_half(u, half):
                r, d = (("qA_r", "qtA_r"), ("qB_r", "qtB_r"))[half]
                eng.wait_ge(s[r], u + 1)
                eng.tensor_copy(QT[:, 8 * half:8 * half + 8, :],
                                QBb.rearrange("p (a b) -> p a b", a=8)).then_inc(s[d], 1)

            def body(t, main, prev, nxt):
                first = not prev
                for h in range(16):
                    if main:
                        eng.wait_ge(s["score_r"], t * 16 + (h + 1))
                        if prev:
                            eng.wait_ge(s["exp_r"], t * 16 + (h - 15))
                        eng.tensor_scalar(junk[:, h % 4, :], S[:, h % 4, :], LN255, None, ALU.add, ALU.min,
                                          accum_out=ebias[:, h:h + 1]).then_inc(s["nb_r"], 1)
                    if h % 2:
                        tt, j = back(t, h // 2 - 2)
                        if j in DVE_PAIRS and (h >= 5 or prev) and (main or h < 5):
                            eng.wait_ge(s["tr_r"], tt * 8 + (j + 1))
                            if not (first and j < 4):
                                eng.wait_ge(s["pv_r"], tt * 8 + (j - 3))
                            eng.tensor_copy(PT[:, j % 4, :], Ti[:, j % 2, :]).then_inc(s["evD"], 1)
                    if h == 2 and main:
                        q_half(t, 1)
                    if h == 1 and prev:
                        eng.wait_ge(s["exp_r"], t * 16)
                        eng.reciprocal(rsum[:, 8:16], esum[:, 8:16]).then_inc(s["rs_r"], 1)
                    if h == 6 and nxt:
                        q_scale(t + 1)
                    if h == 7 and prev:
                        eng.wait_ge(s["pv_r"], t * 8)
                        eng.wait_ge(s["rs_r"], t * 2)
                        if not (isinstance(t, int) and t == 1):
                            eng.wait_ge(s["aoT_r"], t - 1) if isinstance(t, int) else None
                        eng.tensor_tensor(ao[:, :].rearrange("p (h d) -> p h d", h=H), PV[:, 0:C].rearrange("p (h d) -> p h d", h=H),
                                          rsum[:, :].unsqueeze(2).to_broadcast([P, H, HD]), ALU.mult).then_inc(s["ao_r"], 1)
                    if h == 12 and prev:
                        eng.wait_ge(s["op_r"], t)
                        eng.wait_ge(s["xb_r"], t)
                        w = t - 1
                        eng.scalar_tensor_tensor(out=x[:, w, :], in0=QB[:, 0:C], scalar=gates[:, 0:1], in1=x[:, w, :],
                                                 op0=ALU.mult, op1=ALU.add).then_inc(s["x1_r"], 1)
                        eng.wait_ge(s["x1_r"], t)
                        eng.bn_stats(st[:, w, :], x[:, w, :]).then_inc(s["bs_r"], 1)
                    if h == 13 and main:
                        eng.wait_ge(s["exp_r"], t * 16 + 8)
                        if prev:
                            eng.wait_ge(s["ao_r"], t)
                        eng.reciprocal(rsum[:, 0:8], esum[:, 0:8]).then_inc(s["rs_r"], 1)
                    if h == 15 and nxt:
                        q_half(t + 1, 0)

            q_scale(0)
            q_half(0, 0)
            body(0, True, False, True)
            with eng.Fori(1, NT - 1) as t:
                body(t, True, True, True)
            body(NT - 1, True, True, False)
            body(NT, False, True, False)

            eng.wait_ge(s["bs_r"], NT)
            layer_norm_scales(1)

            def f_scale(u):
                eng.wait_ge(s["f_xh"], u + 1)
                eng.tensor_reduce(fmax[:, :], xh[:, :], AX.X, ALU.max, apply_absolute_value=True).then_inc(s["f_max"], 1)
                eng.wait_ge(s["f_max"], u + 1)
                eng.tensor_scalar(fs[:, :], fmax[:, :], F_EPS, 1.0 / 127.0, ALU.max, ALU.mult).then_inc(s["f_s"], 1)
                eng.wait_ge(s["f_s"], u + 1)
                eng.reciprocal(finv[:, :], fs[:, :]).then_inc(s["f_inv"], 1)

            def f_scales2(u):
                if not (isinstance(u, int) and u == 0):
                    eng.wait_ge(s["f_sig"], 2 * u)
                    eng.wait_ge(s["f_hs"], 3 * u)
                eng.tensor_scalar(fg[:, 0:1], fs[:, :], wscale[:, 0:1], None, ALU.mult).then_inc(s["f_fg"], 1)
                eng.tensor_scalar(fu[:, 0:1], fs[:, :], wscale[:, 1:2], None, ALU.mult).then_inc(s["f_fg"], 1)
                eng.wait_ge(s["f_fg"], 2 * u + 2)

            def f_hidden(t):
                if not (isinstance(t, int) and t == 0):
                    eng.wait_ge(s["f_hq"], 2 * t)
                for k in range(2):
                    eng.wait_ge(s["f_sig"], 2 * t + (k + 1))
                    eng.tensor_tensor(hid[:, 512 * k:512 * k + 512], S[:, 2 * k + 1, :], sig[:, k, :], ALU.mult).then_inc(s["f_h"], 1)
                eng.wait_ge(s["f_h"], 2 * t + 2)
                eng.tensor_reduce(hmax[:, :], hid[:, :], AX.X, ALU.max, apply_absolute_value=True).then_inc(s["f_hm"], 1)
                eng.wait_ge(s["f_hm"], t + 1)
                eng.tensor_scalar(hs[:, :], hmax[:, :], fu[:, 0:1], F_EPS, ALU.mult, ALU.max).then_inc(s["f_hs"], 1)
                eng.wait_ge(s["f_hs"], 3 * t + 1)
                eng.reciprocal(hinv[:, :], hs[:, :]).then_inc(s["f_hs"], 1)
                eng.wait_ge(s["f_hs"], 3 * t + 2)
                eng.tensor_scalar(hf[:, :], hinv[:, :], fu[:, 0:1], 127.0, ALU.mult, ALU.mult).then_inc(s["f_hf"], 1)
                eng.tensor_scalar(ho[:, :], hs[:, :], wdg[:, 0:1], None, ALU.mult).then_inc(s["f_hs"], 1)

            def f_out(t):
                eng.wait_ge(s["f_dn"], t + 1)
                eng.wait_ge(s["f_hs"], 3 * t + 3)
                eng.scalar_tensor_tensor(out=x[:, t, :], in0=PV[:, 0:C], scalar=ho[:, 0:1], in1=x[:, t, :],
                                         op0=ALU.mult, op1=ALU.add).then_inc(s["f_x"], 1)
                eng.wait_ge(s["f_x"], t + 1)
                eng.bn_stats(st[:, t, :], x[:, t, :]).then_inc(s["f_bs"], 1)

            f_scale(0)
            f_scales2(0)
            f_scale(1)
            f_hidden(0)
            f_scales2(1)
            with eng.Fori(1, NT - 1) as t:
                f_scale(t + 1)
                f_out(t - 1)
                f_hidden(t)
                f_scales2(t + 1)
            f_out(NT - 2)
            f_hidden(NT - 1)
            f_out(NT - 1)

            eng.wait_ge(s["f_bs"], NT)
            layer_norm_scales(2)
            eng.wait_ge(s["c_mask"], 1)
            with eng.Fori(0, BATCH) as b:
                for i in range(2):
                    eng.wait_ge(s["c_sc"], b * 2 + (i + 1))
                    eng.scalar_tensor_tensor(out=sm[:, i, :], in0=S[:, 2 + i, 0:M], scalar=1.0 / 16.0,
                                             in1=madd[:, bass.ds(b * M, M)], op0=ALU.mult, op1=ALU.add).then_inc(s["c_sm"], 1)
                for i in range(2):
                    eng.wait_ge(s["c_sm"], b * 2 + (i + 1))
                    eng.tensor_reduce(smax[:, i:i + 1], sm[:, i, :], AX.X, ALU.max, negate=True).then_inc(s["c_mx"], 1)
                for i in range(2):
                    eng.wait_ge(s["c_ex"], b * 2 + (i + 1))
                    eng.reciprocal(srec[:, i:i + 1], ssum[:, i:i + 1]).then_inc(s["c_rc"], 1)
                for i in range(2):
                    eng.wait_ge(s["c_rc"], b * 2 + (i + 1))
                    eng.tensor_scalar(sfac[:, i:i + 1], srec[:, i:i + 1], gvalid[:, bass.ds(b, 1)], None, ALU.mult).then_inc(s["c_f"], 1)
                for i in range(2):
                    eng.wait_ge(s["c_rd"], b * 2 + (i + 1))
                    eng.wait_ge(s["c_f"], b * 2 + (i + 1))
                    eng.scalar_tensor_tensor(out=x[:, b * 2 + i, :], in0=(PV, QB)[i][:, 0:C], scalar=sfac[:, i:i + 1],
                                             in1=x[:, b * 2 + i, :], op0=ALU.mult, op1=ALU.add).then_inc(s["c_x"], 1)
                for i in range(2):
                    eng.wait_ge(s["c_x"], b * 2 + (i + 1))
                    eng.bn_stats(st[:, b * 2 + i, :], x[:, b * 2 + i, :]).then_inc(s["c_bs"], 1)

            eng.wait_ge(s["c_bs"], NT)
            layer_norm_scales(3)
            eng.sem_inc(s["rt_lgs"], 1)
            with eng.Fori(0, NT // 4) as g:
                eng.wait_ge(s["rt_lg"], g * 4 + 4)
                eng.tensor_copy(lg[:, :, :], PV[:, 0:4 * E].rearrange("p (i e) -> p i e", i=4)).then_inc(s["rt_lgs"], 1)
                for i in range(4):
                    if i == 0:
                        eng.wait_ge(s["rt_lgs"], g + 2)
                        eng.sem_inc(s["apart_d"], 1)
                    eng.max(top[:, i, :], lg[:, i, :]).then_inc(s["rt_top"], 1)
                for i in range(4):
                    eng.wait_ge(s["rt_top"], g * 4 + (i + 1))
                    eng.sem_inc(s["apart_d"], 1)
                    eng.max_index(topi[:, i, :], top[:, i, :], lg[:, i, :]).then_inc(s["rt_topi"], 1)
                eng.tensor_copy(topv[:, bass.ds(g * 4, 4), :], top[:, :, 0:TOPK]).then_inc(s["rt_sel"], 1)
                eng.wait_ge(s["rt_topi"], g * 4 + 4)
                eng.tensor_copy(topx[:, bass.ds(g * 4, 4), :], topi[:, :, 0:TOPK]).then_inc(s["rt_sel"], 1)
                eng.wait_ge(s["rt_sel"], g * 2 + 2)
            n = [0]

            def step(ins):
                n[0] += 1
                ins.then_inc(s["rt"], 1)
                eng.wait_ge(s["rt"], n[0])

            eng.tensor_tensor(gw[:, 0, :], topv[:, :, 1], topv[:, :, 0], ALU.subtract).then_inc(s["rt_gap"], 1)
            eng.wait_ge(s["rt_const"], 10)
            step(eng.tensor_tensor(pick[:, :, :, :], iota[:, 0:E].unsqueeze(1).unsqueeze(1).to_broadcast([P, TOPK, NT, E]),
                                   topx[:, :, :].rearrange("p t k -> p k t").unsqueeze(3).to_broadcast([P, TOPK, NT, E]), ALU.is_equal))
            eng.tensor_tensor(picks[:, 0:NT, :], pick[:, 0, :, :], pick[:, 1, :, :], ALU.add).then_inc(s["rt_picks"], 1)
            eng.wait_ge(s["rt_exp"], 1)
            step(eng.tensor_scalar(gw[:, 0, :], gw[:, 1, :], 1.0, None, ALU.add))
            step(eng.reciprocal(gw[:, 2, :], gw[:, 0, :]))
            step(eng.tensor_scalar(gk[:, 0, :], gw[:, 2, :], gates[:, 3:4], None, ALU.mult))
            step(eng.tensor_tensor(gk[:, 1, :], gk[:, 0, :], gw[:, 1, :], ALU.mult))
            eng.wait_ge(s["rt_order"], 1)
            pos = PV[:, 0:NT * E].rearrange("p (t e) -> p t e", t=NT)
            step(eng.tensor_scalar(cnt[:, :], PV[:, NT * E:(NT + 1) * E], (P - 1) / 2.0, 1.0 / P, ALU.add, ALU.mult))
            step(eng.tensor_scalar(tiles_of[:, :], cnt[:, :], MAGIC, -MAGIC, ALU.add, ALU.add))
            step(eng.tensor_tensor(lowprod[:, :, :], lower[:, :, :], tiles_of[:, :].unsqueeze(1).to_broadcast([P, E, E]), ALU.mult))
            step(eng.tensor_reduce(base[:, :], lowprod[:, :, :], AX.X, ALU.add))
            step(eng.tensor_tensor(upto[:, :], base[:, :], tiles_of[:, :], ALU.add))
            step(eng.tensor_scalar(order[:, :, :], pos, -(P - 1) / 2.0, 1.0 / P, ALU.add, ALU.mult))
            step(eng.tensor_scalar(block_[:, :, :], order[:, :, :], MAGIC, -MAGIC, ALU.add, ALU.add))
            step(eng.scalar_tensor_tensor(out=row_[:, :, :], in0=block_[:, :, :], scalar=-float(P), in1=pos, op0=ALU.mult, op1=ALU.add))
            step(eng.tensor_tensor(block_[:, :, :], block_[:, :, :], base[:, :].unsqueeze(1).to_broadcast([P, NT, E]), ALU.add))
            for value, chosen in ((row_, tok_row), (block_, tok_tile)):
                step(eng.tensor_tensor(picked[:, :, :, :], pick[:, :, :, :], value[:, :, :].unsqueeze(1).to_broadcast([P, TOPK, NT, E]), ALU.mult))
                step(eng.tensor_reduce(chosen[:, :], picked[:, :, :, :].rearrange("p k t e -> p (k t) e"), AX.X, ALU.add))
            step(eng.tensor_tensor(ended[:, :, :], iota[:, 0:SLOTS].unsqueeze(2).to_broadcast([P, SLOTS, E]),
                                   upto[:, :].unsqueeze(1).to_broadcast([P, SLOTS, E]), ALU.is_ge))
            step(eng.tensor_reduce(tile_e[:, :], ended[:, :, :], AX.X, ALU.add))
            step(eng.tensor_scalar(tile_off[:, :], tile_e[:, :], E - 1.0, float(CC * DI), ALU.min, ALU.mult))
            with eng.Fori(0, NT // 2) as u:
                for i in range(4):
                    k, c = i % 2, u * 2 + i // 2
                    eng.wait_ge(s["rt_mm"], u * 4 + (i + 1))
                    eng.tensor_scalar(hitr[:, i, :], iota[:, :], tok_row[:, bass.ds(c + k * NT, 1)], None, ALU.is_equal).then_inc(s["rt_hit"], 1)
                    eng.tensor_scalar(hitt[:, i, 0, :], iota[:, 0:SLOTS], tok_tile[:, bass.ds(c + k * NT, 1)], token1[:, bass.ds(c, 1)],
                                      ALU.is_equal, ALU.mult).then_inc(s["rt_hit"], 1)
                    eng.tensor_scalar(hitt[:, i, 1, :], iota[:, 0:SLOTS], tok_tile[:, bass.ds(c + k * NT, 1)], gk[:, k, bass.ds(c, 1)],
                                      ALU.is_equal, ALU.mult).then_inc(s["rt_hit"], 1)
            eng.wait_ge(s["rt_mm"], TOPK * NT + 5)
            step(eng.tensor_copy(slot[:, :, :], QB[:, 0:2 * SLOTS].rearrange("p (a j) -> p a j", a=2)))
            eng.tensor_scalar(slot_in[:, :], slot[:, 0, :], -1.0, 0.0, ALU.add, ALU.max).then_inc(s["rt_slots"], 1)
            step(eng.tensor_scalar(empty[:, :], slot[:, 0, :], 0.5, padrow[:, 0:1], ALU.is_lt, ALU.mult))
            step(eng.tensor_scalar(slot[:, 0, :], slot[:, 0, :], -1.0, None, ALU.add))
            eng.tensor_tensor(slot_out[:, :], slot[:, 0, :], empty[:, :], ALU.add).then_inc(s["rt_slots"], 1)
            eng.sem_inc(s["rt_slots"], 1)

            def number(j, b, h):
                after(eng, s[f"ex_in{b}"], h * 16)
                eng.tensor_copy(rows_in[:, b:b + 1], col(slot_in, j)).then_inc(s["ex_from"], 1)

            def turned_h(j, b):
                eng.wait_ge(s["ex_hT"], j + 1)
                after(eng, s["ex_y"], j - 1)
                eng.tensor_copy(hactT[:, b, :], S[:, 2 + b, :]).then_inc(s["ex_hTe"], 1)

            def weigh(j, b):
                eng.wait_ge(s["ex_y"], j + 1)
                after(eng, s["ex_add"], (j - 1) * 16)
                eng.tensor_scalar(yo[:, b, :], (PV, QB)[b][:, 0:C], slot[:, 1, j:j + 1] if isinstance(j, int) else slot[:, 1, bass.ds(j, 1)],
                                  None, ALU.mult).then_inc(s["ex_yo"], 1)
                eng.tensor_copy(rows_out[:, b:b + 1], col(slot_out, j)).then_inc(s["ex_yo"], 1)

            eng.wait_ge(s["rt_slots"], 3)
            number(0, 0, 0)
            number(1, 1, 0)
            number(2, 0, 1)
            turned_h(0, 0)
            for j in (1, 2):
                number(j + 2, j % 2, (j + 2) // 2)
                weigh(j - 1, (j - 1) % 2)
                turned_h(j, j % 2)
            with eng.Fori(0, (SLOTS - 5) // 2) as u:
                for i in range(2):
                    number(u * 2 + (i + 5), 1 - i, u + (i + 5) // 2)
                    weigh(u * 2 + (i + 2), i)
                    turned_h(u * 2 + (i + 3), 1 - i)
            for j in (SLOTS - 2, SLOTS - 1):
                weigh(j - 1, (j - 1) % 2)
                turned_h(j, j % 2)
            weigh(SLOTS - 1, 0)

        @block.tensor
        def _(eng):
            eng.wait_ge(s["w_in1"], 48)
            for kt in range(KB):
                for a in range(CC):
                    mm = eng.matmul(S[:, kt, :], ctxT[:, a, kt * P:kt * P + P], wkv[:, a, :], start=a == 0, stop=a == CC - 1)
                mm.then_inc(s["kvp"], 1)
            eng.wait_ge(s["consts"], 2)
            eng.wait_ge(s["vq"], 1)
            for a in range(CC):
                mm = eng.transpose(PV[:, a * P:a * P + P], vscale[:, a * P:a * P + P], ident[:, :])
            mm.then_inc(s["svT"], 1)
            eng.wait_ge(s["kct_in"], 1)
            for i in range(8):
                kt, half = i // 2, i % 2
                if i >= 2:
                    eng.wait_ge(s["kev" if half else "kevD"], i // 2)
                for k in range(8):
                    mm = eng.transpose(Tb[:, half, k * P:k * P + P], KC[:, kt, 8 * half + k, :], identb[:, :])
                mm.then_inc(s["kct"], 1)

            def q_xhT(u):
                eng.wait_ge(s["xh_r"], u + 1)
                for a in range(CC):
                    mm = eng.transpose(QB[:, a * P:a * P + P], xh[:, a * P:a * P + P], ident[:, :])
                mm.then_inc(s["xhT_r"], 1)

            def q_proj(u):
                eng.wait_ge(s["xT_r"], u + 1)
                for a in range(CC):
                    mm = eng.matmul(QB[:, 0:C], xT[:, a * P:a * P + P], wq[:, a, :], start=a == 0, stop=a == CC - 1)
                mm.then_inc(s["qp_r"], 1)

            def q_turn(u, half):
                for k in range(8):
                    mm = eng.transpose(QBb[:, k * P:k * P + P], QC[:, 8 * half + k, :], identb[:, :])
                mm.then_inc(s[("qA_r", "qB_r")[half]], 1)

            def body(t, main, prev, nxt):
                first = not prev
                for h in range(16):
                    if main:
                        if h == 0:
                            eng.wait_ge(s["qtA_r"], t + 1)
                        if h == 8:
                            eng.wait_ge(s["qtB_r"], t + 1)
                        if not (first and h < 4):
                            eng.wait_ge(s["exp_r"], t * 16 + (h - 3))
                        eng.matmul(S[:, h % 4, :], QT[:, h, :], KT[:, h, :], start=True, stop=True).then_inc(s["score_r"], 1)
                    if h % 2:
                        tt, j = back(t, h // 2 - 2)
                        if (h >= 5 or prev) and (main or h < 5):
                            eng.wait_ge(s["exp_r"], tt * 16 + (2 * j + 2))
                            if not (first and j < 2):
                                eng.wait_ge(*ev_sem(*back(tt, j - 2)))
                            for k in range(2 * KB):
                                mm = eng.transpose(Tb[:, j % 2, k * P:k * P + P], Rb[:, j % 4, k // KB, (k % KB) * P:(k % KB) * P + P], identb[:, :])
                            mm.then_inc(s["tr_r"], 1)
                        tt, j = back(t, h // 2 - 3)
                        if (h >= 7 or prev) and (main or h < 7):
                            eng.wait_ge(*ev_sem(tt, j))
                            if j == 0 and prev:
                                eng.wait_ge(s["ao_r"], tt)
                            for k in range(2 * KB):
                                hh = 2 * j + k // KB
                                mm = eng.matmul(PV[:, hh * HD:hh * HD + HD], PT[:, j % 4, k * P:k * P + P],
                                                V[:, k % KB, hh * HD:hh * HD + HD], start=k % KB == 0, stop=k % KB == KB - 1)
                            mm.then_inc(s["pv_r"], 1)
                    if h == 1 and main:
                        eng.wait_ge(s["qtA_r"], t + 1)
                        q_turn(t, 1)
                    if h == 3 and nxt:
                        eng.wait_ge(s["qtB_r"], t + 1)
                        q_xhT(t + 1)
                    if h == 6 and nxt:
                        q_proj(t + 1)
                    if h == 8 and prev:
                        eng.wait_ge(s["ao_r"], t)
                        if nxt:
                            eng.wait_ge(s["q_r"], t + 2)
                        for a in range(CC):
                            mm = eng.transpose(QB[:, a * P:a * P + P], ao[:, a * P:a * P + P], ident[:, :])
                        mm.then_inc(s["aoT_r"], 1)
                    if h == 11 and prev:
                        eng.wait_ge(s["aoTe_r"], t)
                        for a in range(CC):
                            mm = eng.matmul(QB[:, 0:C], aoT[:, a * P:a * P + P], wps[:, a, :], start=a == 0, stop=a == CC - 1)
                        mm.then_inc(s["op_r"], 1)
                    if h == 14 and nxt:
                        if prev:
                            eng.wait_ge(s["x1_r"], t)
                        eng.wait_ge(s["qprep"], 9 * (t + 1) + 9)
                        q_turn(t + 1, 0)

            eng.wait_ge(s["w_in2"], 96)
            q_xhT(0)
            q_proj(0)
            eng.wait_ge(s["qprep"], 9)
            q_turn(0, 0)
            eng.wait_ge(s["kevD"], 4)
            eng.wait_ge(s["kev"], 4)
            eng.wait_ge(s["vq"], 2)
            eng.wait_ge(s["wps_r"], CC)
            body(0, True, False, True)
            with eng.Fori(1, NT - 1) as t:
                body(t, True, True, True)
            body(NT - 1, True, True, False)
            body(NT, False, True, False)

            def f_turn_x(u):
                eng.wait_ge(s["f_rq"], 2 * u + 2)
                if not (isinstance(u, int) and u == 0):
                    eng.wait_ge(s["f_xiTe"], u)
                for a in range(CC):
                    mm = eng.transpose(Tb[:, 0, a * P:a * P + P], xi[:, a * P:a * P + P], identb[:, :])
                mm.then_inc(s["f_xiT"], 1)

            def f_gate_up(t):
                eng.wait_ge(s["f_xiTe"], t + 1)
                for k in range(2):
                    if not (isinstance(t, int) and t == 0):
                        eng.wait_ge(s["f_h"], 2 * t + (k - 1))
                    for w in range(2):
                        for a in range(CC):
                            mm = eng.matmul(S[:, 2 * k + w, :], xiT[:, a * P:a * P + P],
                                            wi[w][:, a * FF + 512 * k:a * FF + 512 * k + 512], start=a == 0, stop=a == CC - 1)
                    mm.then_inc(s["f_gu"], 1)

            def f_down(t):
                eng.wait_ge(s["f_hq"], 2 * t + 2)
                if not (isinstance(t, int) and t == 0):
                    eng.wait_ge(s["f_hiTe"], t)
                for k in range(8):
                    mm = eng.transpose(Tb[:, 1, k * P:k * P + P], hi[:, k * P:k * P + P], identb[:, :])
                mm.then_inc(s["f_hiT"], 1)

            def f_down2(t):
                eng.wait_ge(s["f_hiTe"], t + 1)
                if not (isinstance(t, int) and t == 0):
                    eng.wait_ge(s["f_x"], t)
                for k in range(8):
                    mm = eng.matmul(PV[:, 0:C], hiT[:, k * P:k * P + P], wi[2][:, k * C:k * C + C], start=k == 0, stop=k == 7)
                mm.then_inc(s["f_dn"], 1)

            eng.wait_ge(s["wpool"], 9)
            f_turn_x(0)
            f_gate_up(0)
            f_turn_x(1)
            f_down(0)
            with eng.Fori(1, NT - 1) as t:
                f_gate_up(t)
                f_down2(t - 1)
                f_turn_x(t + 1)
                f_down(t)
            f_gate_up(NT - 1)
            f_down2(NT - 2)
            f_down(NT - 1)
            f_down2(NT - 1)

            eng.wait_ge(s["f_x"], NT)
            with eng.Fori(0, BATCH) as b:
                for i in range(2):
                    eng.wait_ge(s["c_xh"], b * 2 + (i + 1))
                    for a in range(CC):
                        mm = eng.transpose(S[:, i, a * P:a * P + P], xh2[:, i, a * P:a * P + P], ident[:, :])
                    mm.then_inc(s["c_xhT"], 1)
                for i in range(2):
                    eng.wait_ge(s["c_xT"], b * 2 + (i + 1))
                    for a in range(CC):
                        mm = eng.matmul(S[:, 2 + i, 0:M], xT2[:, i, a * P:a * P + P], ctxT[:, a, bass.ds(b * M, M)],
                                        start=a == 0, stop=a == CC - 1)
                    mm.then_inc(s["c_sc"], 1)
                for i in range(2):
                    eng.wait_ge(s["consts"], 2)
                    eng.wait_ge(s["c_ex"], b * 2 + (i + 1))
                    eng.transpose(T[0:M, i, 0:P], pe_[:, i, :], ident[:, :]).then_inc(s["c_pT"], 1)
                for i in range(2):
                    eng.wait_ge(s["consts"], 2)
                    eng.wait_ge(s["c_pTe"], b * 2 + (i + 1))
                    eng.matmul((PV, QB)[i][:, 0:C], pT[:, i, :], ctxn[:, b, :], start=True, stop=True).then_inc(s["c_rd"], 1)

            with eng.Fori(0, NT // 4) as g:
                for i in range(4):
                    eng.wait_ge(s["rt_xh"], g * 4 + (i + 1))
                    for a in range(CC):
                        mm = eng.transpose(S[:, i, a * P:a * P + P], xr[:, i, a * P:a * P + P], ident[:, :])
                    mm.then_inc(s["rt_T"], 1)
                eng.wait_ge(s["rt_lgs"], g + 1)
                for i in range(4):
                    eng.wait_ge(s["rt_xT"], g * 4 + (i + 1))
                    for a in range(CC):
                        mm = eng.matmul(PV[:, i * E:i * E + E], xrT[:, i, a * P:a * P + P], wr[:, a, :], start=a == 0, stop=a == CC - 1)
                    mm.then_inc(s["rt_lg"], 1)
            eng.wait_ge(s["rt_picks"], 1)
            eng.matmul(PV[:, 0:(NT + 1) * E], trib[:, :], picks[:, :, :].rearrange("p t e -> p (t e)"), start=True, stop=False)
            for t in range(NT):
                mm = eng.matmul(PV[:, (t + 1) * E:(NT + 1) * E], onesb[:, :],
                                picks[:, t:t + 1, :].to_broadcast([P, NT - t, E]), start=False, stop=t == NT - 1)
            mm.then_inc(s["rt_order"], 1)
            eng.sem_inc(s["rt_mm"], 4)
            eng.matmul(QB[:, 0:2 * SLOTS], ident[:, :], zeros[:, :], start=True, stop=False)
            with eng.Fori(0, NT // 2) as u:
                for i in range(4):
                    eng.wait_ge(s["rt_hit"], u * 12 + (3 * i + 3))
                    eng.matmul(QB[:, 0:2 * SLOTS], hitr[:, i, :], hitt[:, i, :, :].rearrange("p a j -> p (a j)"),
                               start=False, stop=False).then_inc(s["rt_mm"], 1)
            eng.matmul(QB[:, 0:2 * SLOTS], ident[:, :], zeros[:, :], start=False, stop=True).then_inc(s["rt_mm"], 1)

            def turn_x(j, b, h):
                eng.wait_ge(s[f"ex_in{b}"], 16 * h + 16)
                after(eng, s["ex_xT"], j - 1)
                for a in range(CC):
                    mm = eng.transpose(T[:, b, a * P:a * P + P], xg[:, b, a * P:a * P + P], ident[:, :])
                mm.then_inc(s["ex_turn"], 1)

            def first(j, b, off):
                eng.wait_ge(s["ex_xT"], j + 1)
                after(eng, s["ex_act"], j - 1)
                for a in range(CC):
                    mm = eng.matmul(S[:, b, :], xgT[:, b, a * P:a * P + P], WIN[:, bass.ds(off + a * DI, DI)], start=a == 0, stop=a == CC - 1)
                mm.then_inc(s["ex_h"], 1)

            def turn_h(j, b):
                eng.wait_ge(s["ex_act"], j + 1)
                after(eng, s["ex_hTe"], j - 1)
                for a in range(DI // P):
                    mm = eng.transpose(S[:, 2 + b, a * P:a * P + P], hact[:, b, a * P:a * P + P], ident[:, :])
                mm.then_inc(s["ex_hT"], 1)

            def second(j, b, off):
                eng.wait_ge(s["ex_hTe"], j + 1)
                after(eng, s["ex_yo"], 2 * (j - 1))
                for a in range(DI // P):
                    mm = eng.matmul((PV, QB)[b][:, 0:C], hactT[:, b, a * P:a * P + P], WOUT[:, bass.ds(off + a * C, C)],
                                    start=a == 0, stop=a == DI // P - 1)
                mm.then_inc(s["ex_y"], 1)

            def weights_of(j):
                return eng.value_load(tile_off[0:1, j:j + 1] if isinstance(j, int) else tile_off[0:1, bass.ds(j, 1)],
                                      min_val=0, max_val=(E - 1) * CC * DI)

            eng.wait_ge(s["rt_slots"], 3)
            eng.wait_ge(s["w_exp"], 16 * 2 * E)
            turn_x(0, 0, 0)
            first(0, 0, weights_of(0))
            turn_x(1, 1, 0)
            turn_h(0, 0)
            for j in (1, 2):
                first(j, j % 2, weights_of(j))
                turn_x(j + 1, (j + 1) % 2, (j + 1) // 2)
                second(j - 1, (j - 1) % 2, weights_of(j - 1))
                turn_h(j, j % 2)
            with eng.Fori(0, (SLOTS - 5) // 2) as u:
                for i in range(2):
                    first(u * 2 + (i + 3), 1 - i, weights_of(u * 2 + (i + 3)))
                    turn_x(u * 2 + (i + 4), i, u + (i + 4) // 2)
                    second(u * 2 + (i + 2), i, weights_of(u * 2 + (i + 2)))
                    turn_h(u * 2 + (i + 3), 1 - i)
            for j in (SLOTS - 2, SLOTS - 1):
                first(j, j % 2, weights_of(j))
                if j + 1 < SLOTS:
                    turn_x(j + 1, (j + 1) % 2, (j + 1) // 2)
                second(j - 1, (j - 1) % 2, weights_of(j - 1))
                turn_h(j, j % 2)
            second(SLOTS - 1, 0, weights_of(SLOTS - 1))


def kernel(**inputs):
    import numpy as _np
    import concourse.bacc as _bacc
    from concourse import mybir as _mybir
    from concourse.bass_utils import run_bass_kernel_spmd as _run

    a = {k: _np.asarray(v) for k, v in inputs.items()}
    laid = {
        "x": a["x"].reshape(TOKENS, C),
        "ctx": a["ctx_2048"].reshape(KEYS, C),
        "ctxT": a["ctx_2048"].reshape(KEYS, C).T,
        "mask": a["mask_BxS2_bk0"].reshape(BATCH * M),
        "gx": a["g_xattn"], "gf": a["g_ffn"],
        "wq": a["L0_xattn_Wq"], "bq": a["L0_xattn_bq"], "wkv": a["L0_xattn_Wkv"], "bkv": a["L0_xattn_bkv"],
        "wp": a["L0_xattn_Wp"], "bp": a["L0_xattn_bp"],
        "wg": a["L0_ffn_w_gate"].T, "wu": a["L0_ffn_w_up"].T, "wd": a["L0_ffn_w_down"].T,
        "wr": a["L1_ffn_Wr"].T, "win": a["L1_ffn_Win"].transpose(0, 2, 1), "wout": a["L1_ffn_Wout"].transpose(0, 2, 1),
    }
    nc = _bacc.Bacc("TRN2", target_bir_lowering=False, num_devices=1)
    arrays, args = {}, []
    for name, v in laid.items():
        v = _np.ascontiguousarray(v)
        arrays[f"in_{name}_dram"] = v
        args.append(nc.dram_tensor(f"in_{name}_dram", v.shape, _mybir.dt.from_np(v.dtype), kind="ExternalInput").ap())
    args.append(nc.dram_tensor("out_dram", (TOKENS + P, C), F32, kind="ExternalOutput").ap())
    flamingo_kernel(nc, *args)
    r = _run(nc, [arrays], core_ids=[0])
    return r.results[0]["out_dram"][:TOKENS].reshape(8, 256, C)
```

```python
import concourse.bass as bass
from concourse import mybir

ReduceOp = bass.bass_isa.ReduceOp
from contextlib import ExitStack

F32 = mybir.dt.float32
BF16 = mybir.dt.bfloat16
I16 = mybir.dt.int16
U8 = mybir.dt.uint8
U32 = mybir.dt.uint32
I32 = mybir.dt.int32
ALU = mybir.AluOpType
ACT = mybir.ActivationFunctionType
AX = mybir.AxisListType

P = 128
TOKENS, C = 2048, 256
NT = TOKENS // P
CC = C // P
KEYS = 512
KB = KEYS // P
H, HD = 16, 16
BATCH, M = 8, 64
FF = 1024
E, DI = 8, 512
TOPK = 2
SLOTS = (TOPK * TOKENS + E * (P - 1)) // P
SPLIT = 8
MAGIC = 12582912.0
LN255 = 5.541263545158426
LN_EPS = 1e-5
Q_EPS = 1e-8
F_EPS = 1e-5
NEG = 1e30
ACT_PAIRS = (0, 2, 4, 6)
DVE_PAIRS = tuple(j for j in range(8) if j not in ACT_PAIRS)


def flamingo_kernel(nc, x_d, ctx_d, ctxT_d, mask_d, gx_d, gf_d, wq_d, bq_d, wkv_d, bkv_d, wp_d, bp_d,
                    wg_d, wu_d, wd_d, wr_d, win_d, wout_d, out_d):
    xn_d = nc.dram_tensor("normalised", (TOKENS, C), F32).ap()
    stack = ExitStack()
    with stack:
        def sb(name, shape, dt=F32):
            return stack.enter_context(nc.sbuf_tensor(name, shape, dt))

        def pb(name, shape, dt=F32):
            return stack.enter_context(nc.psum_tensor(name, shape, dt))

        def sem(name):
            return stack.enter_context(nc.semaphore(name))

        x = sb("x_tokens", [P, NT, C])
        ident = sb("ident", [P, P])
        identb = sb("identb", [P, P], BF16)
        gates = sb("gates", [P, 4])
        graw = sb("graw", [P, 4])
        ctxT = sb("ctxT", [P, CC, KEYS])
        ctxn = sb("ctxn", [M, BATCH, C])
        wq = sb("wq", [P, CC, C])
        wkv = sb("wkv", [P, CC, 2 * C])
        wp = sb("wp", [P, CC, C])
        wps = sb("wps", [P, CC, C])
        bq = sb("bq", [P, C])
        bkv = sb("bkv", [P, 2 * C])
        bp = sb("bp", [P, C])
        wr = sb("wr", [P, CC, E])
        big = sb("big", [P, E * (CC * DI + DI // P * C)])
        WIN, WOUT = big[:, 0:E * CC * DI], big[:, E * CC * DI:]
        KC = big[:, 0:4096].bitcast(BF16).rearrange("p (k h d) -> p k h d", k=KB, h=H)
        KT = big[:, 4096:8192].bitcast(BF16).rearrange("p (h k) -> p h k", h=H)
        wf = [big[:, 8192 + i * CC * FF:8192 + (i + 1) * CC * FF] for i in range(3)]
        R = big[:, 14336:16384].bitcast(I16).rearrange("p (a b c) -> p a b c", a=4, b=2)
        wi = [sb("wgi", [P, CC * FF], BF16), sb("wui", [P, CC * FF], BF16), sb("wdi", [P, CC * FF], BF16)]
        maskb = sb("maskb", [P, BATCH * M], U8)
        madd = sb("madd", [P, BATCH * M])
        valid = sb("valid", [P, BATCH])
        kv = sb("kv", [P, KB, 2 * C])
        ktmp = sb("ktmp", [P, KB, C])
        kamax = sb("kamax", [P, KB * H])
        kscale = sb("kscale", [P, KB * H])
        kinv = sb("kinv", [P, KB * H])
        vmax = sb("vmax", [P, C])
        vmaxb = sb("vmaxb", [P, C])
        vscale = sb("vscale", [P, C])
        vinv = sb("vinv", [P, C])
        V = sb("V", [P, KB, C], BF16)
        wabs = sb("wabs", [P, 3])
        wabs_all = sb("wabs_all", [P, 3])
        wscale = sb("wscale", [P, 3])
        winv = sb("winv", [P, 3])
        st = sb("st", [P, NT, 6])
        mv = sb("mv", [P, NT, 2])
        lnt = sb("lnt", [P, 4, NT])
        rstd = sb("rstd", [P, NT])
        nbias = sb("nbias", [P, NT])
        xh = sb("xh", [P, C])
        xT = sb("xT", [P, C])
        q = sb("q", [P, C])
        qy = sb("qy", [P, C])
        qr = sb("qr", [P, C])
        qamax = sb("qamax", [P, H])
        qscale = sb("qscale", [P, H])
        qinv = sb("qinv", [P, H])
        QC = sb("QC", [P, H, SPLIT * HD], BF16)
        QT = sb("QT", [P, H, P], BF16)
        junk = ktmp[:, :, :].rearrange("p k c -> p (k c)").bitcast(BF16).rearrange("p (a k) -> p a k", a=4)
        ebias = sb("ebias", [P, H])
        PT = sb("PT", [P, 4, 2 * KB * P], BF16)
        esum = sb("esum", [P, H])
        rsum = sb("rsum", [P, H])
        ao = sb("ao", [P, C])
        aoT = sb("aoT", [P, C])
        gbp = sb("gbp", [P, C])
        fmax = sb("fmax", [P, 1])
        fs = sb("fs", [P, 2])
        finv = sb("finv", [P, 1])
        fg = sb("fg", [P, 2])
        fu = sb("fu", [P, 2])
        xq = sb("xq", [P, C])
        xi = sb("xi", [P, C], BF16)
        xiT = sb("xiT", [P, C], BF16)
        sig_ = sb("sig", [P, FF])
        sig = sig_[:, :].rearrange("p (k f) -> p k f", k=2)
        hid_ = PT[:, :, :].rearrange("p a k -> p (a k)").bitcast(F32)
        hid = hid_.rearrange("p (b f) -> p b f", b=2)
        hmax = sb("hmax", [P, 1])
        hs = sb("hs", [P, 1])
        hinv = sb("hinv", [P, 1])
        hf = sb("hf", [P, 1])
        ho = sb("ho", [P, NT])
        wdg = sb("wdg", [P, 1])
        hq = sb("hq", [P, FF])
        hi = sb("hi", [P, FF], BF16)
        hiT = sb("hiT", [P, FF], BF16)
        xh2 = sb("xh2", [P, 2, C])
        xT2 = sb("xT2", [P, 2, C])
        sm = sb("sm", [P, 2, M])
        smax = sb("smax", [P, 2])
        pe_ = sb("pe_", [P, 2, M])
        ssum = sb("ssum", [P, 2])
        srec = sb("srec", [P, 2])
        sfac = sb("sfac", [P, 2])
        pT = sb("pT", [M, 2, P])
        gvalid = sb("gvalid", [P, BATCH])
        xr = [a[:, :].rearrange("p (i c) -> p i c", i=4) for a in (sig_, hq)]
        xrT = [hid[:, b, :].rearrange("p (i c) -> p i c", i=4) for b in range(2)]
        lg = sb("lg", [P, 4, E])
        top = sb("top", [P, 4, 8])
        topi = sb("topi", [P, 4, 8], U32)
        topv = sb("topv", [P, NT, TOPK])
        topx = sb("topx", [P, NT, TOPK])
        gw = sb("gw", [P, 3, NT])
        gk = sb("gk", [P, TOPK, NT])
        pick = sb("pick", [P, TOPK, NT, E])
        picks = sb("picks", [P, NT + 1, E], BF16)
        picked = sb("picked", [P, TOPK, NT, E])
        order = sb("order", [P, NT, E])
        block_ = sb("block", [P, NT, E])
        row_ = sb("row", [P, NT, E])
        tok_row = sb("tok_row", [P, TOPK * NT])
        tok_tile = sb("tok_tile", [P, TOPK * NT])
        cnt = sb("cnt", [P, E])
        tiles_of = sb("tiles_of", [P, E])
        lower = sb("lower", [P, E, E])
        lowprod = sb("lowprod", [P, E, E])
        base = sb("base", [P, E])
        upto = sb("upto", [P, E])
        ended = sb("ended", [P, SLOTS, E])
        tile_e = sb("tile_e", [P, SLOTS])
        tile_off = sb("tile_off", [P, SLOTS], I32)
        iota = sb("iota", [P, P])
        token1 = sb("token1", [P, NT])
        padrow = sb("padrow", [P, 1])
        trib = sb("trib", [P, P], BF16)
        onesb = sb("onesb", [P, P], BF16)
        hitr = sb("hitr", [P, 2, 4, P])
        NK = TOPK * NT
        xflat = x[:, :, :].rearrange("p t c -> p (t c)")
        hit = xflat[:, 0:NK * SLOTS].rearrange("p (m j) -> p m j", m=NK)
        hitt = xflat[:, NK * SLOTS:3 * NK * SLOTS].rearrange("p (m a j) -> p m a j", m=NK, a=2)
        zeros = sb("zeros", [P, 2 * SLOTS])
        slot = sb("slot", [P, 2, SLOTS])
        empty = sb("empty", [P, SLOTS])
        slot_in = sb("slot_in", [P, SLOTS], U32)
        slot_out = sb("slot_out", [P, SLOTS], U32)
        rows_in = sb("rows_in", [P, 2], U32)
        rows_out = sb("rows_out", [P, 2], U32)
        xg = sb("xg", [P, 2, C])
        xgT = sb("xgT", [P, 2, C])
        hact, hactT = kv[:, 0:2, :], kv[:, 2:4, :]
        yo = ktmp[:, 0:2, :]

        S = pb("S", [P, 4, 512])
        T = pb("T", [P, 2, 512])
        PV = pb("PV", [P, 512])
        QB = pb("QB", [P, 512])

        names = """x_in w_in1 w_in2 w_in3 consts iota_r gate_r
            kvp kvb kdv kct kev vred vall vq svT wps_r wabs_r wall wsc wpool wpool_done
            st0 aggr lns lna rstd_r
            xh_r xhT_r xT_r qp_r q_r qa_r qsc_r qi_r qprep qA_r qtA_r qB_r qtB_r
            score_r nm_r nb_r exp_r tr_r evD evA pv_r rs_r ao_r aoT_r aoTe_r op_r xb_r x1_r bs_r gbp_r
            f_xh f_max f_s f_inv f_fg f_rq f_xiT f_xiTe f_gu f_sig f_h f_hm f_hs f_hi f_hf f_hq f_hiT f_hiTe f_dn f_x f_bs
            c_xh c_xhT c_xT c_sc c_sm c_mx c_ex c_rc c_f c_pT c_pTe c_rd c_x c_bs c_mask
            rt_xh rt_T rt_xT rt_lg rt_lgs rt_top rt_topi rt_sel rt rt_gap rt_exp rt_const rt_picks rt_order
            rt_store0 rt_store1 rt_hit rt_hitt rt_mm rt_slots
            w_exp ex_in0 ex_in1 ex_from ex_turn ex_xT ex_h ex_act ex_hT ex_hTe ex_y ex_yo ex_add out_init
            apart apart_d apart_p rstd_r2 kct_in""".split()
        s = {n: sem("s_" + n) for n in names}
        block = stack.enter_context(nc.Block())

        def ev_sem(t, j):
            if j in ACT_PAIRS:
                return s["evA"], t * len(ACT_PAIRS) + ACT_PAIRS.index(j) + 1
            return s["evD"], t * len(DVE_PAIRS) + DVE_PAIRS.index(j) + 1

        def after(eng, which, value):
            if not (isinstance(value, int) and value <= 0):
                eng.wait_ge(which, value)

        def in_range(t):
            return not isinstance(t, int) or 0 <= t < NT

        def in_batches(b):
            return not isinstance(b, int) or 0 <= b < BATCH

        def col(a, j):
            return a[:, j:j + 1] if isinstance(j, int) else a[:, bass.ds(j, 1)]

        def back(t, j):
            return (t, j) if j >= 0 else (t - 1, j + 8)

        Tb = T[:, :, :].rearrange("p a b -> p (a b)").bitcast(BF16).rearrange("p (a b) -> p a b", a=2)
        Ti = T[:, :, :].rearrange("p a b -> p (a b)").bitcast(I16).rearrange("p (a b) -> p a b", a=2)
        QBb = QB[:, :].bitcast(BF16)
        Sb = S[:, :, :].rearrange("p a b -> p (a b)").bitcast(BF16).rearrange("p (a b) -> p a b", a=4)
        Rb = R[:, :, :, :].rearrange("p a b c -> p (a b c)").bitcast(BF16).rearrange("p (a b c) -> p a b c", a=4, b=2)

        @block.sync
        def _(eng):
            eng.dma_start(ctxT[:, :, :], ctxT_d.rearrange("(a p) k -> p a k", p=P)).then_inc(s["w_in1"], 16)
            eng.dma_start(wkv[:, :, :], wkv_d.rearrange("(a p) k -> p a k", p=P)).then_inc(s["w_in1"], 16)
            eng.dma_start(bkv[:, :], bkv_d.partition_broadcast(P)).then_inc(s["w_in1"], 16)
            for a in range(4):
                eng.dma_start(x[:, 4 * a:4 * a + 4, :],
                              x_d.rearrange("(t p) c -> p t c", p=P)[:, 4 * a:4 * a + 4, :]).then_inc(s["x_in"], 16)
            eng.dma_start(wq[:, :, :], wq_d.rearrange("(a p) k -> p a k", p=P)).then_inc(s["w_in2"], 16)
            eng.dma_start(bq[:, :], bq_d.partition_broadcast(P)).then_inc(s["w_in2"], 16)
            eng.dma_start(graw[:, 0:2], gx_d.partition_broadcast(P)).then_inc(s["w_in2"], 16)
            eng.dma_start(graw[:, 2:4], gf_d.partition_broadcast(P)).then_inc(s["w_in2"], 16)
            eng.dma_start(wp[:, :, :], wp_d.rearrange("(a p) k -> p a k", p=P)).then_inc(s["w_in2"], 16)
            eng.dma_start(bp[:, :], bp_d.partition_broadcast(P)).then_inc(s["w_in2"], 16)
            eng.dma_start(wf[0][:, :].rearrange("p (a k) -> p a k", a=CC),
                          wg_d.rearrange("(a p) k -> p a k", p=P)).then_inc(s["w_in3"], 16)
            eng.dma_start(wf[1][:, :].rearrange("p (a k) -> p a k", a=CC),
                          wu_d.rearrange("(a p) k -> p a k", p=P)).then_inc(s["w_in3"], 16)
            eng.dma_start(wf[2][:, :].rearrange("p (a k) -> p a k", a=FF // P),
                          wd_d.rearrange("(a p) k -> p a k", p=P)).then_inc(s["w_in3"], 16)
            eng.dma_start(ctxn[:, :, :], ctx_d.rearrange("(b m) c -> m b c", m=M)).then_inc(s["w_in3"], 16)
            eng.dma_start(wr[:, :, :], wr_d.rearrange("(a p) k -> p a k", p=P)).then_inc(s["w_in3"], 16)
            eng.dma_start(maskb[:, :], mask_d.partition_broadcast(P)).then_inc(s["w_in3"], 16)
            eng.wait_ge(s["x1_r"], NT)
            for e in range(E):
                eng.dma_start(WIN[:, e * CC * DI:(e + 1) * CC * DI].rearrange("p (a k) -> p a k", a=CC),
                              win_d[e].rearrange("(a p) k -> p a k", p=P)).then_inc(s["w_exp"], 16)
            eng.wait_ge(s["wpool"], 18)
            for e in range(E):
                eng.dma_start(WOUT[:, e * CC * DI:(e + 1) * CC * DI].rearrange("p (a k) -> p a k", a=DI // P),
                              wout_d[e].rearrange("(a p) k -> p a k", p=P)).then_inc(s["w_exp"], 16)
            for a in range(4):
                eng.wait_ge(s["c_x"], 4 * a + 4)
                eng.dma_start(out_d[512 * a:512 * a + 512, :].rearrange("(t p) c -> p t c", p=P),
                              x[:, 4 * a:4 * a + 4, :]).then_inc(s["out_init"], 16)
            eng.dma_start(out_d[TOKENS:TOKENS + P, :], x[:, 0, :]).then_inc(s["out_init"], 16)
            for b in range(2):
                eng.sem_inc(s[f"rt_store{b}"], 16)
            with eng.Fori(0, NT // 8) as u:
                for b in range(2):
                    eng.wait_ge(s["rt_xh"], u * 8 + (4 * b + 4))
                    eng.dma_start(xn_d[bass.ds(u * 1024 + b * 512, 512), :].rearrange("(t p) c -> p t c", p=P),
                                  xr[b]).then_inc(s[f"rt_store{b}"], 16)
            eng.wait_ge(s["ex_add"], 16 * SLOTS)

        @block.gpsimd
        def _(eng):
            eng.memset(ident[:, :], 0.0).then_inc(s["iota_r"], 1)
            eng.memset(identb[:, :], 0.0).then_inc(s["iota_r"], 1)
            eng.wait_ge(s["iota_r"], 2)
            for m in (ident, identb):
                eng.affine_select(out=m[:, :], in_=m[:, :], compare_op=ALU.not_equal, fill=1.0, base=0,
                                  pattern=[[-1, P]], channel_multiplier=1).then_inc(s["consts"], 1)
            eng.iota(iota[:, :], [[1, P]], 0, 0, allow_small_or_imprecise_dtypes=True).then_inc(s["rt_const"], 1)
            eng.iota(token1[:, :], [[P, NT]], 1, 1, allow_small_or_imprecise_dtypes=True).then_inc(s["rt_const"], 1)
            eng.iota(padrow[:, :], [[0, 1]], TOKENS + 1, 1, allow_small_or_imprecise_dtypes=True).then_inc(s["rt_const"], 1)
            eng.memset(onesb[:, :], 1.0).then_inc(s["rt_const"], 1)
            eng.memset(trib[:, :], 1.0).then_inc(s["rt_const"], 1)
            eng.memset(lower[:, :, :], 1.0).then_inc(s["rt_const"], 1)
            eng.memset(picks[:, NT, :], 0.0).then_inc(s["rt_const"], 1)
            eng.memset(zeros[:, :], 0.0).then_inc(s["rt_const"], 1)
            eng.wait_ge(s["rt_const"], 8)
            eng.affine_select(out=trib[:, :], in_=trib[:, :], compare_op=ALU.is_gt, fill=0.0, base=0,
                              pattern=[[1, P]], channel_multiplier=-1).then_inc(s["rt_const"], 1)
            eng.affine_select(out=lower[:, :, :], in_=lower[:, :, :], compare_op=ALU.is_gt, fill=0.0, base=0,
                              pattern=[[1, E], [-1, E]], channel_multiplier=0).then_inc(s["rt_const"], 1)
            eng.wait_ge(s["vred"], 2)
            eng.partition_all_reduce(vmaxb[:, :], vmax[:, :], P, ReduceOp.max).then_inc(s["vall"], 1)
            def apart(which, value):
                eng.wait_ge(which, value)
                eng.sem_inc(s["apart"], 1)

            def q_prep(u):
                v3 = lambda a: a[:, :].rearrange("p (h d) -> p h d", h=H)
                slots = QC[:, :, :].rearrange("p h (s d) -> p h s d", s=SPLIT)
                n = [0]

                def step(ins):
                    n[0] += 1
                    ins.then_inc(s["qprep"], 1)
                    apart(s["qprep"], 9 * u + n[0])
                if not (isinstance(u, int) and u == 0):
                    eng.wait_ge(s["qB_r"], u)
                eng.wait_ge(s["qi_r"], u + 1)
                step(eng.tensor_tensor(v3(qy), v3(q), qinv[:, :].unsqueeze(2).to_broadcast([P, H, HD]), ALU.mult))
                step(eng.tensor_scalar(qy[:, :], qy[:, :], 1.0, MAGIC, ALU.mult, ALU.add))
                step(eng.tensor_scalar(qy[:, :], qy[:, :], -MAGIC, 1.0, ALU.add, ALU.mult))
                step(eng.tensor_tensor(v3(qy), v3(qy), qscale[:, :].unsqueeze(2).to_broadcast([P, H, HD]), ALU.mult))
                step(eng.tensor_scalar(slots[:, :, 0:3, :], v3(qy).unsqueeze(2).to_broadcast([P, H, 3, HD]), 1.0, 0.0, ALU.mult, ALU.add))
                step(eng.tensor_tensor(v3(qr), v3(qy), slots[:, :, 0, :], ALU.subtract))
                step(eng.tensor_scalar(slots[:, :, 3:6, :], v3(qr).unsqueeze(2).to_broadcast([P, H, 3, HD]), 1.0, 0.0, ALU.mult, ALU.add))
                step(eng.tensor_tensor(v3(qy), v3(qr), slots[:, :, 3, :], ALU.subtract))
                step(eng.tensor_scalar(slots[:, :, 6:8, :], v3(qy).unsqueeze(2).to_broadcast([P, H, 2, HD]), 1.0, 0.0, ALU.mult, ALU.add))

            def add_bias(w):
                eng.wait_ge(s["xh_r"], w + 1)
                eng.tensor_tensor(x[:, w, :], x[:, w, :], gbp[:, :], ALU.add).then_inc(s["xb_r"], 1)

            q_prep(0)
            eng.wait_ge(s["wabs_r"], 3)
            eng.partition_all_reduce(wabs_all[:, :], wabs[:, :], P, ReduceOp.add).then_inc(s["wall"], 1)
            eng.wait_ge(s["gbp_r"], 1)
            HALF = CC * FF // 2

            def ternary(i, half):
                w = wf[i][:, half * HALF:(half + 1) * HALF]
                n = 6 * i + 3 * half
                eng.tensor_scalar(w, w, winv[:, i:i + 1], MAGIC, ALU.mult, ALU.add).then_inc(s["wpool"], 1)
                eng.wait_ge(s["wpool"], n + 1)
                eng.tensor_scalar(w, w, -MAGIC, 1.0, ALU.add, ALU.mult).then_inc(s["wpool"], 1)
                eng.wait_ge(s["wpool"], n + 2)
                eng.tensor_scalar(wi[i][:, half * HALF:(half + 1) * HALF], w, 1.0, -1.0, ALU.min, ALU.max).then_inc(s["wpool"], 1)

            eng.wait_ge(s["wsc"], 2)
            for i in range(6):
                with eng.Fori(2 * i, 2 * i + 2) as t:
                    add_bias(t)
                    q_prep(t + 1)
                ternary(i // 2, i % 2)
            with eng.Fori(12, NT - 1) as t:
                add_bias(t)
                q_prep(t + 1)
            add_bias(NT - 1)

            def round_h(t, b):
                apart(s["f_hf"], t + 1)
                eng.tensor_scalar(hq[:, :], hid[:, b, :], hf[:, 0:1], MAGIC, ALU.mult, ALU.add).then_inc(s["f_hq"], 1)
                if not (isinstance(t, int) and t == 0):
                    apart(s["f_hiT"], t)
                apart(s["f_hq"], 2 * t + 1)
                eng.tensor_scalar(hi[:, :], hq[:, :], -MAGIC, 1.0, ALU.add, ALU.mult).then_inc(s["f_hq"], 1)

            def rx(u):
                apart(s["f_inv"], u + 1)
                eng.tensor_scalar(xq[:, :], xh[:, :], finv[:, 0:1], MAGIC, ALU.mult, ALU.add).then_inc(s["f_rq"], 1)
                if not (isinstance(u, int) and u == 0):
                    apart(s["f_xiT"], u)
                apart(s["f_rq"], 2 * u + 1)
                eng.tensor_scalar(xi[:, :], xq[:, :], -MAGIC, 1.0, ALU.add, ALU.mult).then_inc(s["f_rq"], 1)

            def f_step(t, b):
                if in_range(t - 1):
                    round_h(t - 1, 1 - b)
                if in_range(t + 2):
                    rx(t + 2)

            for t in range(-2, 4):
                f_step(t, t % 2)
            with eng.Fori(0, (NT - 6) // 2) as u:
                for b in range(2):
                    f_step(u * 2 + (b + 4), b)
            for t in range(NT - 2, NT + 3):
                f_step(t, t % 2)

            def gather(j, b=None):
                b = j % 2 if b is None else b
                if not (isinstance(j, int) and j < 2):
                    eng.wait_ge(s["ex_turn"], j - 1)
                apart(s["ex_from"], j + 1)
                eng.indirect_dma_start(xg[:, b, :], None, xn_d[:, :],
                                       bass.IndirectOffsetOnAxis(ap=rows_in[:, b:b + 1], axis=0)).then_inc(s[f"ex_in{b}"], 16)

            def scatter(j, b):
                if not (isinstance(j, int) and j < 1):
                    eng.wait_ge(s["ex_add"], j * 16)
                apart(s["ex_yo"], 2 * j + 2)
                eng.indirect_dma_start(out_d[:, :], bass.IndirectOffsetOnAxis(ap=rows_out[:, b:b + 1], axis=0),
                                       yo[:, b, :], None, compute_op=ALU.add).then_inc(s["ex_add"], 16)

            for b in range(2):
                eng.wait_ge(s[f"rt_store{b}"], 16 * (NT // 8) + 16)
            gather(0)
            gather(1)
            gather(2)
            eng.wait_ge(s["out_init"], 80)
            for j in range(3):
                gather(j + 3)
                scatter(j, j % 2)
            with eng.Fori(0, (SLOTS - 7) // 2) as u:
                for i in range(2):
                    gather(u * 2 + (i + 6), i)
                    scatter(u * 2 + (i + 3), 1 - i)
            gather(SLOTS - 1)
            for j in range(SLOTS - 4, SLOTS):
                scatter(j, j % 2)

        @block.scalar
        def _(eng):
            def ln_sqrt(n):
                eng.wait_ge(s["lns"], 3 * n + 1)
                eng.activation(lnt[:, 1, :], lnt[:, 0, :], ACT.Sqrt).then_inc(s["lna"], 1)

            def normalise(out, t):
                return eng.activation(out, x[:, t, :], ACT.Identity, bias=nbias[:, t:t + 1] if isinstance(t, int) else nbias[:, bass.ds(t, 1)],
                                      scale=rstd[:, t:t + 1] if isinstance(t, int) else rstd[:, bass.ds(t, 1)])

            def q_norm(u):
                if isinstance(u, int) and u == 0:
                    eng.wait_ge(s["rstd_r"], 2)
                else:
                    eng.wait_ge(s["xhT_r"], u)
                normalise(xh[:, :], u).then_inc(s["xh_r"], 1)

            def q_xT(u):
                eng.wait_ge(s["xhT_r"], u + 1)
                eng.activation(xT[:, :], QB[:, 0:C], ACT.Copy).then_inc(s["xT_r"], 1)

            def body(t, main, prev, nxt):
                first = not prev
                if nxt:
                    q_norm(t + 1)
                for h in range(16):
                    if main:
                        eng.wait_ge(s["nb_r"], t * 16 + (h + 1))
                        if h % 2 == 0 and not (first and h < 8):
                            eng.wait_ge(s["tr_r"], t * 8 + (h // 2 - 3))
                        if h % 8 == 0 and prev:
                            eng.wait_ge(s["rs_r"], t * 2 + (h // 8 - 1))
                        eng.activation(R[:, (h // 2) % 4, h % 2, :], S[:, h % 4, :], ACT.Exp,
                                       bias=ebias[:, h:h + 1], scale=-1.0, accum_out=esum[:, h:h + 1]).then_inc(s["exp_r"], 1)
                    if h == 1 and nxt:
                        q_xT(t + 1)
                    if h % 2 == 1:
                        tt, j = back(t, (h - 3) // 2)
                        if j in ACT_PAIRS and (h >= 3 or prev) and (main or h < 3):
                            eng.wait_ge(s["tr_r"], tt * 8 + (j + 1))
                            if not (first and j < 4):
                                eng.wait_ge(s["pv_r"], tt * 8 + (j - 3))
                            eng.activation(PT[:, j % 4, :], Ti[:, j % 2, :], ACT.Copy).then_inc(s["evA"], 1)
                    if h == 9 and prev:
                        eng.wait_ge(s["aoT_r"], t)
                        eng.activation(aoT[:, :], QB[:, 0:C], ACT.Copy).then_inc(s["aoTe_r"], 1)

            ln_sqrt(0)
            q_norm(0)
            q_xT(0)
            eng.wait_ge(s["w_in2"], 96)
            eng.activation(gates[:, :], graw[:, :], ACT.Tanh).then_inc(s["gate_r"], 1)
            eng.wait_ge(s["w_in3"], 96)
            for i in range(3):
                eng.activation(KT[:, 4 * i:4 * i + 4, :].rearrange("p h k -> p (h k)"), wf[i][:, :], ACT.Abs,
                               accum_out=wabs[:, i:i + 1]).then_inc(s["wabs_r"], 1)
            eng.wait_ge(s["wabs_r"], 3)
            for i in range(8):
                eng.wait_ge(s["kct"], i + 1)
                eng.activation(KT[:, 8 * (i % 2):8 * (i % 2) + 8, P * (i // 2):P * (i // 2) + P],
                               Tb[:, i % 2, :].rearrange("p (a b) -> p a b", a=8), ACT.Copy).then_inc(s["kev"], 1)
            body(0, True, False, True)
            with eng.Fori(1, NT - 1) as t:
                body(t, True, True, True)
            body(NT - 1, True, True, False)
            body(NT, False, True, False)

            ln_sqrt(1)

            def f_stage1(u):
                if isinstance(u, int) and u == 0:
                    eng.wait_ge(s["rstd_r"], 4)
                else:
                    eng.wait_ge(s["f_rq"], 2 * u)
                normalise(xh[:, :], u).then_inc(s["f_xh"], 1)

            def f_xiT(u):
                eng.wait_ge(s["f_xiT"], u + 1)
                eng.activation(xiT[:, :], Tb[:, 0, 0:C], ACT.Copy).then_inc(s["f_xiTe"], 1)

            def f_sig(t, b):
                for k in range(2):
                    eng.wait_ge(s["f_gu"], 2 * t + (k + 1))
                    if k == 0:
                        eng.wait_ge(s["f_fg"], 2 * t + 1)
                    if not (isinstance(t, int) and t == 0):
                        eng.wait_ge(s["f_h"], 2 * t + (k - 1))
                    eng.activation(sig[:, k, :], S[:, 2 * k, :], ACT.Sigmoid, scale=fg[:, b:b + 1]).then_inc(s["f_sig"], 1)

            def f_hiT(t):
                eng.wait_ge(s["f_hiT"], t + 1)
                eng.activation(hiT[:, :], Tb[:, 1, :], ACT.Copy).then_inc(s["f_hiTe"], 1)

            def f_step(t, b):
                if in_range(t - 2):
                    f_hiT(t - 2)
                if in_range(t):
                    f_sig(t, b)
                if in_range(t + 2):
                    f_stage1(t + 2)
                if in_range(t + 1):
                    f_xiT(t + 1)

            for t in range(-2, 4):
                f_step(t, t % 2)
            with eng.Fori(0, (NT - 6) // 2) as u:
                for b in range(2):
                    f_step(u * 2 + (b + 4), b)
            for t in range(NT - 2, NT + 3):
                f_step(t, t % 2)

            ln_sqrt(2)
            eng.wait_ge(s["rstd_r"], 6)

            def c_step(b):
                for i in range(2):
                    if in_batches(b + 1):
                        if not (isinstance(b, int) and b == -1):
                            eng.wait_ge(s["c_xhT"], b * 2 + (i + 1))
                        n = 2 * (b + 1) + i
                        eng.activation(xh2[:, i, :], x[:, n, :], ACT.Identity, bias=col(nbias, n), scale=col(rstd, n)).then_inc(s["c_xh"], 1)
                for i in range(2):
                    if in_batches(b - 1):
                        eng.wait_ge(s["c_pT"], b * 2 + (i - 1))
                        eng.activation(pT[:, i, :], T[0:M, i, 0:P], ACT.Copy).then_inc(s["c_pTe"], 1)
                for i in range(2):
                    if in_batches(b):
                        if not (isinstance(b, int) and b == 0):
                            eng.wait_ge(s["c_rc"], b * 2 + (i - 1))
                        eng.wait_ge(s["c_mx"], b * 2 + (i + 1))
                        eng.activation(pe_[:, i, :], sm[:, i, :], ACT.Exp, bias=smax[:, i:i + 1],
                                       accum_out=ssum[:, i:i + 1]).then_inc(s["c_ex"], 1)
                for i in range(2):
                    if in_batches(b + 1):
                        eng.wait_ge(s["c_xhT"], b * 2 + (i + 3))
                        eng.activation(xT2[:, i, :], S[:, i, 0:C], ACT.Copy).then_inc(s["c_xT"], 1)

            for b in (-1, 0, 1):
                c_step(b)
            with eng.Fori(2, BATCH - 1) as b:
                c_step(b)
            for b in (BATCH - 1, BATCH):
                c_step(b)

            ln_sqrt(3)
            eng.wait_ge(s["rstd_r"], 8)
            with eng.Fori(0, NT // 8) as u:
                for b in range(2):
                    eng.wait_ge(s[f"rt_store{b}"], u * 16 + 16)
                    for i in range(4):
                        n = u * 8 + (4 * b + i)
                        eng.activation(xr[b][:, i, :], x[:, n, :], ACT.Identity, bias=col(nbias, n), scale=col(rstd, n)).then_inc(s["rt_xh"], 1)
                    for i in range(4):
                        eng.wait_ge(s["rt_T"], u * 8 + (4 * b + i + 1))
                        if i == 0:
                            eng.wait_ge(s["rt_lg"], u * 8 + (4 * b + 1))
                        eng.activation(xrT[b][:, i, :], S[:, i, 0:C], ACT.Copy).then_inc(s["rt_xT"], 1)
            eng.wait_ge(s["rt_gap"], 1)
            eng.activation(gw[:, 1, :], gw[:, 0, :], ACT.Exp).then_inc(s["rt_exp"], 1)

            def turned_x(j, b):
                eng.wait_ge(s["ex_turn"], j + 1)
                after(eng, s["ex_h"], j - 1)
                eng.activation(xgT[:, b, :], T[:, b, 0:C], ACT.Copy).then_inc(s["ex_xT"], 1)

            def silu(j, b):
                eng.wait_ge(s["ex_h"], j + 1)
                after(eng, s["ex_hT"], j - 1)
                eng.activation(hact[:, b, :], S[:, b, :], ACT.Silu).then_inc(s["ex_act"], 1)

            turned_x(0, 0)
            for j in range(2):
                silu(j, j % 2)
                turned_x(j + 1, (j + 1) % 2)
            with eng.Fori(0, (SLOTS - 3) // 2) as u:
                for i in range(2):
                    silu(u * 2 + (i + 2), i)
                    turned_x(u * 2 + (i + 3), 1 - i)
            silu(SLOTS - 1, 0)

        @block.vector
        def _(eng):
            def layer_norm_scales(n):
                for t in range(NT):
                    last = eng.bn_aggr(mv[:, t, :], st[:, t, :])
                    last.then_inc(s["aggr"], 1)
                eng.wait_ge(s["aggr"], NT * (n + 1))
                eng.tensor_scalar(lnt[:, 0, :], mv[:, :, 1], LN_EPS, None, ALU.add).then_inc(s["lns"], 1)
                eng.wait_ge(s["lna"], n + 1)
                eng.reciprocal(lnt[:, 2, :], lnt[:, 1, :]).then_inc(s["lns"], 1)
                eng.wait_ge(s["lns"], 3 * n + 2)
                eng.tensor_tensor(lnt[:, 3, :], lnt[:, 2, :], lnt[:, 2, :], ALU.mult).then_inc(s["lns"], 1)
                eng.wait_ge(s["lns"], 3 * n + 3)
                eng.tensor_tensor(lnt[:, 1, :], lnt[:, 3, :], lnt[:, 0, :], ALU.mult).then_inc(s["rstd_r2"], 1)
                eng.wait_ge(s["rstd_r2"], 2 * n + 1)
                eng.tensor_scalar(lnt[:, 3, :], lnt[:, 1, :], -0.5, 1.5, ALU.mult, ALU.add).then_inc(s["rstd_r2"], 1)
                eng.wait_ge(s["rstd_r2"], 2 * n + 2)
                eng.tensor_tensor(rstd[:, :], lnt[:, 2, :], lnt[:, 3, :], ALU.mult).then_inc(s["rstd_r"], 1)
                eng.wait_ge(s["rstd_r"], 2 * n + 1)
                eng.scalar_tensor_tensor(out=nbias[:, :], in0=mv[:, :, 0], scalar=-1.0, in1=rstd[:, :], op0=ALU.mult, op1=ALU.mult).then_inc(s["rstd_r"], 1)

            n = [0]

            def link(ins):
                n[0] += 1
                ins.then_inc(s["kdv"], 1)
                eng.wait_ge(s["kdv"], n[0])

            eng.wait_ge(s["w_in1"], 48)
            for kt in range(KB):
                eng.wait_ge(s["kvp"], kt + 1)
                eng.tensor_tensor(kv[:, kt, :], S[:, kt, :], bkv[:, :], ALU.add).then_inc(s["kvb"], 1)
            eng.wait_ge(s["kvb"], KB)
            link(eng.tensor_reduce(vmax[:, :], kv[:, :, C:].rearrange("p k c -> p c k"), AX.X, ALU.max, apply_absolute_value=True))
            eng.sem_inc(s["vred"], 2)
            eng.wait_ge(s["x_in"], 64)
            for t in range(NT):
                eng.bn_stats(st[:, t, :], x[:, t, :]).then_inc(s["st0"], 1)
            eng.wait_ge(s["st0"], NT)
            layer_norm_scales(0)
            k4 = kv[:, :, 0:C].rearrange("p k (h d) -> p k h d", h=H)
            t4 = ktmp[:, :, :].rearrange("p k (h d) -> p k h d", h=H)
            b4 = lambda a: a[:, :].rearrange("p (k h) -> p k h", k=KB).unsqueeze(3).to_broadcast([P, KB, H, HD])
            flat = ktmp[:, :, :].rearrange("p k c -> p (k c)")
            link(eng.tensor_reduce(kamax[:, :].rearrange("p (k h) -> p k h", k=KB), k4, AX.X, ALU.max, apply_absolute_value=True))
            link(eng.tensor_scalar(kscale[:, :], kamax[:, :], 1.0 / 127.0, Q_EPS, ALU.mult, ALU.max))
            link(eng.reciprocal(kinv[:, :], kscale[:, :]))
            link(eng.tensor_tensor(t4, k4, b4(kinv), ALU.mult))
            link(eng.tensor_scalar(flat, flat, MAGIC, -MAGIC, ALU.add, ALU.add))
            link(eng.tensor_scalar(kscale[:, :], kscale[:, :], -1.0, None, ALU.mult))
            link(eng.tensor_tensor(t4, t4, b4(kscale), ALU.mult))
            eng.wait_ge(s["w_in2"], 96)
            link(eng.tensor_scalar(bq[:, :], bq[:, :], 0.25, None, ALU.mult))
            def q_scale(u):
                if not (isinstance(u, int) and u == 0):
                    eng.wait_ge(s["qprep"], 9 * u)
                eng.wait_ge(s["qp_r"], u + 1)
                eng.scalar_tensor_tensor(out=q[:, :], in0=QB[:, 0:C], scalar=0.25, in1=bq[:, :], op0=ALU.mult, op1=ALU.add).then_inc(s["q_r"], 1)
                eng.wait_ge(s["q_r"], u + 1)
                eng.tensor_reduce(qamax[:, :], q[:, :].rearrange("p (h d) -> p h d", h=H), AX.X, ALU.max, apply_absolute_value=True).then_inc(s["qa_r"], 1)
                eng.wait_ge(s["qa_r"], u + 1)
                eng.tensor_scalar(qscale[:, :], qamax[:, :], 1.0 / 127.0, Q_EPS, ALU.mult, ALU.max).then_inc(s["qsc_r"], 1)
                eng.wait_ge(s["qsc_r"], u + 1)
                eng.reciprocal(qinv[:, :], qscale[:, :]).then_inc(s["qi_r"], 1)

            q_scale(0)
            parts = KC[:, :, :, :].rearrange("p k h (s d) -> p (k h) s d", s=SPLIT)
            tf = ktmp[:, :, :].rearrange("p k (h d) -> p (k h) d", h=H)
            kf = kv[:, :, 0:C].rearrange("p k (h d) -> p k h d", h=H)
            for part in range(3):
                slots = [i for i in range(SPLIT) if i % 3 == part]
                for i in slots:
                    link(eng.tensor_copy(parts[:, :, i, :], tf))
                if part < 2:
                    link(eng.tensor_tensor(tf, tf, parts[:, :, part, :], ALU.subtract))
            eng.sem_inc(s["kct_in"], 1)
            eng.wait_ge(s["vall"], 1)
            link(eng.tensor_scalar(vscale[:, :], vmaxb[:, :], 1.0 / 127.0, Q_EPS, ALU.mult, ALU.max))
            eng.sem_inc(s["vq"], 1)
            link(eng.reciprocal(vinv[:, :], vscale[:, :]))
            link(eng.tensor_tensor(ktmp[:, :, :], kv[:, :, C:], vinv[:, :].unsqueeze(1).to_broadcast([P, KB, C]), ALU.mult))
            link(eng.tensor_scalar(V[:, :, :].rearrange("p k c -> p (k c)"), flat, MAGIC, -MAGIC, ALU.add, ALU.add))
            eng.sem_inc(s["vq"], 1)
            eng.wait_ge(s["wall"], 1)
            link(eng.tensor_scalar(wscale[:, :], wabs_all[:, :], 1.0 / (C * FF), F_EPS, ALU.mult, ALU.add))
            eng.reciprocal(winv[:, :], wscale[:, :]).then_inc(s["wsc"], 1)
            eng.wait_ge(s["gate_r"], 1)
            eng.tensor_scalar(wdg[:, :], wscale[:, 2:3], gates[:, 2:3], 1.0 / 127.0, ALU.mult, ALU.mult).then_inc(s["wsc"], 1)
            eng.tensor_scalar(gbp[:, :], bp[:, :], gates[:, 0:1], None, ALU.mult).then_inc(s["gbp_r"], 1)
            link(eng.tensor_scalar(madd[:, :], maskb[:, :], -1.0, NEG, ALU.add, ALU.mult))
            link(eng.tensor_reduce(valid[:, :], maskb[:, :].rearrange("p (b m) -> p b m", b=BATCH), AX.X, ALU.max))
            eng.tensor_scalar(gvalid[:, :], valid[:, :], gates[:, 1:2], None, ALU.mult).then_inc(s["c_mask"], 1)
            for a in range(CC):
                eng.wait_ge(s["svT"], 1)
                eng.tensor_scalar(wps[:, a, :], wp[:, a, :], PV[:, a * P:a * P + 1], None, ALU.mult).then_inc(s["wps_r"], 1)
            def q_half(u, half):
                r, d = (("qA_r", "qtA_r"), ("qB_r", "qtB_r"))[half]
                eng.wait_ge(s[r], u + 1)
                eng.tensor_copy(QT[:, 8 * half:8 * half + 8, :],
                                QBb.rearrange("p (a b) -> p a b", a=8)).then_inc(s[d], 1)

            def body(t, main, prev, nxt):
                first = not prev
                for h in range(16):
                    if main:
                        eng.wait_ge(s["score_r"], t * 16 + (h + 1))
                        if prev:
                            eng.wait_ge(s["exp_r"], t * 16 + (h - 15))
                        eng.tensor_scalar(junk[:, h % 4, :], S[:, h % 4, :], LN255, None, ALU.add, ALU.min,
                                          accum_out=ebias[:, h:h + 1]).then_inc(s["nb_r"], 1)
                    if h % 2 == 1:
                        tt, j = back(t, (h - 5) // 2)
                        if j in DVE_PAIRS and (h >= 5 or prev) and (main or h < 5):
                            eng.wait_ge(s["tr_r"], tt * 8 + (j + 1))
                            if not (first and j < 4):
                                eng.wait_ge(s["pv_r"], tt * 8 + (j - 3))
                            eng.tensor_copy(PT[:, j % 4, :], Ti[:, j % 2, :]).then_inc(s["evD"], 1)
                    if h == 2 and main:
                        q_half(t, 1)
                    if h == 1 and prev:
                        eng.wait_ge(s["exp_r"], t * 16)
                        eng.reciprocal(rsum[:, 8:16], esum[:, 8:16]).then_inc(s["rs_r"], 1)
                    if h == 6 and nxt:
                        q_scale(t + 1)
                    if h == 7 and prev:
                        eng.wait_ge(s["pv_r"], t * 8)
                        eng.wait_ge(s["rs_r"], t * 2)
                        if not (isinstance(t, int) and t == 1):
                            eng.wait_ge(s["aoT_r"], t - 1) if isinstance(t, int) else None
                        eng.tensor_tensor(ao[:, :].rearrange("p (h d) -> p h d", h=H), PV[:, 0:C].rearrange("p (h d) -> p h d", h=H),
                                          rsum[:, :].unsqueeze(2).to_broadcast([P, H, HD]), ALU.mult).then_inc(s["ao_r"], 1)
                    if h == 13 and prev:
                        eng.wait_ge(s["op_r"], t)
                        eng.wait_ge(s["xb_r"], t)
                        w = t - 1
                        eng.scalar_tensor_tensor(out=x[:, w, :], in0=QB[:, 0:C], scalar=gates[:, 0:1], in1=x[:, w, :],
                                                 op0=ALU.mult, op1=ALU.add).then_inc(s["x1_r"], 1)
                        eng.wait_ge(s["x1_r"], t)
                        eng.bn_stats(st[:, w, :], x[:, w, :]).then_inc(s["bs_r"], 1)
                    if h == 13 and main:
                        eng.wait_ge(s["exp_r"], t * 16 + 8)
                        if prev:
                            eng.wait_ge(s["ao_r"], t)
                        eng.reciprocal(rsum[:, 0:8], esum[:, 0:8]).then_inc(s["rs_r"], 1)
                    if h == 14 and nxt:
                        q_half(t + 1, 0)

            q_half(0, 0)
            body(0, True, False, True)
            with eng.Fori(1, NT - 1) as t:
                body(t, True, True, True)
            body(NT - 1, True, True, False)
            body(NT, False, True, False)

            eng.wait_ge(s["bs_r"], NT)
            layer_norm_scales(1)

            def f_hidden(t, b):
                if not (isinstance(t, int) and t < 2):
                    eng.wait_ge(s["f_hq"], 2 * t - 2)
                for k in range(2):
                    eng.wait_ge(s["f_sig"], 2 * t + (k + 1))
                    eng.tensor_tensor(hid[:, b, 512 * k:512 * k + 512], S[:, 2 * k + 1, :], sig[:, k, :], ALU.mult).then_inc(s["f_h"], 1)

            def f_scales(t, b):
                u = t + 2
                if in_range(t):
                    eng.wait_ge(s["f_h"], 2 * t + 2)
                    eng.tensor_reduce(hmax[:, :], hid[:, b, :], AX.X, ALU.max, apply_absolute_value=True).then_inc(s["f_hm"], 1)
                if in_range(u):
                    eng.wait_ge(s["f_xh"], u + 1)
                    eng.tensor_reduce(fmax[:, :], xh[:, :], AX.X, ALU.max, apply_absolute_value=True).then_inc(s["f_max"], 1)
                if in_range(t):
                    eng.wait_ge(s["f_hm"], t + 1)
                    eng.wait_ge(s["f_fg"], 2 * t + 2)
                    eng.tensor_scalar(hs[:, :], hmax[:, :], fu[:, b:b + 1], F_EPS, ALU.mult, ALU.max).then_inc(s["f_hs"], 1)
                if in_range(u):
                    eng.wait_ge(s["f_max"], u + 1)
                    eng.tensor_scalar(fs[:, b:b + 1], fmax[:, :], F_EPS, 1.0 / 127.0, ALU.max, ALU.mult).then_inc(s["f_s"], 1)
                if in_range(t):
                    eng.wait_ge(s["f_hs"], 3 * t + 1)
                    eng.reciprocal(hinv[:, :], hs[:, :]).then_inc(s["f_hs"], 1)
                if in_range(u):
                    eng.wait_ge(s["f_s"], u + 1)
                    eng.reciprocal(finv[:, :], fs[:, b:b + 1]).then_inc(s["f_inv"], 1)
                if in_range(t):
                    eng.wait_ge(s["f_hs"], 3 * t + 2)
                    if not (isinstance(t, int) and t == 0):
                        eng.wait_ge(s["f_hq"], 2 * t)
                    eng.tensor_scalar(hf[:, :], hinv[:, :], fu[:, b:b + 1], 127.0, ALU.mult, ALU.mult).then_inc(s["f_hf"], 1)
                    eng.tensor_scalar(col(ho, t), hs[:, :], wdg[:, 0:1], None, ALU.mult).then_inc(s["f_hs"], 1)
                if in_range(u):
                    if not (isinstance(u, int) and u < 2):
                        eng.wait_ge(s["f_sig"], 2 * u - 2)
                        eng.wait_ge(s["f_hf"], u - 1)
                    eng.tensor_scalar(fg[:, b:b + 1], fs[:, b:b + 1], wscale[:, 0:1], None, ALU.mult).then_inc(s["f_fg"], 1)
                    eng.tensor_scalar(fu[:, b:b + 1], fs[:, b:b + 1], wscale[:, 1:2], None, ALU.mult).then_inc(s["f_fg"], 1)

            def f_out(t, b):
                eng.wait_ge(s["f_dn"], t + 1)
                eng.wait_ge(s["f_hs"], 3 * t + 3)
                eng.scalar_tensor_tensor(out=x[:, t, :], in0=(PV, QB)[b][:, 0:C], scalar=col(ho, t), in1=x[:, t, :],
                                         op0=ALU.mult, op1=ALU.add).then_inc(s["f_x"], 1)

            def f_stats(t):
                eng.wait_ge(s["f_x"], t + 1)
                eng.bn_stats(st[:, t, :], x[:, t, :]).then_inc(s["f_bs"], 1)

            def f_step(t, b):
                if in_range(t):
                    f_hidden(t, b)
                if in_range(t - 3):
                    f_out(t - 3, 1 - b)
                f_scales(t, b)
                if in_range(t - 3):
                    f_stats(t - 3)

            for t in range(-2, 4):
                f_step(t, t % 2)
            with eng.Fori(0, (NT - 6) // 2) as u:
                for b in range(2):
                    f_step(u * 2 + (b + 4), b)
            for t in range(NT - 2, NT + 3):
                f_step(t, t % 2)

            eng.wait_ge(s["f_bs"], NT)
            layer_norm_scales(2)
            eng.wait_ge(s["c_mask"], 1)

            def c_step(b):
                if in_batches(b - 1):
                    if not (isinstance(b, int) and b == 1):
                        eng.wait_ge(s["c_x"], b * 2 - 2)
                    for i in range(2):
                        eng.wait_ge(s["c_ex"], b * 2 + (i - 1))
                        eng.reciprocal(srec[:, i:i + 1], ssum[:, i:i + 1]).then_inc(s["c_rc"], 1)
                if in_batches(b):
                    for i in range(2):
                        eng.wait_ge(s["c_sc"], b * 2 + (i + 1))
                        eng.scalar_tensor_tensor(out=sm[:, i, :], in0=S[:, 2 + i, 0:M], scalar=1.0 / 16.0,
                                                 in1=madd[:, b * M:b * M + M] if isinstance(b, int) else madd[:, bass.ds(b * M, M)],
                                                 op0=ALU.mult, op1=ALU.add).then_inc(s["c_sm"], 1)
                if in_batches(b - 1):
                    for i in range(2):
                        eng.wait_ge(s["c_rc"], b * 2 + (i - 1))
                        eng.tensor_scalar(sfac[:, i:i + 1], srec[:, i:i + 1], col(gvalid, b - 1), None, ALU.mult).then_inc(s["c_f"], 1)
                if in_batches(b):
                    for i in range(2):
                        eng.wait_ge(s["c_sm"], b * 2 + (i + 1))
                        eng.tensor_reduce(smax[:, i:i + 1], sm[:, i, :], AX.X, ALU.max, negate=True).then_inc(s["c_mx"], 1)
                if in_batches(b - 1):
                    for i in range(2):
                        n = 2 * (b - 1) + i
                        eng.wait_ge(s["c_rd"], b * 2 + (i - 1))
                        eng.wait_ge(s["c_f"], b * 2 + (i - 1))
                        eng.scalar_tensor_tensor(out=x[:, n, :], in0=(PV, QB)[i][:, 0:C], scalar=sfac[:, i:i + 1],
                                                 in1=x[:, n, :], op0=ALU.mult, op1=ALU.add).then_inc(s["c_x"], 1)
                    for i in range(2):
                        n = 2 * (b - 1) + i
                        eng.wait_ge(s["c_x"], b * 2 + (i - 1))
                        eng.bn_stats(st[:, n, :], x[:, n, :]).then_inc(s["c_bs"], 1)

            c_step(0)
            c_step(1)
            with eng.Fori(2, BATCH) as b:
                c_step(b)
            c_step(BATCH)

            eng.wait_ge(s["c_bs"], NT)
            layer_norm_scales(3)
            eng.sem_inc(s["rt_lgs"], 1)
            with eng.Fori(0, NT // 4) as g:
                eng.wait_ge(s["rt_lg"], g * 4 + 9)
                eng.tensor_copy(lg[:, :, :], PV[:, 0:4 * E].rearrange("p (i e) -> p i e", i=4)).then_inc(s["rt_lgs"], 1)
                for i in range(4):
                    if i == 0:
                        eng.wait_ge(s["rt_lgs"], g + 2)
                        eng.sem_inc(s["apart_d"], 1)
                    eng.max(top[:, i, :], lg[:, i, :]).then_inc(s["rt_top"], 1)
                for i in range(4):
                    eng.wait_ge(s["rt_top"], g * 4 + (i + 1))
                    eng.sem_inc(s["apart_d"], 1)
                    eng.max_index(topi[:, i, :], top[:, i, :], lg[:, i, :]).then_inc(s["rt_topi"], 1)
                eng.tensor_copy(topv[:, bass.ds(g * 4, 4), :], top[:, :, 0:TOPK]).then_inc(s["rt_sel"], 1)
                eng.wait_ge(s["rt_topi"], g * 4 + 4)
                eng.tensor_copy(topx[:, bass.ds(g * 4, 4), :], topi[:, :, 0:TOPK]).then_inc(s["rt_sel"], 1)
                eng.wait_ge(s["rt_sel"], g * 2 + 2)
            n = [0]

            def step(ins):
                n[0] += 1
                ins.then_inc(s["rt"], 1)
                eng.wait_ge(s["rt"], n[0])

            eng.tensor_tensor(gw[:, 0, :], topv[:, :, 1], topv[:, :, 0], ALU.subtract).then_inc(s["rt_gap"], 1)
            eng.wait_ge(s["rt_const"], 10)
            step(eng.tensor_tensor(pick[:, :, :, :], iota[:, 0:E].unsqueeze(1).unsqueeze(1).to_broadcast([P, TOPK, NT, E]),
                                   topx[:, :, :].rearrange("p t k -> p k t").unsqueeze(3).to_broadcast([P, TOPK, NT, E]), ALU.is_equal))
            eng.tensor_tensor(picks[:, 0:NT, :], pick[:, 0, :, :], pick[:, 1, :, :], ALU.add).then_inc(s["rt_picks"], 1)
            eng.wait_ge(s["rt_exp"], 1)
            step(eng.tensor_scalar(gw[:, 0, :], gw[:, 1, :], 1.0, None, ALU.add))
            step(eng.reciprocal(gw[:, 2, :], gw[:, 0, :]))
            step(eng.tensor_scalar(gk[:, 0, :], gw[:, 2, :], gates[:, 3:4], None, ALU.mult))
            step(eng.tensor_tensor(gk[:, 1, :], gk[:, 0, :], gw[:, 1, :], ALU.mult))
            eng.wait_ge(s["rt_order"], 1)
            pos = PV[:, 0:NT * E].rearrange("p (t e) -> p t e", t=NT)
            step(eng.tensor_scalar(cnt[:, :], PV[:, NT * E:(NT + 1) * E], (P - 1) / 2.0, 1.0 / P, ALU.add, ALU.mult))
            step(eng.tensor_scalar(tiles_of[:, :], cnt[:, :], MAGIC, -MAGIC, ALU.add, ALU.add))
            step(eng.tensor_tensor(lowprod[:, :, :], lower[:, :, :], tiles_of[:, :].unsqueeze(1).to_broadcast([P, E, E]), ALU.mult))
            step(eng.tensor_reduce(base[:, :], lowprod[:, :, :], AX.X, ALU.add))
            step(eng.tensor_tensor(upto[:, :], base[:, :], tiles_of[:, :], ALU.add))
            step(eng.tensor_scalar(order[:, :, :], pos, -(P - 1) / 2.0, 1.0 / P, ALU.add, ALU.mult))
            step(eng.tensor_scalar(block_[:, :, :], order[:, :, :], MAGIC, -MAGIC, ALU.add, ALU.add))
            step(eng.scalar_tensor_tensor(out=row_[:, :, :], in0=block_[:, :, :], scalar=-float(P), in1=pos, op0=ALU.mult, op1=ALU.add))
            step(eng.tensor_tensor(block_[:, :, :], block_[:, :, :], base[:, :].unsqueeze(1).to_broadcast([P, NT, E]), ALU.add))
            for value, chosen in ((row_, tok_row), (block_, tok_tile)):
                step(eng.tensor_tensor(picked[:, :, :, :], pick[:, :, :, :], value[:, :, :].unsqueeze(1).to_broadcast([P, TOPK, NT, E]), ALU.mult))
                step(eng.tensor_reduce(chosen[:, :], picked[:, :, :, :].rearrange("p k t e -> p (k t) e"), AX.X, ALU.add))
            step(eng.tensor_tensor(ended[:, :, :], iota[:, 0:SLOTS].unsqueeze(2).to_broadcast([P, SLOTS, E]),
                                   upto[:, :].unsqueeze(1).to_broadcast([P, SLOTS, E]), ALU.is_ge))
            step(eng.tensor_reduce(tile_e[:, :], ended[:, :, :], AX.X, ALU.add))
            step(eng.tensor_scalar(tile_off[:, :], tile_e[:, :], E - 1.0, float(CC * DI), ALU.min, ALU.mult))
            eng.wait_ge(s["out_init"], 80)
            step(eng.tensor_tensor(hit, iota[:, 0:SLOTS].unsqueeze(1).to_broadcast([P, NK, SLOTS]),
                                   tok_tile[:, :].unsqueeze(2).to_broadcast([P, NK, SLOTS]), ALU.is_equal))
            for k in range(TOPK):
                mine = slice(k * NT, (k + 1) * NT)
                eng.tensor_tensor(hitt[:, mine, 0, :], hit[:, mine, :], token1[:, :].unsqueeze(2).to_broadcast([P, NT, SLOTS]),
                                  ALU.mult).then_inc(s["rt_hitt"], 1)
                eng.tensor_tensor(hitt[:, mine, 1, :], hit[:, mine, :], gk[:, k, :].unsqueeze(2).to_broadcast([P, NT, SLOTS]),
                                  ALU.mult).then_inc(s["rt_hitt"], 1)
            with eng.Fori(0, NK // 8) as u:
                for b in range(2):
                    eng.wait_ge(s["rt_mm"], u * 8 + (4 * b + 4))
                    eng.tensor_tensor(hitr[:, b, :, :], iota[:, :].unsqueeze(1).to_broadcast([P, 4, P]),
                                      tok_row[:, bass.ds(u * 8 + 4 * b, 4)].unsqueeze(2).to_broadcast([P, 4, P]),
                                      ALU.is_equal).then_inc(s["rt_hit"], 1)
            eng.wait_ge(s["rt_mm"], NK + 9)
            step(eng.tensor_copy(slot[:, :, :], QB[:, 0:2 * SLOTS].rearrange("p (a j) -> p a j", a=2)))
            eng.tensor_scalar(slot_in[:, :], slot[:, 0, :], -1.0, 0.0, ALU.add, ALU.max).then_inc(s["rt_slots"], 1)
            step(eng.tensor_scalar(empty[:, :], slot[:, 0, :], 0.5, padrow[:, 0:1], ALU.is_lt, ALU.mult))
            step(eng.tensor_scalar(slot[:, 0, :], slot[:, 0, :], -1.0, None, ALU.add))
            eng.tensor_tensor(slot_out[:, :], slot[:, 0, :], empty[:, :], ALU.add).then_inc(s["rt_slots"], 1)
            eng.sem_inc(s["rt_slots"], 1)

            def number(j, b, h):
                after(eng, s[f"ex_in{b}"], h * 16)
                eng.tensor_copy(rows_in[:, b:b + 1], col(slot_in, j)).then_inc(s["ex_from"], 1)

            def turned_h(j, b):
                eng.wait_ge(s["ex_hT"], j + 1)
                after(eng, s["ex_y"], j - 1)
                eng.tensor_copy(hactT[:, b, :], S[:, 2 + b, :]).then_inc(s["ex_hTe"], 1)

            def weigh(j, b):
                eng.wait_ge(s["ex_y"], j + 1)
                after(eng, s["ex_add"], (j - 1) * 16)
                eng.tensor_scalar(yo[:, b, :], (PV, QB)[b][:, 0:C], slot[:, 1, j:j + 1] if isinstance(j, int) else slot[:, 1, bass.ds(j, 1)],
                                  None, ALU.mult).then_inc(s["ex_yo"], 1)
                eng.tensor_copy(rows_out[:, b:b + 1], col(slot_out, j)).then_inc(s["ex_yo"], 1)

            eng.wait_ge(s["rt_slots"], 3)
            number(0, 0, 0)
            number(1, 1, 0)
            number(2, 0, 1)
            turned_h(0, 0)
            for j in (1, 2):
                number(j + 2, j % 2, (j + 2) // 2)
                weigh(j - 1, (j - 1) % 2)
                turned_h(j, j % 2)
            with eng.Fori(0, (SLOTS - 5) // 2) as u:
                for i in range(2):
                    number(u * 2 + (i + 5), 1 - i, u + (i + 5) // 2)
                    weigh(u * 2 + (i + 2), i)
                    turned_h(u * 2 + (i + 3), 1 - i)
            for j in (SLOTS - 2, SLOTS - 1):
                weigh(j - 1, (j - 1) % 2)
                turned_h(j, j % 2)
            weigh(SLOTS - 1, 0)

        @block.tensor
        def _(eng):
            eng.wait_ge(s["w_in1"], 48)
            for kt in range(KB):
                for a in range(CC):
                    mm = eng.matmul(S[:, kt, :], ctxT[:, a, kt * P:kt * P + P], wkv[:, a, :], start=a == 0, stop=a == CC - 1)
                mm.then_inc(s["kvp"], 1)
            def q_xhT(u):
                eng.wait_ge(s["xh_r"], u + 1)
                for a in range(CC):
                    mm = eng.transpose(QB[:, a * P:a * P + P], xh[:, a * P:a * P + P], ident[:, :])
                mm.then_inc(s["xhT_r"], 1)

            def q_proj(u):
                eng.wait_ge(s["xT_r"], u + 1)
                for a in range(CC):
                    mm = eng.matmul(QB[:, 0:C], xT[:, a * P:a * P + P], wq[:, a, :], start=a == 0, stop=a == CC - 1)
                mm.then_inc(s["qp_r"], 1)

            eng.wait_ge(s["consts"], 2)
            eng.wait_ge(s["w_in2"], 96)
            q_xhT(0)
            q_proj(0)
            eng.wait_ge(s["kct_in"], 1)
            for i in range(8):
                kt, half = i // 2, i % 2
                if i >= 2:
                    eng.wait_ge(s["kev"], i - 1)
                for k in range(8):
                    mm = eng.transpose(Tb[:, half, k * P:k * P + P], KC[:, kt, 8 * half + k, :], identb[:, :])
                mm.then_inc(s["kct"], 1)

            def q_turn(u, half):
                for k in range(8):
                    mm = eng.transpose(QBb[:, k * P:k * P + P], QC[:, 8 * half + k, :], identb[:, :])
                mm.then_inc(s[("qA_r", "qB_r")[half]], 1)

            def body(t, main, prev, nxt):
                first = not prev
                for h in range(16):
                    if main:
                        if h == 0:
                            eng.wait_ge(s["qtA_r"], t + 1)
                        if h == 8:
                            eng.wait_ge(s["qtB_r"], t + 1)
                        if not (first and h < 4):
                            eng.wait_ge(s["exp_r"], t * 16 + (h - 3))
                        eng.matmul(S[:, h % 4, :], QT[:, h, :], KT[:, h, :], start=True, stop=True).then_inc(s["score_r"], 1)
                    if h % 2 == 1:
                        tt, j = back(t, (h - 5) // 2)
                        if (h >= 5 or prev) and (main or h < 5):
                            eng.wait_ge(s["exp_r"], tt * 16 + (2 * j + 2))
                            if not (first and j < 2):
                                eng.wait_ge(*ev_sem(*back(tt, j - 2)))
                            for k in range(2 * KB):
                                mm = eng.transpose(Tb[:, j % 2, k * P:k * P + P], Rb[:, j % 4, k // KB, (k % KB) * P:(k % KB) * P + P], identb[:, :])
                            mm.then_inc(s["tr_r"], 1)
                    if h % 2 == 1:
                        tt, j = back(t, (h - 9) // 2)
                        if (h >= 9 or prev) and (main or h < 9):
                            eng.wait_ge(*ev_sem(tt, j))
                            if j == 0 and prev:
                                eng.wait_ge(s["ao_r"], tt)
                            for k in range(2 * KB):
                                hh = 2 * j + k // KB
                                mm = eng.matmul(PV[:, hh * HD:hh * HD + HD], PT[:, j % 4, k * P:k * P + P],
                                                V[:, k % KB, hh * HD:hh * HD + HD], start=k % KB == 0, stop=k % KB == KB - 1)
                            mm.then_inc(s["pv_r"], 1)
                    if h == 2 and main:
                        eng.wait_ge(s["qtA_r"], t + 1)
                        q_turn(t, 1)
                    if h == 3 and nxt:
                        eng.wait_ge(s["qtB_r"], t + 1)
                        q_xhT(t + 1)
                    if h == 6 and nxt:
                        q_proj(t + 1)
                    if h == 10 and prev:
                        eng.wait_ge(s["ao_r"], t)
                        if nxt:
                            eng.wait_ge(s["q_r"], t + 2)
                        for a in range(CC):
                            mm = eng.transpose(QB[:, a * P:a * P + P], ao[:, a * P:a * P + P], ident[:, :])
                        mm.then_inc(s["aoT_r"], 1)
                    if h == 13 and prev:
                        eng.wait_ge(s["aoTe_r"], t)
                        for a in range(CC):
                            mm = eng.matmul(QB[:, 0:C], aoT[:, a * P:a * P + P], wps[:, a, :], start=a == 0, stop=a == CC - 1)
                        mm.then_inc(s["op_r"], 1)
                    if h == 15 and nxt:
                        if prev:
                            eng.wait_ge(s["x1_r"], t)
                        eng.wait_ge(s["qprep"], 9 * (t + 1) + 9)
                        q_turn(t + 1, 0)

            eng.wait_ge(s["qprep"], 9)
            q_turn(0, 0)
            eng.wait_ge(s["vq"], 1)
            for a in range(CC):
                mm = eng.transpose(PV[:, a * P:a * P + P], vscale[:, a * P:a * P + P], ident[:, :])
            mm.then_inc(s["svT"], 1)
            eng.wait_ge(s["kev"], 8)
            eng.wait_ge(s["vq"], 2)
            eng.wait_ge(s["wps_r"], CC)
            body(0, True, False, True)
            with eng.Fori(1, NT - 1) as t:
                body(t, True, True, True)
            body(NT - 1, True, True, False)
            body(NT, False, True, False)

            def f_turn_x(u):
                eng.wait_ge(s["f_rq"], 2 * u + 2)
                if not (isinstance(u, int) and u == 0):
                    eng.wait_ge(s["f_xiTe"], u)
                for a in range(CC):
                    mm = eng.transpose(Tb[:, 0, a * P:a * P + P], xi[:, a * P:a * P + P], identb[:, :])
                mm.then_inc(s["f_xiT"], 1)

            def f_gate_up(t):
                eng.wait_ge(s["f_xiTe"], t + 1)
                for k in range(2):
                    if not (isinstance(t, int) and t == 0):
                        eng.wait_ge(s["f_h"], 2 * t + (k - 1))
                    for w in range(2):
                        for a in range(CC):
                            mm = eng.matmul(S[:, 2 * k + w, :], xiT[:, a * P:a * P + P],
                                            wi[w][:, a * FF + 512 * k:a * FF + 512 * k + 512], start=a == 0, stop=a == CC - 1)
                    mm.then_inc(s["f_gu"], 1)

            def f_turn_h(t):
                eng.wait_ge(s["f_hq"], 2 * t + 2)
                if not (isinstance(t, int) and t == 0):
                    eng.wait_ge(s["f_hiTe"], t)
                for k in range(8):
                    mm = eng.transpose(Tb[:, 1, k * P:k * P + P], hi[:, k * P:k * P + P], identb[:, :])
                mm.then_inc(s["f_hiT"], 1)

            def f_down(t, b):
                eng.wait_ge(s["f_hiTe"], t + 1)
                if not (isinstance(t, int) and t < 2):
                    eng.wait_ge(s["f_x"], t - 1)
                for k in range(8):
                    mm = eng.matmul((PV, QB)[b][:, 0:C], hiT[:, k * P:k * P + P], wi[2][:, k * C:k * C + C], start=k == 0, stop=k == 7)
                mm.then_inc(s["f_dn"], 1)

            def f_step(t, b):
                if in_range(t - 3):
                    f_down(t - 3, 1 - b)
                if in_range(t - 2):
                    f_turn_h(t - 2)
                if in_range(t):
                    f_gate_up(t)
                if in_range(t + 1):
                    f_turn_x(t + 1)

            eng.wait_ge(s["wpool"], 18)
            for t in range(-1, 4):
                f_step(t, t % 2)
            with eng.Fori(0, (NT - 6) // 2) as u:
                for b in range(2):
                    f_step(u * 2 + (b + 4), b)
            for t in range(NT - 2, NT + 3):
                f_step(t, t % 2)

            eng.wait_ge(s["f_x"], NT)

            def c_step(b):
                for i in range(2):
                    if in_batches(b - 1):
                        if not (isinstance(b, int) and b == 1):
                            eng.wait_ge(s["c_pTe"], b * 2 + (i - 3))
                        eng.wait_ge(s["c_ex"], b * 2 + (i - 1))
                        eng.sem_inc(s["apart_p"], 1)
                        eng.transpose(T[0:M, i, 0:P], pe_[:, i, :], ident[:, :]).then_inc(s["c_pT"], 1)
                for i in range(2):
                    if in_batches(b):
                        if not (isinstance(b, int) and b == 0):
                            eng.wait_ge(s["c_sm"], b * 2 + (i - 1))
                        eng.wait_ge(s["c_xT"], b * 2 + (i + 1))
                        for a in range(CC):
                            mm = eng.matmul(S[:, 2 + i, 0:M], xT2[:, i, a * P:a * P + P],
                                            ctxT[:, a, b * M:b * M + M] if isinstance(b, int) else ctxT[:, a, bass.ds(b * M, M)],
                                            start=a == 0, stop=a == CC - 1)
                        mm.then_inc(s["c_sc"], 1)
                for i in range(2):
                    if in_batches(b + 1):
                        eng.wait_ge(s["c_xh"], b * 2 + (i + 3))
                        for a in range(CC):
                            mm = eng.transpose(S[:, i, a * P:a * P + P], xh2[:, i, a * P:a * P + P], ident[:, :])
                        mm.then_inc(s["c_xhT"], 1)
                for i in range(2):
                    if in_batches(b - 1):
                        if not (isinstance(b, int) and b == 1):
                            eng.wait_ge(s["c_x"], b * 2 + (i - 3))
                        eng.wait_ge(s["c_pTe"], b * 2 + (i - 1))
                        eng.sem_inc(s["apart_p"], 1)
                        eng.matmul((PV, QB)[i][:, 0:C], pT[:, i, :], ctxn[:, b - 1, :], start=True, stop=True).then_inc(s["c_rd"], 1)

            for b in (-1, 0, 1):
                c_step(b)
            with eng.Fori(2, BATCH - 1) as b:
                c_step(b)
            for b in (BATCH - 1, BATCH):
                c_step(b)

            eng.sem_inc(s["rt_lg"], 5)
            with eng.Fori(0, NT // 8) as u:
                for b in range(2):
                    for i in range(4):
                        eng.wait_ge(s["rt_xh"], u * 8 + (4 * b + i + 1))
                        for a in range(CC):
                            mm = eng.transpose(S[:, i, a * P:a * P + P], xr[b][:, i, a * P:a * P + P], ident[:, :])
                        mm.then_inc(s["rt_T"], 1)
                    eng.wait_ge(s["rt_lgs"], u * 2 + (b + 1))
                    for i in range(4):
                        eng.wait_ge(s["rt_xT"], u * 8 + (4 * b + i + 1))
                        for a in range(CC):
                            mm = eng.matmul(PV[:, i * E:i * E + E], xrT[b][:, i, a * P:a * P + P], wr[:, a, :], start=a == 0, stop=a == CC - 1)
                        mm.then_inc(s["rt_lg"], 1)
            eng.wait_ge(s["rt_picks"], 1)
            eng.matmul(PV[:, 0:(NT + 1) * E], trib[:, :], picks[:, :, :].rearrange("p t e -> p (t e)"), start=True, stop=False)
            for t in range(NT):
                mm = eng.matmul(PV[:, (t + 1) * E:(NT + 1) * E], onesb[:, :],
                                picks[:, t:t + 1, :].to_broadcast([P, NT - t, E]), start=False, stop=t == NT - 1)
            mm.then_inc(s["rt_order"], 1)
            eng.sem_inc(s["rt_mm"], 8)
            eng.matmul(QB[:, 0:2 * SLOTS], ident[:, :], zeros[:, :], start=True, stop=False)
            eng.wait_ge(s["rt_hitt"], 2 * TOPK)
            hflat = hitt.rearrange("p m a j -> p (m a j)")
            with eng.Fori(0, NK // 8) as u:
                for b in range(2):
                    eng.wait_ge(s["rt_hit"], u * 2 + (b + 1))
                    for i in range(4):
                        eng.matmul(QB[:, 0:2 * SLOTS], hitr[:, b, i, :],
                                   hflat[:, bass.ds(u * (8 * 2 * SLOTS) + (4 * b + i) * 2 * SLOTS, 2 * SLOTS)],
                                   start=False, stop=False).then_inc(s["rt_mm"], 1)
            eng.matmul(QB[:, 0:2 * SLOTS], ident[:, :], zeros[:, :], start=False, stop=True).then_inc(s["rt_mm"], 1)

            def turn_x(j, b, h):
                eng.wait_ge(s[f"ex_in{b}"], 16 * h + 16)
                after(eng, s["ex_xT"], j - 1)
                for a in range(CC):
                    mm = eng.transpose(T[:, b, a * P:a * P + P], xg[:, b, a * P:a * P + P], ident[:, :])
                mm.then_inc(s["ex_turn"], 1)

            def first(j, b, off):
                eng.wait_ge(s["ex_xT"], j + 1)
                after(eng, s["ex_act"], j - 1)
                for a in range(CC):
                    mm = eng.matmul(S[:, b, :], xgT[:, b, a * P:a * P + P], WIN[:, bass.ds(off + a * DI, DI)], start=a == 0, stop=a == CC - 1)
                mm.then_inc(s["ex_h"], 1)

            def turn_h(j, b):
                eng.wait_ge(s["ex_act"], j + 1)
                after(eng, s["ex_hTe"], j - 1)
                for a in range(DI // P):
                    mm = eng.transpose(S[:, 2 + b, a * P:a * P + P], hact[:, b, a * P:a * P + P], ident[:, :])
                mm.then_inc(s["ex_hT"], 1)

            def second(j, b, off):
                eng.wait_ge(s["ex_hTe"], j + 1)
                after(eng, s["ex_yo"], 2 * (j - 1))
                for a in range(DI // P):
                    mm = eng.matmul((PV, QB)[b][:, 0:C], hactT[:, b, a * P:a * P + P], WOUT[:, bass.ds(off + a * C, C)],
                                    start=a == 0, stop=a == DI // P - 1)
                mm.then_inc(s["ex_y"], 1)

            def weights_of(j):
                return eng.value_load(tile_off[0:1, j:j + 1] if isinstance(j, int) else tile_off[0:1, bass.ds(j, 1)],
                                      min_val=0, max_val=(E - 1) * CC * DI)

            eng.wait_ge(s["rt_slots"], 3)
            eng.wait_ge(s["w_exp"], 16 * 2 * E)
            turn_x(0, 0, 0)
            first(0, 0, weights_of(0))
            turn_x(1, 1, 0)
            turn_h(0, 0)
            for j in (1, 2):
                first(j, j % 2, weights_of(j))
                turn_x(j + 1, (j + 1) % 2, (j + 1) // 2)
                second(j - 1, (j - 1) % 2, weights_of(j - 1))
                turn_h(j, j % 2)
            with eng.Fori(0, (SLOTS - 5) // 2) as u:
                for i in range(2):
                    first(u * 2 + (i + 3), 1 - i, weights_of(u * 2 + (i + 3)))
                    turn_x(u * 2 + (i + 4), i, u + (i + 4) // 2)
                    second(u * 2 + (i + 2), i, weights_of(u * 2 + (i + 2)))
                    turn_h(u * 2 + (i + 3), 1 - i)
            for j in (SLOTS - 2, SLOTS - 1):
                first(j, j % 2, weights_of(j))
                if j + 1 < SLOTS:
                    turn_x(j + 1, (j + 1) % 2, (j + 1) // 2)
                second(j - 1, (j - 1) % 2, weights_of(j - 1))
                turn_h(j, j % 2)
            second(SLOTS - 1, 0, weights_of(SLOTS - 1))


def kernel(**inputs):
    import numpy as _np
    import concourse.bacc as _bacc
    from concourse import mybir as _mybir
    from concourse.bass_utils import run_bass_kernel_spmd as _run

    a = {k: _np.asarray(v) for k, v in inputs.items()}
    laid = {
        "x": a["x"].reshape(TOKENS, C),
        "ctx": a["ctx_2048"].reshape(KEYS, C),
        "ctxT": a["ctx_2048"].reshape(KEYS, C).T,
        "mask": a["mask_BxS2_bk0"].reshape(BATCH * M),
        "gx": a["g_xattn"], "gf": a["g_ffn"],
        "wq": a["L0_xattn_Wq"], "bq": a["L0_xattn_bq"], "wkv": a["L0_xattn_Wkv"], "bkv": a["L0_xattn_bkv"],
        "wp": a["L0_xattn_Wp"], "bp": a["L0_xattn_bp"],
        "wg": a["L0_ffn_w_gate"].T, "wu": a["L0_ffn_w_up"].T, "wd": a["L0_ffn_w_down"].T,
        "wr": a["L1_ffn_Wr"].T, "win": a["L1_ffn_Win"].transpose(0, 2, 1), "wout": a["L1_ffn_Wout"].transpose(0, 2, 1),
    }
    nc = _bacc.Bacc("TRN2", target_bir_lowering=False, num_devices=1)
    arrays, args = {}, []
    for name, v in laid.items():
        v = _np.ascontiguousarray(v)
        arrays[f"in_{name}_dram"] = v
        args.append(nc.dram_tensor(f"in_{name}_dram", v.shape, _mybir.dt.from_np(v.dtype), kind="ExternalInput").ap())
    args.append(nc.dram_tensor("out_dram", (TOKENS + P, C), F32, kind="ExternalOutput").ap())
    flamingo_kernel(nc, *args)
    r = _run(nc, [arrays], core_ids=[0])
    return r.results[0]["out_dram"][:TOKENS].reshape(8, 256, C)
```
